# Optimizing a Trainium2 kernel written in Bass

```python
import numpy as np
import jax
import jax.numpy as jnp

def _softmax(x, axis=-1):
    return jax.nn.softmax(x, axis=axis)

def _gelu(x):
    return jax.nn.gelu(x, approximate=True)

def _silu(x):
    return jax.nn.silu(x)

def _sigmoid(x):
    return jax.nn.sigmoid(x)

def _layernorm(x, axis=-1, eps=1e-05):
    m = jnp.mean(x, axis=axis, keepdims=True)
    v = jnp.var(x, axis=axis, keepdims=True)
    return (x - m) / jnp.sqrt(v + eps)

def _scatter_add(tgt, idx, src, axis=0):
    return tgt.at[idx].add(src)

def _segment_sum(src, seg, n):
    return jax.ops.segment_sum(src, seg, n)
kernel_name = 'mk_prb_d1_jaxref_r8_103808'

def setup_inputs(seed: int=0):
    np.random.seed(seed)
    _w = jnp.asarray

    def _L0_attn_setup():
        import jax, jax.numpy as jnp
        import numpy as np
        D_MODEL = 256
        N_HEADS = 16
        HEAD_DIM = D_MODEL // N_HEADS
        ROPE_THETA = 10000.0
        BATCH = 2
        SEQ_LEN = 256

        def _apply_rope(x):
            S = x.shape[2]
            inv_freq = 1.0 / ROPE_THETA ** (jnp.arange(0, HEAD_DIM, 2, dtype=jnp.float32) / HEAD_DIM)
            t = jnp.arange(S, dtype=jnp.float32)
            freqs = jnp.outer(t, inv_freq)
            cos = jnp.cos(freqs)
            sin = jnp.sin(freqs)
            x1 = x[..., 0::2]
            x2 = x[..., 1::2]
            rot = jnp.stack([x1 * cos - x2 * sin, x1 * sin + x2 * cos], axis=-1)
            return rot.reshape(x.shape)
        key = jax.random.key(seed)
        ks = jax.random.split(key, 5)
        scale = 1.0 / np.sqrt(D_MODEL)
        x = jax.random.normal(ks[0], (BATCH, SEQ_LEN, D_MODEL), dtype=jnp.float32)
        Wq = jax.random.normal(ks[1], (D_MODEL, D_MODEL), dtype=jnp.float32) * scale
        Wk = jax.random.normal(ks[2], (D_MODEL, D_MODEL), dtype=jnp.float32) * scale
        Wv = jax.random.normal(ks[3], (D_MODEL, D_MODEL), dtype=jnp.float32) * scale
        Wo = jax.random.normal(ks[4], (D_MODEL, D_MODEL), dtype=jnp.float32) * scale
        return {'x': x, 'Wq': Wq, 'Wk': Wk, 'Wv': Wv, 'Wo': Wo}
    _L0_attn_in = _L0_attn_setup()

    def _L0_ffn_setup():
        import jax, jax.numpy as jnp
        import numpy as np
        H = 256
        M = 176
        E = 32
        TOPK = 6
        G = 8
        TOPK_G = 4
        SH = 2
        B, S = (1, 128)
        key = jax.random.key(seed)
        ks = jax.random.split(key, 9)
        sc = 0.02
        return {'x': jax.random.normal(ks[0], (B, S, H), dtype=jnp.float32), 'w_router': jax.random.normal(ks[1], (H, E), dtype=jnp.float32) * sc, 'corr_bias': jax.random.normal(ks[2], (E,), dtype=jnp.float32) * 0.1, 'gate_w': jax.random.normal(ks[3], (E, H, M), dtype=jnp.float32) * sc, 'up_w': jax.random.normal(ks[4], (E, H, M), dtype=jnp.float32) * sc, 'down_w': jax.random.normal(ks[5], (E, M, H), dtype=jnp.float32) * sc, 'sh_gate_w': jax.random.normal(ks[6], (H, M * SH), dtype=jnp.float32) * sc, 'sh_up_w': jax.random.normal(ks[7], (H, M * SH), dtype=jnp.float32) * sc, 'sh_down_w': jax.random.normal(ks[8], (M * SH, H), dtype=jnp.float32) * sc}
    _L0_ffn_in = _L0_ffn_setup()
    _d = {'L0_attn_x': _L0_attn_in['x'], 'L0_attn_Wq': _L0_attn_in['Wq'], 'L0_attn_Wk': _L0_attn_in['Wk'], 'L0_attn_Wv': _L0_attn_in['Wv'], 'L0_attn_Wo': _L0_attn_in['Wo'], 'L0_ffn_w_router': _L0_ffn_in['w_router'], 'L0_ffn_corr_bias': _L0_ffn_in['corr_bias'], 'L0_ffn_gate_w': _L0_ffn_in['gate_w'], 'L0_ffn_up_w': _L0_ffn_in['up_w'], 'L0_ffn_down_w': _L0_ffn_in['down_w'], 'L0_ffn_sh_gate_w': _L0_ffn_in['sh_gate_w'], 'L0_ffn_sh_up_w': _L0_ffn_in['sh_up_w'], 'L0_ffn_sh_down_w': _L0_ffn_in['sh_down_w']}
    _x0 = _d['L0_attn_x']
    _d['L0_attn_x'] = jax.random.normal(jax.random.fold_in(jax.random.key(seed), 1), (4, 512, 256), dtype=_x0.dtype)
    del _x0
    return _d

def reference(L0_attn_x, L0_attn_Wq, L0_attn_Wk, L0_attn_Wv, L0_attn_Wo, L0_ffn_w_router, L0_ffn_corr_bias, L0_ffn_gate_w, L0_ffn_up_w, L0_ffn_down_w, L0_ffn_sh_gate_w, L0_ffn_sh_up_w, L0_ffn_sh_down_w):

    def _L0_attn_ref(x, Wq, Wk, Wv, Wo):
        import jax, jax.numpy as jnp
        import numpy as np
        D_MODEL = 256
        N_HEADS = 16
        HEAD_DIM = D_MODEL // N_HEADS
        ROPE_THETA = 10000.0
        BATCH = 2
        SEQ_LEN = 256

        def _apply_rope(x):
            S = x.shape[2]
            inv_freq = 1.0 / ROPE_THETA ** (jnp.arange(0, HEAD_DIM, 2, dtype=jnp.float32) / HEAD_DIM)
            t = jnp.arange(S, dtype=jnp.float32)
            freqs = jnp.outer(t, inv_freq)
            cos = jnp.cos(freqs)
            sin = jnp.sin(freqs)
            x1 = x[..., 0::2]
            x2 = x[..., 1::2]
            rot = jnp.stack([x1 * cos - x2 * sin, x1 * sin + x2 * cos], axis=-1)
            return rot.reshape(x.shape)
        B, S, _ = x.shape
        q = (x @ Wq.T).reshape(B, S, N_HEADS, HEAD_DIM).transpose(0, 2, 1, 3)
        k = (x @ Wk.T).reshape(B, S, N_HEADS, HEAD_DIM).transpose(0, 2, 1, 3)
        v = (x @ Wv.T).reshape(B, S, N_HEADS, HEAD_DIM).transpose(0, 2, 1, 3)
        q = _apply_rope(q)
        k = _apply_rope(k)
        scores = jnp.einsum('bhqd,bhkd->bhqk', q, k) / np.sqrt(HEAD_DIM).astype(np.float32)
        causal = jnp.tril(jnp.ones((S, S), dtype=bool))
        scores = jnp.where(causal, scores, -jnp.inf)
        attn = jax.nn.softmax(scores, axis=-1)
        out = jnp.einsum('bhqk,bhkd->bhqd', attn, v)
        out = out.transpose(0, 2, 1, 3).reshape(B, S, N_HEADS * HEAD_DIM)
        return out @ Wo.T

    def _L0_ffn_ref(x, w_router, corr_bias, gate_w, up_w, down_w, sh_gate_w, sh_up_w, sh_down_w):
        import jax, jax.numpy as jnp
        import numpy as np
        H = 256
        M = 176
        E = 32
        TOPK = 6
        G = 8
        TOPK_G = 4
        SH = 2
        B, S = (1, 128)
        b, s, h = x.shape
        xf = x.reshape(-1, h)
        T = xf.shape[0]
        logits = xf @ w_router
        scores = jax.nn.sigmoid(logits)
        sfc = scores + corr_bias
        grp = sfc.reshape(T, G, E // G)
        top2, _ = jax.lax.top_k(grp, 2)
        group_scores = top2.sum(-1)
        _, gidx = jax.lax.top_k(group_scores, TOPK_G)
        group_mask = jax.nn.one_hot(gidx, G, dtype=jnp.float32).sum(axis=1) > 0
        score_mask = jnp.repeat(group_mask, E // G, axis=1)
        masked = jnp.where(score_mask, sfc, -jnp.inf)
        _, topk_idx = jax.lax.top_k(masked, TOPK)
        topk_w = jnp.take_along_axis(scores, topk_idx, axis=1)
        combine = jnp.zeros((T, E), dtype=x.dtype).at[jnp.arange(T)[:, None], topk_idx].add(topk_w)
        g = jnp.einsum('th,ehm->etm', xf, gate_w)
        u = jnp.einsum('th,ehm->etm', xf, up_w)
        eo = jnp.einsum('etm,emh->eth', jax.nn.silu(g) * u, down_w)
        routed = jnp.einsum('te,eth->th', combine, eo)
        shared = jax.nn.silu(xf @ sh_gate_w) * (xf @ sh_up_w) @ sh_down_w
        return (routed + shared).reshape(b, s, h)
    x = L0_attn_x
    xn = _layernorm(x, axis=-1)
    x = x + _L0_attn_ref(xn, L0_attn_Wq, L0_attn_Wk, L0_attn_Wv, L0_attn_Wo) + _L0_ffn_ref(xn, L0_ffn_w_router, L0_ffn_corr_bias, L0_ffn_gate_w, L0_ffn_up_w, L0_ffn_down_w, L0_ffn_sh_gate_w, L0_ffn_sh_up_w, L0_ffn_sh_down_w)
    return x

_drawn_inputs = setup_inputs


def setup_inputs(seed=0):
    import zlib

    import numpy as np

    out = dict(_drawn_inputs(seed))
    spreads = {}
    factors = {'L0_ffn_w_router': 4.228,
     'L0_ffn_corr_bias': 3.591,
     'L0_ffn_gate_w': 3.008,
     'L0_ffn_up_w': 2.979,
     'L0_ffn_down_w': 2.983,
     'L0_ffn_sh_gate_w': 2.943,
     'L0_ffn_sh_up_w': 2.893,
     'L0_ffn_sh_down_w': 2.898}
    for name, (base, spread) in spreads.items():
        noise = np.random.default_rng([zlib.crc32(name.encode()), seed]).standard_normal(out[name].shape)
        drawn = base * np.exp(spread * noise) if base else spread * noise
        out[name] = jnp.asarray(drawn.astype(out[name].dtype))
    for name, factor in factors.items():
        out[name] = (out[name] * factor).astype(out[name].dtype)
    return out
```

```python
from contextlib import ExitStack

import numpy as np

import concourse.bass as bass
from concourse import mybir

ALU = mybir.AluOpType
ACT = mybir.ActivationFunctionType
AX = mybir.AxisListType
F32 = mybir.dt.float32
BF16 = mybir.dt.bfloat16
I32 = mybir.dt.int32
U32 = mybir.dt.uint32

P = 128
BATCH, SEQ, D = 4, 512, 256
T = BATCH * SEQ
NT = T // P
TPB = SEQ // P
KD = D // P
HEADS, HD = 16, 16
E, M, TOPK = 32, 176, 6
GROUPS, TOPG = 8, 4
PER = E // GROUPS
MS = 2 * M
MH = M // 2
SLOT_TILES = (T * TOPK + E * (P - 1)) // P
EPS = 1e-5
NEG = -3.0e38

CONST_COLS = [("ident", P), ("before", P), ("ones", P), ("expert", E), ("tile", 1), ("steps", NT),
              ("lower", GROUPS * GROUPS), ("cos", TPB * HD), ("nsin", TPB * HD // 2), ("sin", TPB * HD // 2),
              ("future", P), ("futureT", P)]
CONST_AT = {}
_at = 0
for _name, _n in CONST_COLS:
    CONST_AT[_name] = (_at, _at + _n)
    _at += _n
CONST_N = _at


def constants():
    c = np.zeros((P, CONST_N), np.float32)

    def put(name, a):
        lo, hi = CONST_AT[name]
        c[:, lo:hi] = np.asarray(a, np.float32).reshape(P, hi - lo)

    r = np.arange(P)
    put("ident", np.eye(P))
    put("before", r[:, None] < r[None, :])
    put("ones", np.ones((P, P)))
    put("expert", np.broadcast_to(np.arange(E), (P, E)))
    put("tile", r)
    put("steps", np.broadcast_to(np.arange(NT) * P, (P, NT)))
    g = np.arange(GROUPS)
    put("lower", np.broadcast_to((g[None, :] < g[:, None]).reshape(1, -1), (P, GROUPS * GROUPS)))
    inv = (1.0 / np.float32(10000.0) ** (np.arange(0, HD, 2, dtype=np.float32) / np.float32(HD))).astype(np.float32)
    pos = (np.arange(TPB)[None, :] * P + r[:, None]).astype(np.float32)
    ang = (pos[:, :, None] * inv).astype(np.float32)
    put("cos", np.repeat(np.cos(ang), 2, axis=-1))
    put("nsin", -np.sin(ang))
    put("sin", np.sin(ang))
    put("futureT", np.where(r[:, None] > r[None, :], -1.0e30, 0.0))
    put("future", np.where(r[None, :] > r[:, None], -1.0e30, 0.0))
    return c


def repeat(ap, axis, n):
    shape = list(ap.shape)
    assert shape[axis] == 1
    shape[axis] = n
    return ap.broadcast_to(shape)


def wait(eng, sem, n):
    if isinstance(n, int) and n <= 0:
        return
    eng.wait_ge(sem, n)


def ffn_attention_program(nc, A, out, debug=None, stop=9):
    scratch_kind = "ExternalOutput" if debug else "Internal"

    def dram(name, shape, dt):
        return nc.dram_tensor(name, shape, dt, kind=scratch_kind).ap()

    xn_dram = dram("xn_dram", [T, D], F32)
    slots_x = dram("slots_x_dram", [SLOT_TILES * P, D], F32)
    slots_y = dram("slots_y_dram", [SLOT_TILES * P, D], F32)
    shared_y = dram("shared_y_dram", [T, D], F32)
    qk_parts = dram("qk_parts_dram", [3, 2 * KD, P, T], BF16)
    v_dram = dram("v_dram", [T, D], F32)

    with ExitStack() as whole:
        def sb(ctx, name, shape, dt=F32):
            return ctx.enter_context(nc.sbuf_tensor(name, shape, dt))

        bank = [whole.enter_context(nc.psum_tensor(f"bank{i}", [P, 512], F32)) for i in range(8)]
        const = sb(whole, "const", [P, CONST_N])

        def cst(name):
            lo, hi = CONST_AT[name]
            return const[:, lo:hi]

        ident = cst("ident")
        topw = sb(whole, "topw", [P, NT, TOPK])
        slot = sb(whole, "slot", [P, NT, TOPK], U32)

        with ExitStack() as ffn:
            w_gu = sb(ffn, "w_gu", [P, 2, E, KD, M])
            w_dn = sb(ffn, "w_dn", [MH, E, 2, D])
            ws_gu = sb(ffn, "ws_gu", [P, 2, KD, MS])
            ws_dn = sb(ffn, "ws_dn", [MH, 4, D])
            w_qkv = sb(ffn, "w_qkv", [P, KD, 3, D])
            tile_expert = sb(ffn, "tile_expert", [1, P], I32)
            weights_in = ffn.enter_context(nc.semaphore("weights_in"))
            dense_in = ffn.enter_context(nc.semaphore("dense_in"))

            route_block(nc, A, whole, locals())
            dense_block(nc, locals())
            if stop > 2:
                expert_block(nc, locals())
        if stop > 3:
            attention_block(nc, A, out, locals())


def route_block(nc, A, whole, L):
    bank, cst, ident, topw, slot = L["bank"], L["cst"], L["ident"], L["topw"], L["slot"]
    w_gu, w_dn, ws_gu, ws_dn, w_qkv = L["w_gu"], L["w_dn"], L["ws_gu"], L["ws_dn"], L["w_qkv"]
    ZC = 1016
    PAIRS = NT // 2
    with ExitStack() as ctx:
        def sb(name, shape, dt=F32):
            return ctx.enter_context(nc.sbuf_tensor(name, shape, dt))

        def sem(name):
            return ctx.enter_context(nc.semaphore(name))

        x = sb("x", [P, NT, D])
        w_router = sb("w_router", [P, KD, E])
        bias = sb("bias", [P, E])
        zeros = sb("zeros", [P, ZC])
        stats = sb("stats", [P, NT, 6])
        mv = sb("mv", [P, NT, 2])
        var = sb("var", [P, NT])
        std = sb("std", [P, NT])
        rstd = sb("rstd", [P, NT])
        xT = sb("xT", [P, 2, 4, P])
        scores = sb("scores", [P, NT, E])
        sfc = sb("sfc", [P, NT, E])
        spare = w_gu[:, 1, E - 8:E].rearrange("p e k m -> p (e k m)")
        tmpa = spare[:, 0:NT * GROUPS * GROUPS]
        tmpb = spare[:, NT * GROUPS * GROUPS:2 * NT * GROUPS * GROUPS]
        gs = sb("gs", [P, NT, GROUPS])
        keep = sb("keep", [P, NT, GROUPS])
        pen = sb("pen", [P, NT, GROUPS])
        top8 = sb("top8", [P, NT, 8])
        top8i = sb("top8i", [P, NT, 8], U32)
        topf = sb("topf", [P, NT, 8])
        flat = x[:].rearrange("p t n -> p (t n)")
        onehot = flat[:, 0:TOPK * NT * E // 2].bitcast(BF16).rearrange("p (j t e) -> p j t e", j=TOPK, t=NT)
        earlier = flat[:, TOPK * NT * E // 2:TOPK * NT * E // 2 + (NT + 1) * E].rearrange("p (t e) -> p t e", e=E)
        chosen = sb("chosen", [P, NT, E], BF16)
        before16 = sb("before16", [P, P], BF16)
        ones16 = sb("ones16", [P, P], BF16)
        ntile = sb("ntile", [P, 6, E])
        slotf = sb("slotf", [P, NT, TOPK])
        own = sb("own", [P, 1])

        x_in = [sem(f"x_in{i}") for i in range(4)]
        small_in = sem("small_in")
        zero_made = sem("zero_made")
        zero_filled = sem("zero_filled")
        xn_stored = sem("xn_stored")
        var_ready = sem("var_ready")
        std_ready = sem("std_ready")
        xn_ready = sem("xn_ready")
        turned = sem("turned")
        xT_ready = sem("xT_ready")
        logits_done = sem("logits_done")
        sig_done = sem("sig_done")
        step = sem("route_step")
        chosen_ready = sem("chosen_ready")
        counted = sem("counted")
        own_ready = sem("own_ready")
        own_turned = sem("own_turned")
        routed = sem("routed")
        block = ctx.enter_context(nc.Block())

        @block.sync
        def _(sp):
            xv = A["x"].rearrange("(t p) n -> p t n", p=P)
            for i in range(4):
                sp.dma_start(x[:, 4 * i:4 * i + 4, :], xv[:, 4 * i:4 * i + 4, :]).then_inc(x_in[i], 16)
                if i == 0:
                    sp.dma_start(L["const"][:], A["const"]).then_inc(small_in, 16)
                    sp.dma_start(w_router[:], A["w_router"].rearrange("(p k) e -> p k e", k=KD)).then_inc(small_in, 16)
                    sp.dma_start(bias[:], repeat(A["bias"].rearrange("(a e) -> a e", a=1), 0, P)).then_inc(small_in, 16)
            sp.dma_start(w_qkv[:, :, 0, :], A["wqT"].rearrange("(p k) n -> p k n", k=KD)).then_inc(L["dense_in"], 16)
            sp.dma_start(w_qkv[:, :, 1, :], A["wkT"].rearrange("(p k) n -> p k n", k=KD)).then_inc(L["dense_in"], 16)
            sp.dma_start(w_qkv[:, :, 2, :], A["wvT"].rearrange("(p k) n -> p k n", k=KD)).then_inc(L["dense_in"], 16)
            sp.dma_start(ws_gu[:, 0], A["sh_gate"].rearrange("(p k) n -> p k n", k=KD)).then_inc(L["dense_in"], 16)
            sp.dma_start(ws_gu[:, 1], A["sh_up"].rearrange("(p k) n -> p k n", k=KD)).then_inc(L["dense_in"], 16)
            sp.dma_start(ws_dn[:], A["sh_down"].rearrange("(p k) n -> p k n", k=4)).then_inc(L["dense_in"], 16)

            sp.wait_ge(zero_made, 1)
            zv = L["slots_x"].rearrange("(p a) n -> p (a n)", p=P)
            for c in range(SLOT_TILES * D // ZC):
                if c == 10:
                    sp.wait_ge(xn_ready, NT)
                    sp.dma_start(L["xn_dram"].rearrange("(t p) n -> p t n", p=P), x[:]).then_inc(xn_stored, 16)
                sp.dma_start(zv[:, c * ZC:(c + 1) * ZC], zeros[:]).then_inc(zero_filled, 16)
            sp.wait_ge(xn_stored, 16)
            sp.wait_ge(zero_filled, 16 * (SLOT_TILES * D // ZC))

        @block.scalar
        def _(act):
            for j in range(PAIRS + 1):
                if j < PAIRS:
                    act.wait_ge(var_ready, j + 1)
                    nc.scalar.activation(std[:, 2 * j:2 * j + 2], var[:, 2 * j:2 * j + 2], ACT.Sqrt).then_inc(std_ready, 1)
                if j >= 1:
                    act.wait_ge(turned, j)
                    if j >= 3:
                        act.wait_ge(logits_done, j - 2)
                    nc.scalar.activation(xT[:, (j - 1) % 2], bank[(j - 1) % 2][:].rearrange("p (a b) -> p a b", a=4),
                                         ACT.Copy).then_inc(xT_ready, 1)
            act.wait_ge(logits_done, PAIRS)
            nc.scalar.activation(scores[:], bank[2][:].rearrange("p (t e) -> p t e", e=E), ACT.Sigmoid).then_inc(sig_done, 1)

        @block.tensor
        def _(pe):
            pe.wait_ge(small_in, 48)

            def logits(j):
                pe.wait_ge(xT_ready, j + 1)
                for i in range(2):
                    for k in range(KD):
                        mm = pe.matmul(bank[2][:, (2 * j + i) * E:(2 * j + i + 1) * E], xT[:, j % 2, 2 * i + k, :],
                                       w_router[:, k, :], start=(k == 0), stop=(k == KD - 1))
                mm.then_inc(logits_done, 1)

            for j in range(PAIRS):
                pe.wait_ge(xn_ready, 2 * j + 2)
                if j >= 2:
                    pe.wait_ge(xT_ready, j - 1)
                for i in range(2):
                    for k in range(KD):
                        mm = pe.transpose(bank[j % 2][:, (2 * i + k) * P:(2 * i + k + 1) * P],
                                          x[:, 2 * j + i, k::KD], ident)
                mm.then_inc(turned, 1)
                if j >= 1:
                    logits(j - 1)
            logits(PAIRS - 1)
            pe.wait_ge(chosen_ready, 1)
            pe.matmul(bank[3][:], before16[:], chosen[:].rearrange("p t e -> p (t e)"), start=True, stop=True)
            pe.matmul(bank[4][:], ones16[:], chosen[:].rearrange("p t e -> p (t e)"), start=True, stop=True).then_inc(counted, 1)
            pe.wait_ge(own_ready, 1)
            pe.transpose(bank[5][0:1, 0:P], own[:], ident).then_inc(own_turned, 1)

        @block.vector
        def _(dve):
            n = [0]

            def link(ins):
                n[0] += 1
                ins.then_inc(step, 1)
                dve.wait_ge(step, n[0])

            dve.memset(zeros[:], 0.0).then_inc(zero_made, 1)
            for j in range(PAIRS):
                if j % 2 == 0:
                    dve.wait_ge(x_in[j // 2], 16)
                a = slice(2 * j, 2 * j + 2)
                dve.bn_stats(stats[:, 2 * j, :], x[:, 2 * j, :])
                link(dve.bn_stats(stats[:, 2 * j + 1, :], x[:, 2 * j + 1, :]))
                dve.bn_aggr(mv[:, 2 * j, :], stats[:, 2 * j, :])
                link(dve.bn_aggr(mv[:, 2 * j + 1, :], stats[:, 2 * j + 1, :]))
                dve.tensor_scalar(var[:, a], mv[:, a, 1], EPS, None, ALU.add).then_inc(var_ready, 1)
                dve.wait_ge(std_ready, j + 1)
                link(dve.reciprocal(rstd[:, a], std[:, a]))
                for t in range(2 * j, 2 * j + 2):
                    dve.tensor_scalar(x[:, t, :], x[:, t, :], mv[:, t, 0:1], rstd[:, t:t + 1],
                                      ALU.subtract, ALU.mult).then_inc(xn_ready, 1)
            dve.wait_ge(small_in, 48)
            dve.tensor_copy(before16[:], cst("before"))
            dve.tensor_copy(ones16[:], cst("ones"))

            dve.wait_ge(sig_done, 1)
            link(dve.tensor_tensor(sfc[:], scores[:], repeat(bias[:].unsqueeze(1), 1, NT), ALU.add))
            pairs = sfc[:].rearrange("p t (g a b) -> p (t g) a b", a=2, b=2)
            G = NT * GROUPS
            hi = tmpa[:, 0:2 * G].rearrange("p (g a) -> p g a", a=2)
            lo = tmpa[:, 2 * G:4 * G].rearrange("p (g a) -> p g a", a=2)
            dve.tensor_tensor(hi, pairs[:, :, :, 0], pairs[:, :, :, 1], ALU.max)
            link(dve.tensor_tensor(lo, pairs[:, :, :, 0], pairs[:, :, :, 1], ALU.min))
            m1, m2, m3 = tmpb[:, 0:G], tmpb[:, G:2 * G], tmpb[:, 2 * G:3 * G]
            dve.tensor_tensor(m1, hi[:, :, 0], hi[:, :, 1], ALU.max)
            dve.tensor_tensor(m2, hi[:, :, 0], hi[:, :, 1], ALU.min)
            link(dve.tensor_tensor(m3, lo[:, :, 0], lo[:, :, 1], ALU.max))
            link(dve.tensor_tensor(m2, m2, m3, ALU.max))
            gflat = gs[:].rearrange("p t g -> p (t g)")
            link(dve.tensor_tensor(gflat, m1, m2, ALU.add))
            def square(a):
                return a.rearrange("p (t g h) -> p t g h", g=GROUPS, h=GROUPS)
            other = repeat(gs[:].unsqueeze(2), 2, GROUPS)
            this = repeat(gs[:].unsqueeze(3), 3, GROUPS)
            dve.tensor_tensor(square(tmpa), other, this, ALU.is_gt)
            link(dve.tensor_tensor(square(tmpb), other, this, ALU.is_ge))
            lower = repeat(cst("lower").unsqueeze(1), 1, NT)
            link(dve.tensor_tensor(tmpb.rearrange("p (t a) -> p t a", t=NT), tmpb.rearrange("p (t a) -> p t a", t=NT),
                                   lower, ALU.mult))
            link(dve.tensor_tensor(tmpa, tmpa, tmpb, ALU.max))
            link(dve.tensor_reduce(gflat, tmpa.rearrange("p (g h) -> p g h", h=GROUPS), AX.X, ALU.add))
            link(dve.tensor_scalar(keep[:], gs[:], TOPG - 0.5, None, ALU.is_lt))
            dve.tensor_scalar(pen[:], keep[:], -NEG, NEG, ALU.mult, ALU.add)
            s4 = sfc[:].rearrange("p t (g a) -> p (t g) a", a=PER)
            k4 = repeat(keep[:].rearrange("p t g -> p (t g)").unsqueeze(2), 2, PER)
            p4 = repeat(pen[:].rearrange("p t g -> p (t g)").unsqueeze(2), 2, PER)
            link(dve.tensor_tensor(s4, s4, k4, ALU.mult))
            link(dve.tensor_tensor(s4, s4, p4, ALU.add))
            for t in range(NT):
                ins = dve.max(top8[:, t, :], sfc[:, t, :])
            link(ins)
            for t in range(NT):
                ins = dve.max_index(top8i[:, t, :], top8[:, t, :], sfc[:, t, :])
            link(ins)
            link(dve.tensor_copy(topf[:], top8i[:]))
            ex = repeat(cst("expert").unsqueeze(1), 1, NT)
            dve.wait_ge(xn_stored, 16)
            for j in range(TOPK):
                ins = dve.tensor_tensor(onehot[:, j], ex, repeat(topf[:, :, j:j + 1], 2, E), ALU.is_equal)
            link(ins)
            link(dve.tensor_tensor(chosen[:], onehot[:, 0], onehot[:, 1], ALU.add))
            for j in range(2, TOPK):
                ins = dve.tensor_tensor(chosen[:], chosen[:], onehot[:, j], ALU.add)
                if j < TOPK - 1:
                    link(ins)
            ins.then_inc(chosen_ready, 1)
            for j in range(TOPK):
                tm = (tmpa if j % 2 == 0 else tmpb)[:, 0:NT * E].rearrange("p (t e) -> p t e", e=E)
                link(dve.tensor_tensor(tm, onehot[:, j], scores[:], ALU.mult))
                ins = dve.tensor_reduce(topw[:, :, j:j + 1], tm, AX.X, ALU.add)
            link(ins)
            dve.memset(earlier[:, 0, :], 0.0)
            dve.wait_ge(counted, 1)
            per_tile = bank[4][:].rearrange("p (t e) -> p t e", e=E)
            link(dve.tensor_copy(earlier[:, 1, :], per_tile[:, 0, :]))
            for t in range(1, NT):
                link(dve.tensor_tensor(earlier[:, t + 1, :], earlier[:, t, :], per_tile[:, t, :], ALU.add))
            big = tmpa[:, 0:E * NT].rearrange("p (e s) -> p e s", s=NT)
            link(dve.tensor_tensor(big, repeat(earlier[:, NT, :].unsqueeze(2), 2, NT),
                                   repeat(cst("steps").unsqueeze(1), 1, E), ALU.is_gt))
            link(dve.tensor_reduce(ntile[:, 0, :].unsqueeze(2), big, AX.X, ALU.add))
            at, width = 0, 1
            while width < E:
                dve.tensor_copy(ntile[:, at + 1, 0:width], ntile[:, at, 0:width])
                link(dve.tensor_tensor(ntile[:, at + 1, width:E], ntile[:, at, width:E], ntile[:, at, 0:E - width], ALU.add))
                at, width = at + 1, 2 * width
            ends = ntile[:, at, :]
            link(dve.tensor_scalar(tmpb[:, 0:E], ends, cst("tile"), None, ALU.is_le))
            link(dve.tensor_reduce(own[:], tmpb[:, 0:E], AX.X, ALU.add))
            dve.tensor_scalar(own[:], own[:], float(E - 1), None, ALU.min).then_inc(own_ready, 1)
            link(dve.tensor_tensor(ntile[:, 0, :], ends, ntile[:, 0, :], ALU.subtract))
            link(dve.tensor_scalar(ntile[:, 0, :], ntile[:, 0, :], float(P), None, ALU.mult))
            link(dve.tensor_tensor(earlier[:, 0:NT, :], earlier[:, 0:NT, :], repeat(ntile[:, 0:1, :], 1, NT), ALU.add))
            link(dve.tensor_tensor(earlier[:, 0:NT, :], earlier[:, 0:NT, :], bank[3][:].rearrange("p (t e) -> p t e", e=E), ALU.add))
            for j in range(TOPK):
                tm = (tmpa if j % 2 == 0 else tmpb)[:, 0:NT * E].rearrange("p (t e) -> p t e", e=E)
                link(dve.tensor_tensor(tm, onehot[:, j], earlier[:, 0:NT, :], ALU.mult))
                ins = dve.tensor_reduce(slotf[:, :, j:j + 1], tm, AX.X, ALU.add)
            ins.then_inc(routed, 1)
            dve.wait_ge(routed, 1)
            dve.tensor_copy(slot[:], slotf[:])
            dve.wait_ge(own_turned, 1)
            dve.tensor_copy(L["tile_expert"][:], bank[5][0:1, 0:P])


def dense_block(nc, L):
    bank, cst, ident, slot = L["bank"], L["cst"], L["ident"], L["slot"]
    A, w_gu, w_dn, w_qkv, ws_gu, ws_dn = L["A"], L["w_gu"], L["w_dn"], L["w_qkv"], L["ws_gu"], L["ws_dn"]
    psX, psQK, psV, psG, psU, psR, psH, psY = bank
    with ExitStack() as ctx:
        def sb(name, shape, dt=F32):
            return ctx.enter_context(nc.sbuf_tensor(name, shape, dt))

        def sem(name):
            return ctx.enter_context(nc.semaphore(name))

        xin = sb("xin", [P, 2, D])
        idx = sb("idx", [P, 2, TOPK], U32)
        xT = sb("dxT", [P, 2, KD, P])
        rot = sb("rot", [P, 2, 2 * D])
        turn = sb("turn", [P, 2 * D])
        rest = sb("rest", [P, 2 * D])
        parts = sb("parts", [P, 3, 2 * KD, 2, P], BF16)
        vout = sb("vout", [P, 2, D])
        silu = sb("silu", [P, MS])
        h = sb("h", [P, 2, MS])
        hT = sb("hT", [MH, 4, P])
        yout = sb("yout", [P, 2, D])

        x_in = [sem(f"dx_in{i}") for i in range(2)]
        idx_ready = sem("idx_ready")
        waited = sem("waited")
        waited_sp = sem("waited_sp")
        scattered = [sem(f"scattered{i}") for i in range(2)]
        xt_done, xT_ready = sem("xt_done"), sem("xT_ready_d")
        qk_done, rope_cos, rope_read, rot_ready = sem("qk_done"), sem("rope_cos"), sem("rope_read"), sem("rot_ready")
        rotT_done, part1, rest_ready, part2, part3 = (sem(s) for s in ("rotT_done", "part1", "rest_ready", "part2", "part3"))
        v_done, v_copied = sem("v_done"), sem("v_copied")
        g_done, u_done, silu_ready, h_ready = sem("g_done"), sem("u_done"), sem("silu_ready"), sem("h_ready")
        hT_done, hT_ready, y_done, y_copied = sem("hT_done"), sem("hT_ready"), sem("y_done"), sem("y_copied")
        parts_stored = sem("parts_stored")
        v_stored = [sem(f"v_stored{i}") for i in range(2)]
        y_stored = [sem(f"y_stored{i}") for i in range(2)]
        block = ctx.enter_context(nc.Block())

        @block.sync
        def _(sp):
            def load(t, b, use):
                wait(sp, scattered[b], 16 * TOPK * use)
                sp.sem_inc(waited_sp, 1)
                wait(sp, xt_done, t - 1)
                sp.sem_inc(waited_sp, 1)
                sp.dma_start(xin[:, b, :], L["xn_dram"][bass.ts(t, P), :]).then_inc(x_in[b], 16)

            def load_experts(t):
                e = bass.ts(t, 2)
                for g, name in enumerate(("gate_w", "up_w")):
                    sp.dma_start(w_gu[:, g, e], A[name][e].rearrange("e (p k) m -> p e k m", k=KD)).then_inc(L["weights_in"], 16)
                sp.dma_start(w_dn[:, e], A["down_w"][e].rearrange("e (p k) n -> p e k n", k=2)).then_inc(L["weights_in"], 16)

            def store(t, b, use):
                sp.wait_ge(v_copied, t + 1)
                sp.dma_start(L["v_dram"][bass.ts(t, P), :], vout[:, b, :]).then_inc(v_stored[b], 16)

            def store_y(t, b):
                sp.wait_ge(y_copied, t + 1)
                sp.dma_start(L["shared_y"][bass.ts(t, P), :], yout[:, b, :]).then_inc(y_stored[b], 16)

            def store_parts(pair):
                sp.wait_ge(part3, 2 * pair + 2)
                sp.dma_start(L["qk_parts"][:, :, :, bass.ts(pair, 2 * P)].rearrange("a c p t -> p (a c) t"),
                             parts[:].rearrange("p a c b t -> p (a c) (b t)")).then_inc(parts_stored, 16)

            load(0, 0, 0)
            load(1, 1, 0)
            store(0, 0, 0)
            load_experts(0)
            load(2, 0, 1)
            store_y(0, 0)
            store(1, 1, 0)
            load_experts(1)
            store_parts(0)
            with sp.Fori(1, NT // 2 - 1) as i:
                load(2 * i + 1, 1, i)
                store_y(2 * i - 1, 1)
                store(2 * i, 0, i)
                load_experts(2 * i)
                load(2 * i + 2, 0, i + 1)
                store_y(2 * i, 0)
                store(2 * i + 1, 1, i)
                load_experts(2 * i + 1)
                store_parts(i)
            i = NT // 2 - 1
            load(2 * i + 1, 1, i)
            store_y(2 * i - 1, 1)
            store(2 * i, 0, i)
            load_experts(2 * i)
            store_y(2 * i, 0)
            store(2 * i + 1, 1, i)
            load_experts(2 * i + 1)
            store_parts(i)
            store_y(NT - 1, 1)
            sp.wait_ge(L["weights_in"], 16 * 3 * NT)
            for b in range(2):
                sp.wait_ge(v_stored[b], 16 * (NT // 2))
                sp.wait_ge(y_stored[b], 16 * (NT // 2))
            sp.wait_ge(parts_stored, 16 * (NT // 2))

        @block.gpsimd
        def _(pool):
            with pool.Fori(0, NT // 2) as i:
                for b in range(2):
                    t = 2 * i + b
                    pool.wait_ge(x_in[b], 16 * i + 16)
                    pool.tensor_copy(idx[:, b, :], slot[:, bass.ds(t, 1), :].rearrange("p a j -> p (a j)")).then_inc(idx_ready, 1)
                    pool.wait_ge(idx_ready, t + 1)
                    pool.sem_inc(waited, 1)
                    for j in range(TOPK):
                        pool.indirect_dma_start(out=L["slots_x"], out_offset=bass.IndirectOffsetOnAxis(ap=idx[:, b, j:j + 1], axis=0),
                                                in_=xin[:, b, :], in_offset=None).then_inc(scattered[b], 16)
            for b in range(2):
                pool.wait_ge(scattered[b], 16 * TOPK * (NT // 2))

        @block.tensor
        def _(pe):
            pe.wait_ge(L["dense_in"], 96)

            def turn_x(t, b, use):
                pe.wait_ge(x_in[b], 16 * use + 16)
                wait(pe, xT_ready, t)
                for k in range(KD):
                    mm = pe.transpose(psX[:, k * P:(k + 1) * P], xin[:, b, k::KD], ident)
                mm.then_inc(xt_done, 1)

            def turn_h(t, b):
                pe.wait_ge(h_ready, t + 1)
                wait(pe, hT_ready, t)
                for q in range(4):
                    mm = pe.transpose(psH[0:MH, q * P:(q + 1) * P], h[:, b, q::4], ident)
                mm.then_inc(hT_done, 1)

            def down(t):
                pe.wait_ge(hT_ready, t + 1)
                wait(pe, y_copied, t)
                for q in range(4):
                    mm = pe.matmul(psY[:, 0:D], hT[:, q, :], ws_dn[:, q, :], start=(q == 0), stop=(q == 3))
                mm.then_inc(y_done, 1)

            def body(t, b, use, first=False, last=False):
                pe.wait_ge(xT_ready, t + 1)
                wait(pe, rope_read, t)
                for k in range(KD):
                    mm = pe.matmul(psQK[:], xT[:, b, k, :], w_qkv[:, k, 0:2, :].rearrange("p a n -> p (a n)"),
                                   start=(k == 0), stop=(k == KD - 1))
                mm.then_inc(qk_done, 1)
                if not first:
                    turn_h(t - 1, 1 - b)
                wait(pe, v_copied, t)
                for k in range(KD):
                    mm = pe.matmul(psV[:, 0:D], xT[:, b, k, :], w_qkv[:, k, 2, :], start=(k == 0), stop=(k == KD - 1))
                mm.then_inc(v_done, 1)
                if not first:
                    down(t - 1)
                wait(pe, silu_ready, t)
                for k in range(KD):
                    mm = pe.matmul(psG[:, 0:MS], xT[:, b, k, :], ws_gu[:, 0, k, :], start=(k == 0), stop=(k == KD - 1))
                mm.then_inc(g_done, 1)
                wait(pe, h_ready, t)
                for k in range(KD):
                    mm = pe.matmul(psU[:, 0:MS], xT[:, b, k, :], ws_gu[:, 1, k, :], start=(k == 0), stop=(k == KD - 1))
                mm.then_inc(u_done, 1)
                if not last:
                    turn_x(t + 1, 1 - b, use if b == 0 else use + 1)
                pe.wait_ge(rot_ready, t + 1)
                wait(pe, rest_ready, t)
                for c in range(2 * KD):
                    mm = pe.transpose(psR[:, c * P:(c + 1) * P], rot[:, b, c * P:(c + 1) * P], ident)
                mm.then_inc(rotT_done, 1)

            turn_x(0, 0, 0)
            body(0, 0, 0, first=True)
            body(1, 1, 0)
            with pe.Fori(1, NT // 2 - 1) as i:
                body(2 * i, 0, i)
                body(2 * i + 1, 1, i)
            i = NT // 2 - 1
            body(2 * i, 0, i)
            body(2 * i + 1, 1, i, last=True)
            turn_h(NT - 1, 1)
            down(NT - 1)

        @block.scalar
        def _(act):
            def copy_xT(t, b):
                act.wait_ge(xt_done, t + 1)
                wait(act, u_done, t - 1)
                nc.scalar.activation(xT[:, b].rearrange("p k t -> p (k t)"), psX[:, 0:D], ACT.Copy).then_inc(xT_ready, 1)

            def copy_hT(t):
                act.wait_ge(hT_done, t + 1)
                wait(act, y_done, t)
                nc.scalar.activation(hT[:].rearrange("p q t -> p (q t)"), psH[0:MH, :], ACT.Copy).then_inc(hT_ready, 1)

            def body(t, b, use, first=False, last=False):
                if not first:
                    copy_hT(t - 1)
                act.wait_ge(v_done, t + 1)
                wait(act, v_stored[b], 16 * use)
                nc.scalar.activation(vout[:, b, :], psV[:, 0:D], ACT.Copy).then_inc(v_copied, 1)
                act.wait_ge(g_done, t + 1)
                wait(act, h_ready, t)
                nc.scalar.activation(silu[:], psG[:, 0:MS], ACT.Silu).then_inc(silu_ready, 1)
                if not last:
                    copy_xT(t + 1, 1 - b)
                act.wait_ge(rotT_done, t + 1)
                if b == 0:
                    wait(act, parts_stored, 16 * use)
                nc.scalar.activation(parts[:, 0, :, b, :], psR[:].rearrange("p (c t) -> p c t", c=2 * KD), ACT.Copy).then_inc(part1, 1)
                act.wait_ge(rest_ready, t + 1)
                nc.scalar.activation(parts[:, 1, :, b, :], rest[:].rearrange("p (c t) -> p c t", c=2 * KD), ACT.Copy).then_inc(part2, 1)

            copy_xT(0, 0)
            body(0, 0, 0, first=True)
            body(1, 1, 0)
            with act.Fori(1, NT // 2 - 1) as i:
                body(2 * i, 0, i)
                body(2 * i + 1, 1, i)
            i = NT // 2 - 1
            body(2 * i, 0, i)
            body(2 * i + 1, 1, i, last=True)
            copy_hT(NT - 1)

        @block.vector
        def _(dve):
            def copy_y(t, b, use):
                dve.wait_ge(y_done, t + 1)
                wait(dve, y_stored[b], 16 * use)
                dve.tensor_copy(yout[:, b, :], psY[:, 0:D]).then_inc(y_copied, 1)

            def rope(t, b, c):
                dve.wait_ge(qk_done, t + 1)
                wait(dve, rotT_done, t - 1)
                heads = psQK[:].rearrange("p (h d) -> p h d", d=HD)
                pairs = psQK[:].rearrange("p (h i a) -> p h i a", i=HD // 2, a=2)
                tp = turn[:].rearrange("p (h i a) -> p h i a", i=HD // 2, a=2)
                cos = repeat(cst("cos")[:, c * HD:(c + 1) * HD].unsqueeze(1), 1, 2 * HEADS)
                nsin = repeat(cst("nsin")[:, c * HD // 2:(c + 1) * HD // 2].unsqueeze(1), 1, 2 * HEADS)
                sin = repeat(cst("sin")[:, c * HD // 2:(c + 1) * HD // 2].unsqueeze(1), 1, 2 * HEADS)
                dve.tensor_tensor(rot[:, b, :].rearrange("p (h d) -> p h d", d=HD), heads, cos, ALU.mult)
                dve.tensor_tensor(tp[:, :, :, 0], pairs[:, :, :, 1], nsin, ALU.mult)
                dve.tensor_tensor(tp[:, :, :, 1], pairs[:, :, :, 0], sin, ALU.mult).then_inc(rope_read, 1)
                dve.wait_ge(rope_read, t + 1)
                dve.tensor_tensor(rot[:, b, :], rot[:, b, :], turn[:], ALU.add).then_inc(rot_ready, 1)

            def split(t, b):
                dve.wait_ge(part1, t + 1)
                wait(dve, part3, t)
                dve.tensor_tensor(rest[:].rearrange("p (c t) -> p c t", c=2 * KD), psR[:].rearrange("p (c t) -> p c t", c=2 * KD),
                                  parts[:, 0, :, b, :], ALU.subtract).then_inc(rest_ready, 1)

            def body(t, b, use, c, first=False):
                rope(t, b, c)
                if not first:
                    copy_y(t - 1, 1 - b, (use if b == 1 else use - 1))
                dve.wait_ge(u_done, t + 1)
                dve.wait_ge(silu_ready, t + 1)
                wait(dve, hT_done, t - 1)
                dve.tensor_tensor(h[:, b, :], psU[:, 0:MS], silu[:], ALU.mult).then_inc(h_ready, 1)
                split(t, b)
                dve.wait_ge(part2, t + 1)
                dve.tensor_tensor(parts[:, 2, :, b, :], rest[:].rearrange("p (c t) -> p c t", c=2 * KD),
                                  parts[:, 1, :, b, :], ALU.subtract).then_inc(part3, 1)

            for t in range(TPB):
                body(t, t % 2, t // 2, t, first=(t == 0))
            with dve.Fori(1, NT // TPB) as g:
                for c in range(TPB):
                    body(TPB * g + c, c % 2, (TPB // 2) * g + c // 2, c)
            copy_y(NT - 1, 1, NT // 2 - 1)

def expert_block(nc, L):
    ident, w_gu, w_dn, tile_expert = L["ident"], L["w_gu"], L["w_dn"], L["tile_expert"]
    bank = L["bank"]
    psX, psGU, psH, psY = bank[0:2], bank[2:4], bank[4:6], bank[6:8]
    N = SLOT_TILES
    FIRST = 5
    assert (N - FIRST) % 2 == 0
    with ExitStack() as ctx:
        def sb(name, shape, dt=F32):
            return ctx.enter_context(nc.sbuf_tensor(name, shape, dt))

        def sem(name):
            return ctx.enter_context(nc.semaphore(name))

        xg = sb("xg", [P, 2, D])
        xT = sb("exT", [P, 2, KD, P])
        silu = sb("esilu", [P, 2, M])
        h = sb("eh", [P, 2, M])
        hT = sb("ehT", [MH, 2, 2, P])
        y = sb("ey", [P, 2, D])
        x_in = [sem(f"ex_in{i}") for i in range(2)]
        y_stored = [sem(f"ey_stored{i}") for i in range(2)]
        xt_done, xT_ready, gu_done, silu_ready, h_ready, ht_done, hT_ready, y_done, y_copied = (
            sem(f"e_{s}") for s in ("xt_done", "xT_ready", "gu_done", "silu_ready", "h_ready", "ht_done", "hT_ready",
                                    "y_done", "y_copied"))
        block = ctx.enter_context(nc.Block())

        def steps(eng, step):
            for s in range(FIRST):
                step(s, s % 2, s // 2)
            with eng.Fori(FIRST // 2, N // 2) as i:
                step(2 * i + 1, 1, i)
                step(2 * i + 2, 0, i + 1)
            for s in range(N, N + 3):
                step(s, s % 2, s // 2)

        def inside(j):
            return not isinstance(j, int) or 0 <= j < N

        @block.sync
        def _(sp):
            def load(j, b, use):
                wait(sp, xt_done, j - 1)
                sp.dma_start(xg[:, b, :], L["slots_x"][bass.ts(j, P), :]).then_inc(x_in[b], 16)

            for j in range(3):
                load(j, j % 2, j // 2)
            with sp.Fori(1, N // 2) as i:
                load(2 * i + 1, 1, i)
                load(2 * i + 2, 0, i + 1)

        @block.gpsimd
        def _(pool):
            def store(j, b):
                pool.wait_ge(y_copied, j + 1)
                pool.dma_start(L["slots_y"][bass.ts(j, P), :], y[:, b, :]).then_inc(y_stored[b], 16)

            store(0, 0)
            with pool.Fori(0, N // 2) as i:
                store(2 * i + 1, 1)
                store(2 * i + 2, 0)
            pool.wait_ge(y_stored[0], 16 * ((N + 1) // 2))
            pool.wait_ge(y_stored[1], 16 * (N // 2))

        @block.tensor
        def _(pe):
            def turn_x(j, b, use):
                pe.wait_ge(x_in[b], 16 * use + 16)
                wait(pe, xT_ready, j - 1)
                for k in range(KD):
                    mm = pe.transpose(psX[b][:, k * P:(k + 1) * P], xg[:, b, k::KD], ident)
                mm.then_inc(xt_done, 1)

            def gate_up(j, b, e):
                pe.wait_ge(xT_ready, j + 1)
                wait(pe, h_ready, j - 1)
                for k in range(KD):
                    mm = pe.matmul(psGU[b][:, 0:2 * M].rearrange("p (g m) -> p g m", g=2), xT[:, b, k, :],
                                   w_gu[:, :, bass.ds(e, 1), k, :].rearrange("p g e m -> p g (e m)"),
                                   start=(k == 0), stop=(k == KD - 1))
                mm.then_inc(gu_done, 1)

            def turn_h(j, b):
                pe.wait_ge(h_ready, j + 1)
                wait(pe, hT_ready, j - 1)
                for k in range(2):
                    mm = pe.transpose(psH[b][0:MH, k * P:(k + 1) * P], h[:, b, k::2], ident)
                mm.then_inc(ht_done, 1)

            def down(j, b, e):
                pe.wait_ge(hT_ready, j + 1)
                wait(pe, y_copied, j - 1)
                for k in range(2):
                    mm = pe.matmul(psY[b][:, 0:D], hT[:, b, k, :], w_dn[:, bass.ds(e, 1), k, :].rearrange("p e n -> p (e n)"),
                                   start=(k == 0), stop=(k == 1))
                mm.then_inc(y_done, 1)

            def expert(j):
                return pe.value_load(tile_expert[0:1, bass.ds(j, 1)], min_val=0, max_val=E - 1)

            coming = pe.alloc_register("coming_expert")

            def read_ahead(j):
                pe.reg_load(coming, tile_expert[0:1, bass.ds(j, 1)])

            def step(s, b, use):
                if inside(s - 3):
                    turn_h(s - 3, 1 - b)
                if inside(s):
                    turn_x(s, b, use)
                if inside(s - 1):
                    gate_up(s - 1, 1 - b, pe.snap(coming, min_val=0, max_val=E - 1))
                if inside(s - 3):
                    down(s - 3, 1 - b, expert(s - 3))
                if inside(s):
                    read_ahead(s)

            steps(pe, step)

        @block.scalar
        def _(act):
            def copy_hT(j, b):
                act.wait_ge(ht_done, j + 1)
                wait(act, y_done, j - 1)
                nc.scalar.activation(hT[:, b].rearrange("p k t -> p (k t)"), psH[b][0:MH, 0:2 * P], ACT.Copy).then_inc(hT_ready, 1)

            def gate(j, b):
                act.wait_ge(gu_done, j + 1)
                wait(act, h_ready, j - 1)
                nc.scalar.activation(silu[:, b, :], psGU[b][:, 0:M], ACT.Silu).then_inc(silu_ready, 1)

            def step(s, b, use):
                if inside(s - 3):
                    copy_hT(s - 3, 1 - b)
                if inside(s - 1):
                    gate(s - 1, 1 - b)

            steps(act, step)

        @block.vector
        def _(dve):
            def copy_xT(j, b):
                dve.wait_ge(xt_done, j + 1)
                wait(dve, gu_done, j - 1)
                dve.tensor_copy(xT[:, b].rearrange("p k t -> p (k t)"), psX[b][:, 0:D]).then_inc(xT_ready, 1)

            def gated(j, b):
                dve.wait_ge(silu_ready, j + 1)
                wait(dve, ht_done, j - 1)
                dve.tensor_tensor(h[:, b, :], psGU[b][:, M:2 * M], silu[:, b, :], ALU.mult).then_inc(h_ready, 1)

            def copy_y(j, b, use):
                dve.wait_ge(y_done, j + 1)
                wait(dve, y_stored[b], 16 * use)
                dve.tensor_copy(y[:, b, :], psY[b][:, 0:D]).then_inc(y_copied, 1)

            def step(s, b, use):
                if inside(s):
                    copy_xT(s, b)
                if inside(s - 1):
                    gated(s - 1, 1 - b)
                if inside(s - 3):
                    copy_y(s - 3, 1 - b, use - 1 if b == 1 else use - 2)

            steps(dve, step)


def attention_block(nc, A, out, L):
    bank, cst, ident, slot, topw = L["bank"], L["cst"], L["ident"], L["slot"], L["topw"]
    G = 4
    NG = BATCH * HEADS // G
    GPB = HEADS // G
    LEAD = 5
    QPART, KPART = (0, 0, 1, 0, 1, 2), (0, 1, 0, 2, 1, 0)
    ROWS = len(QPART) * HD
    WIDE = [SEQ - P * j for j in range(TPB)]
    AT = [0, SEQ, 2 * SEQ, 2 * SEQ - WIDE[3]]
    PT_N = sum(WIDE)
    MAXBATCHES = 3
    SCALE = 1.0 / np.sqrt(HD)
    bST, bS, bO, bT, bW = bank[0:3], bank[3:5], bank[5], bank[6], bank[7]
    MUNITS = [(3, [h]) for h in range(G)] + [(2, [h]) for h in range(G)] + [(1, [0, 1]), (1, [2, 3]), (0, [0, 1, 2, 3])]
    NM = len(MUNITS)
    SUNITS = []
    for h in (0, 2):
        SUNITS += [[(h, 0, 0)], [(h, 1, 0), (h, 3, WIDE[1])], [(h, 2, 0), (h + 1, 2, WIDE[2])],
                   [(h + 1, 0, 0)], [(h + 1, 1, 0), (h + 1, 3, WIDE[1])]]
    NS = len(SUNITS)
    max_dram = nc.dram_tensor("max_dram", [BATCH, 3, HEADS, SEQ], BF16, kind="Internal").ap()

    with ExitStack() as ctx:
        def sb(name, shape, dt=F32):
            return ctx.enter_context(nc.sbuf_tensor(name, shape, dt))

        def sem(name):
            return ctx.enter_context(nc.semaphore(name))

        qs = sb("qs", [ROWS + 3, MAXBATCHES, HEADS, SEQ], BF16)
        ks = sb("ks", [ROWS + 3, MAXBATCHES, HEADS, SEQ], BF16)
        vraw = sb("vraw", [P, NG, TPB, G * HD])
        vpad = sb("vpad", [P, 2, TPB, G, 32])
        pt = sb("pt", [P, 2, G, PT_N])
        oT = sb("oT", [P, 2, SEQ])
        attn = sb("attn", [P, TPB, D])
        aT = sb("aT", [P, TPB, KD, P])
        recip = sb("recip", [P, TPB, G])
        mx = sb("mx", [P, 2, TPB, HEADS])
        negm = sb("negm", [HEADS, 3, SEQ], BF16)
        mrest = sb("mrest", [HEADS, SEQ])
        w_o = sb("w_o", [P, KD, D])
        ident16 = sb("ident16", [P, P], BF16)
        future16 = sb("future16", [P, P], BF16)
        futureT16 = sb("futureT16", [P, P], BF16)
        gath = sb("gath", [P, 2, TOPK, D])
        base = sb("base", [P, 2, 2, D])
        acc = sb("acc", [P, 2 * TPB, D])
        idx = sb("cidx", [P, 2, TOPK], U32)

        qk_in = [sem(f"qk_in{b}") for b in range(BATCH)]
        v_in, wo_in, ones_ready, masks_ready = sem("v_in"), sem("wo_in"), sem("ones_ready"), sem("masks_ready")
        vpad_zero, vpad_ready = sem("vpad_zero"), sem("vpad_ready")
        s_done, s_read = sem("s_done"), sem("s_read")
        m_turned, m_part1, m_rest, m_part2, m_part3, m_out = (sem(f"m_{s}") for s in ("turned", "part1", "rest", "part2", "part3", "out"))
        m_in = [sem(f"m_in{b}") for b in range(BATCH)]
        st_done, exp_done = sem("st_done"), sem("exp_done")
        pv_done, oT_ready, o_turned, recip_ready, attn_ready = (sem(s) for s in ("pv_done", "oT_ready", "o_turned", "recip_ready", "attn_ready"))
        a_turned, aT_ready, wo_done, added = (sem(s) for s in ("a_turned", "aT_ready", "wo_done", "added"))
        base_in = [sem(f"base_in{b}") for b in range(2)]
        gathered = [sem(f"gathered{b}") for b in range(2)]
        cidx_ready, cwaited = sem("cidx_ready"), sem("cwaited")
        combine, combined, stored = sem("combine"), sem("combined"), sem("stored")
        block = ctx.enter_context(nc.Block())

        @block.sync
        def _(sp):
            def load_qk(b):
                if b >= MAXBATCHES:
                    sp.wait_ge(st_done, NS * GPB * (b - MAXBATCHES + 1))
                for r, (q, k) in enumerate(zip(QPART, KPART)):
                    rows = slice(HD * r, HD * (r + 1))
                    for dst, part, c in ((qs, q, 0), (ks, k, KD)):
                        sp.dma_start(dst[rows, b % MAXBATCHES],
                                     L["qk_parts"][part, c:c + KD, :, SEQ * b:SEQ * (b + 1)].rearrange("c (h d) t -> d (c h) t", d=HD)
                                     ).then_inc(qk_in[b], 16)

            def load_base(t):
                wait(sp, combined, t - 1)
                sp.dma_start(base[:, t % 2, 0, :], A["x"][t * P:(t + 1) * P, :]).then_inc(base_in[t % 2], 16)
                sp.dma_start(base[:, t % 2, 1, :], L["shared_y"][t * P:(t + 1) * P, :]).then_inc(base_in[t % 2], 16)

            def max_rows(b):
                sp.wait_ge(m_part3, b + 1)
                sp.dma_start(max_dram[b].rearrange("a h t -> h a t"), negm[:]).then_inc(m_out, 16)
                sp.wait_ge(m_out, 16 * (b + 1))
                sp.dma_start(qs[ROWS:ROWS + 3, b % MAXBATCHES], max_dram[b]).then_inc(m_in[b], 16)

            load_qk(0)
            for b in range(BATCH):
                sp.dma_start(vraw[:, GPB * b:GPB * (b + 1)],
                             L["v_dram"][SEQ * b:SEQ * (b + 1), :].rearrange("(j p) (g n) -> p g j n", p=P, g=GPB)).then_inc(v_in, 16)
            sp.dma_start(w_o[:], A["woT"].rearrange("(p k) n -> p k n", k=KD)).then_inc(wo_in, 16)
            load_qk(1)
            load_qk(2)
            load_base(0)
            load_base(1)
            max_rows(0)
            for k in range(2, NT):
                if k == GPB + 1:
                    load_qk(3)
                load_base(k)
                if k % GPB == 0:
                    max_rows(k // GPB)
            sp.wait_ge(stored, 16 * BATCH)

        @block.gpsimd
        def _(pool):
            pool.memset(vpad[:], 0.0).then_inc(vpad_zero, 1)
            pool.wait_ge(vpad_zero, 1)
            pool.memset(vpad[:, :, :, :, HD:HD + 1], 1.0).then_inc(vpad_zero, 1)
            pool.wait_ge(vpad_zero, 2)
            pool.wait_ge(v_in, 16 * BATCH)

            def body(t, b, use):
                wait(pool, pv_done, t - 1)
                pool.sem_inc(cwaited, 1)
                pool.tensor_copy(vpad[:, b, :, :, 0:HD],
                                 vraw[:, bass.ds(t, 1)].rearrange("p a j (h d) -> p (a j) h d", d=HD)).then_inc(vpad_ready, 1)
                wait(pool, combined, t - 1)
                pool.sem_inc(cwaited, 1)
                pool.tensor_copy(idx[:, b, :], slot[:, bass.ds(t, 1), :].rearrange("p a j -> p (a j)")).then_inc(cidx_ready, 1)
                pool.wait_ge(cidx_ready, t + 1)
                pool.sem_inc(cwaited, 1)
                for j in range(TOPK):
                    pool.indirect_dma_start(out=gath[:, b, j, :], out_offset=None, in_=L["slots_y"],
                                            in_offset=bass.IndirectOffsetOnAxis(ap=idx[:, b, j:j + 1], axis=0)).then_inc(gathered[b], 16)

            body(0, 0, 0)
            body(1, 1, 0)
            with pool.Fori(1, NT // 2) as i:
                body(2 * i, 0, i)
                body(2 * i + 1, 1, i)

        @block.tensor
        def _(pe):
            pe.wait_ge(masks_ready, 3)

            def max_unit(g, u):
                b, n = g // GPB, NM * g + u
                c, heads = MUNITS[u]
                if u == 0:
                    pe.wait_ge(qk_in[b], 16 * 12)
                wait(pe, s_read, n - 1)
                bk, w = bS[n % 2], P * (c + 1)
                for i, h in enumerate(heads):
                    hh = G * (g % GPB) + h
                    pe.matmul(bk[:, i * w:(i + 1) * w], qs[0:ROWS, b % MAXBATCHES, hh, c * P:(c + 1) * P],
                              ks[0:ROWS, b % MAXBATCHES, hh, 0:w], start=True, stop=True)
                    mm = pe.matmul(bk[:, i * w + c * P:(i + 1) * w], ident16[:], future16[:], start=False, stop=True,
                                   skip_group_check=True)
                mm.then_inc(s_done, 1)

            def exp_unit(g, u):
                b, n = g // GPB, NS * g + u
                if u == 0:
                    pe.wait_ge(m_in[b], 16)
                    pe.wait_ge(ones_ready, 1)
                wait(pe, exp_done, n - 2)
                bk = bST[n % 3]
                for h, j, col in SUNITS[u]:
                    hh = G * (g % GPB) + h
                    pe.matmul(bk[:, col:col + WIDE[j]], ks[:, b % MAXBATCHES, hh, j * P:(j + 1) * P],
                              qs[:, b % MAXBATCHES, hh, j * P:SEQ], start=True, stop=True)
                    mm = pe.matmul(bk[:, col:col + P], ident16[:], futureT16[:], start=False, stop=True, skip_group_check=True)
                mm.then_inc(st_done, 1)

            def pv(g):
                pe.wait_ge(exp_done, NS * (g + 1))
                pe.wait_ge(vpad_ready, g + 1)
                wait(pe, oT_ready, g)
                for j in range(TPB):
                    for h in range(G):
                        mm = pe.matmul(bO[32 * h:32 * h + 32, j * P:SEQ], vpad[:, g % 2, j, h, :],
                                       pt[:, g % 2, h, AT[j]:AT[j] + WIDE[j]], start=(j == 0), stop=True,
                                       skip_group_check=True)
                mm.then_inc(pv_done, 1)

            def turn_o(g):
                pe.wait_ge(oT_ready, g + 1)
                wait(pe, attn_ready, g)
                for c in range(TPB):
                    mm = pe.transpose(bT[:, c * P:(c + 1) * P], oT[:, g % 2, c * P:(c + 1) * P], ident)
                mm.then_inc(o_turned, 1)

            def turn_max(b):
                pe.wait_ge(s_read, NM * GPB * (b + 1))
                if b >= 2:
                    pe.wait_ge(added, 2 * (b - 2) + 2)
                wait(pe, m_rest, b)
                for c in range(TPB):
                    mm = pe.transpose(bW[0:HEADS, c * P:(c + 1) * P], mx[:, b % 2, c, :], ident)
                mm.then_inc(m_turned, 1)

            def turn_attn(b, half):
                pe.wait_ge(attn_ready, GPB * (b + 1))
                wait(pe, m_rest, min(b + 2, BATCH))
                wait(pe, added, 2 * b)
                if half:
                    pe.wait_ge(aT_ready, 2 * b + 1)
                for c in range(2):
                    for k in range(KD):
                        mm = pe.transpose(bW[:, (2 * c + k) * P:(2 * c + k + 1) * P], attn[:, 2 * half + c, k::KD], ident)
                mm.then_inc(a_turned, 1)

            def project(b, half):
                pe.wait_ge(aT_ready, 2 * b + 2)
                if half:
                    pe.wait_ge(added, 2 * b + 1)
                for c in range(2):
                    for k in range(KD):
                        mm = pe.matmul(bW[:, c * D:(c + 1) * D], aT[:, 2 * half + c, k, :], w_o[:, k, :],
                                       start=(k == 0), stop=(k == KD - 1))
                mm.then_inc(wo_done, 1)

            for g in range(LEAD):
                for u in range(NM):
                    max_unit(g, u)
                if g == GPB - 1:
                    turn_max(0)
            pe.wait_ge(wo_in, 16)
            for g in range(NG + 2):
                b, r = g // GPB, g % GPB
                for u in range(NM):
                    if g + LEAD < NG:
                        max_unit(g + LEAD, u)
                    if g < NG and u < NS:
                        exp_unit(g, u)
                    if u == 3 and 1 <= g <= NG:
                        pv(g - 1)
                    if u == 6 and r == 1 and b >= 1:
                        turn_attn(b - 1, 0)
                    if u == 8 and r == 1 and b >= 1:
                        turn_attn(b - 1, 1)
                if 1 <= g <= NG:
                    turn_o(g - 1)
                if r == 1 and b >= 1:
                    project(b - 1, 0)
                    project(b - 1, 1)
                if (g + LEAD) % GPB == GPB - 1 and g + LEAD < NG:
                    turn_max((g + LEAD) // GPB)

        @block.scalar
        def _(act):
            nc.scalar.activation(ident16[:], ident, ACT.Copy).then_inc(masks_ready, 1)
            nc.scalar.activation(future16[:], cst("future"), ACT.Copy).then_inc(masks_ready, 1)
            nc.scalar.activation(futureT16[:], cst("futureT"), ACT.Copy).then_inc(masks_ready, 1)

            def exp_unit(g, u):
                n = NS * g + u
                act.wait_ge(st_done, n + 1)
                if u == 0:
                    wait(act, pv_done, g - 1)
                bk = bST[n % 3]
                pieces = SUNITS[u]
                if len(pieces) == 1 or pieces[0][0] == pieces[1][0]:
                    h, j, _ = pieces[0]
                    nc.scalar.activation(pt[:, g % 2, h, AT[j]:AT[j] + SEQ], bk[:], ACT.Exp, scale=float(SCALE)).then_inc(exp_done, 1)
                else:
                    h, j, _ = pieces[0]
                    nc.scalar.activation(pt[:, g % 2, h:h + 2, AT[j]:AT[j] + WIDE[j]], bk[:].rearrange("p (h q) -> p h q", h=2),
                                         ACT.Exp, scale=float(SCALE)).then_inc(exp_done, 1)

            def copy_o(g):
                act.wait_ge(pv_done, g + 1)
                wait(act, o_turned, g - 1)
                nc.scalar.activation(oT[:, g % 2, :], bO[:], ACT.Copy).then_inc(oT_ready, 1)

            def part1(b):
                act.wait_ge(m_turned, b + 1)
                wait(act, m_out, 16 * b)
                nc.scalar.activation(negm[:, 0, :], bW[0:HEADS, :], ACT.Copy, scale=-1.0).then_inc(m_part1, 1)

            def copy_attn(b, half):
                act.wait_ge(a_turned, 2 * b + half + 1)
                wait(act, wo_done, 2 * b)
                nc.scalar.activation(aT[:, 2 * half:2 * half + 2].rearrange("p c k t -> p (c k t)"), bW[:], ACT.Copy).then_inc(aT_ready, 1)

            part1(0)
            for g in range(NG + 2):
                b, r = g // GPB, g % GPB
                for u in range(NS):
                    if g < NG:
                        exp_unit(g, u)
                    if u == 5 and 1 <= g <= NG:
                        copy_o(g - 1)
                    if u == 7 and r == 1 and b >= 1:
                        copy_attn(b - 1, 0)
                    if u == 9 and r == 1 and b >= 1:
                        copy_attn(b - 1, 1)
                if (g + LEAD) % GPB == GPB - 1 and g + LEAD < NG:
                    part1((g + LEAD) // GPB)
                if r == 1 and b >= 1:
                    act.wait_ge(added, 2 * b)
                    act.dma_start(out[SEQ * (b - 1):SEQ * b, :].rearrange("(c p) n -> p c n", p=P),
                                  acc[:, TPB * ((b - 1) % 2):TPB * ((b - 1) % 2 + 1), :]).then_inc(stored, 16)

        @block.vector
        def _(dve):
            dve.memset(ks[ROWS:ROWS + 3, :, :, :], 1.0).then_inc(ones_ready, 1)
            n_combine = [0]

            def max_unit(g, u):
                b, n = g // GPB, NM * g + u
                c, heads = MUNITS[u]
                w, h0 = P * (c + 1), G * (g % GPB) + heads[0]
                dve.wait_ge(s_done, n + 1)
                if u == 0:
                    wait(dve, m_turned, b - 1)
                dve.tensor_reduce(mx[:, b % 2, c, h0:h0 + len(heads)], bS[n % 2][:, 0:w * len(heads)].rearrange("p (h k) -> p h k", k=w),
                                  AX.X, ALU.max).then_inc(s_read, 1)

            def split_max(b):
                dve.wait_ge(m_part1, b + 1)
                dve.scalar_tensor_tensor(out=mrest[:], in0=bW[0:HEADS, :], scalar=-1.0, in1=negm[:, 0, :],
                                         op0=ALU.mult, op1=ALU.subtract).then_inc(m_rest, 1)
                dve.wait_ge(m_rest, b + 1)
                dve.tensor_copy(negm[:, 1, :], mrest[:]).then_inc(m_part2, 1)
                dve.wait_ge(m_part2, b + 1)
                dve.tensor_tensor(negm[:, 2, :], mrest[:], negm[:, 1, :], ALU.subtract).then_inc(m_part3, 1)

            def add_experts(t, j):
                a = acc[:, t % (2 * TPB), :]
                if j < 0:
                    dve.wait_ge(base_in[t % 2], 32 * (t // 2 + 1))
                    if t % TPB == 0 and t >= 2 * TPB:
                        dve.wait_ge(stored, 16 * (t // TPB - 1))
                    ins = dve.tensor_tensor(a, base[:, t % 2, 0, :], base[:, t % 2, 1, :], ALU.add)
                else:
                    dve.wait_ge(combine, n_combine[0])
                    if j == 0:
                        dve.wait_ge(gathered[t % 2], 16 * TOPK * (t // 2 + 1))
                    ins = dve.scalar_tensor_tensor(out=a, in0=gath[:, t % 2, j, :], scalar=topw[:, t, j:j + 1], in1=a,
                                                   op0=ALU.mult, op1=ALU.add)
                if j == TOPK - 1:
                    ins.then_inc(combined, 1)
                else:
                    n_combine[0] += 1
                    ins.then_inc(combine, 1)

            def normalise(g):
                dve.wait_ge(o_turned, g + 1)
                if g % GPB == 0:
                    wait(dve, a_turned, 2 * (g // GPB))
                o = bT[:].rearrange("p (c h x) -> p c h x", c=TPB, h=G)
                dve.reciprocal(recip[:], o[:, :, :, HD]).then_inc(recip_ready, 1)
                dve.wait_ge(recip_ready, g + 1)
                dst = attn[:, :, G * HD * (g % GPB):G * HD * (g % GPB + 1)].rearrange("p c (h d) -> p c h d", h=G)
                dve.tensor_tensor(dst, o[:, :, :, 0:HD], repeat(recip[:].unsqueeze(3), 3, HD), ALU.mult).then_inc(attn_ready, 1)

            def add_attention(b, half):
                dve.wait_ge(wo_done, 2 * b + half + 1)
                dve.wait_ge(combined, TPB * (b + 1))
                a = acc[:, TPB * (b % 2) + 2 * half:TPB * (b % 2) + 2 * half + 2, :].rearrange("p c n -> p (c n)")
                dve.tensor_tensor(a, bW[:], a, ALU.add).then_inc(added, 1)

            for g in range(LEAD):
                for u in range(NM):
                    max_unit(g, u)
                if g == GPB - 1:
                    split_max(0)
            for g in range(NG + 2):
                b, r = g // GPB, g % GPB
                for u in range(NM):
                    if g + LEAD < NG:
                        max_unit(g + LEAD, u)
                    if g < NT and u < TOPK + 1:
                        add_experts(g, u - 1)
                if 1 <= g <= NG:
                    normalise(g - 1)
                if r == 1 and b >= 1:
                    add_attention(b - 1, 0)
                    add_attention(b - 1, 1)
                if (g + LEAD) % GPB == GPB - 1 and g + LEAD < NG:
                    split_max((g + LEAD) // GPB)



INPUTS = {"x": "L0_attn_x", "wqT": "L0_attn_Wq", "wkT": "L0_attn_Wk", "wvT": "L0_attn_Wv", "woT": "L0_attn_Wo",
          "w_router": "L0_ffn_w_router", "bias": "L0_ffn_corr_bias", "gate_w": "L0_ffn_gate_w", "up_w": "L0_ffn_up_w",
          "down_w": "L0_ffn_down_w", "sh_gate": "L0_ffn_sh_gate_w", "sh_up": "L0_ffn_sh_up_w", "sh_down": "L0_ffn_sh_down_w"}


def host_arrays(inputs):
    arrays = {}
    for short, name in INPUTS.items():
        a = np.asarray(inputs[name])
        if short == "x":
            a = a.reshape(T, D)
        arrays[short] = np.ascontiguousarray(a.T if short.endswith("T") else a)
    arrays["const"] = constants()
    return arrays


def kernel(**inputs):
    from concourse import bacc
    from concourse.bass_utils import run_bass_kernel_spmd

    nc = bacc.Bacc("TRN2", target_bir_lowering=False, num_devices=1)
    arrays = host_arrays(inputs)
    A = {n: nc.dram_tensor(f"in_{n}_dram", a.shape, mybir.dt.from_np(a.dtype), kind="ExternalInput").ap()
         for n, a in arrays.items()}
    out = nc.dram_tensor("out_dram", [T, D], F32, kind="ExternalOutput").ap()
    ffn_attention_program(nc, A, out)
    r = run_bass_kernel_spmd(nc, [{f"in_{n}_dram": a for n, a in arrays.items()}], core_ids=[0])
    return r.results[0]["out_dram"].reshape(BATCH, SEQ, D)
```

```python
from contextlib import ExitStack

import numpy as np

import concourse.bass as bass
from concourse import mybir

ALU = mybir.AluOpType
ACT = mybir.ActivationFunctionType
AX = mybir.AxisListType
F32 = mybir.dt.float32
F16 = mybir.dt.float16
BF16 = mybir.dt.bfloat16
I32 = mybir.dt.int32
U32 = mybir.dt.uint32

P = 128
BATCH, SEQ, D = 4, 512, 256
T = BATCH * SEQ
NT = T // P
TPB = SEQ // P
KD = D // P
HEADS, HD = 16, 16
E, M, TOPK = 32, 176, 6
GROUPS, TOPG = 8, 4
PER = E // GROUPS
MS = 2 * M
MH = M // 2
SLOT_TILES = (T * TOPK + E * (P - 1)) // P
QPART, KPART = (0, 0, 1, 0, 1, 2), (0, 1, 0, 2, 1, 0)
ROWS = len(QPART) * HD
EPS = 1e-5
NEG = -3.0e38

CONST_COLS = [("ident", P), ("before", P), ("row", P), ("expert", E), ("tile", 1), ("steps", NT),
              ("lower", GROUPS * GROUPS), ("cos", TPB * HD), ("nsin", TPB * HD // 2), ("sin", TPB * HD // 2),
              ("future", P), ("futureT", P)]
CONST_AT = {}
_at = 0
for _name, _n in CONST_COLS:
    CONST_AT[_name] = (_at, _at + _n)
    _at += _n
CONST_N = _at


def constants():
    c = np.zeros((P, CONST_N), np.float32)

    def put(name, a):
        lo, hi = CONST_AT[name]
        c[:, lo:hi] = np.asarray(a, np.float32).reshape(P, hi - lo)

    r = np.arange(P)
    put("ident", np.eye(P))
    put("before", r[:, None] < r[None, :])
    put("row", np.broadcast_to(r, (P, P)))
    put("expert", np.broadcast_to(np.arange(E), (P, E)))
    put("tile", r)
    put("steps", np.broadcast_to(np.arange(NT) * P, (P, NT)))
    g = np.arange(GROUPS)
    put("lower", np.broadcast_to((g[None, :] < g[:, None]).reshape(1, -1), (P, GROUPS * GROUPS)))
    inv = (1.0 / np.float32(10000.0) ** (np.arange(0, HD, 2, dtype=np.float32) / np.float32(HD))).astype(np.float32)
    pos = (np.arange(TPB)[None, :] * P + r[:, None]).astype(np.float32)
    ang = (pos[:, :, None] * inv).astype(np.float32)
    put("cos", np.repeat(np.cos(ang), 2, axis=-1))
    put("nsin", -np.sin(ang))
    put("sin", np.sin(ang))
    put("futureT", np.where(r[:, None] > r[None, :], -1.0e30, 0.0))
    put("future", np.where(r[None, :] > r[:, None], -1.0e30, 0.0))
    return c


def repeat(ap, axis, n):
    shape = list(ap.shape)
    assert shape[axis] == 1
    shape[axis] = n
    return ap.broadcast_to(shape)


class Carver:

    def __init__(self, tensor):
        self.tensor, self.at = tensor, 0

    def __call__(self, shape, dt=F32):
        n = int(np.prod(shape[1:]))
        words = n if dt in (F32, U32) else n // 2
        piece = self.tensor[0:shape[0], self.at:self.at + words]
        self.at += words
        assert self.at <= self.tensor.shape[1]
        if dt != F32:
            piece = piece.bitcast(dt)
        if len(shape) == 2:
            return piece
        names = [f"d{i}" for i in range(len(shape) - 1)]
        return piece.rearrange(f"p ({' '.join(names)}) -> p {' '.join(names)}", **dict(zip(names, shape[1:])))


def operand_loads(qk_parts, q, k, b, half):
    for i, (qpart, kpart) in enumerate(zip(QPART, KPART)):
        rows = slice(HD * i, HD * (i + 1))
        for dst, part, chunk in ((q, qpart, half), (k, kpart, KD + half)):
            yield (dst[rows, HEADS // KD * half:HEADS // KD * (half + 1)],
                   qk_parts[part, chunk, :, SEQ * b:SEQ * (b + 1)].rearrange("(h d) t -> d h t", d=HD))


def wait(eng, sem, n):
    if isinstance(n, int) and n <= 0:
        return
    eng.wait_ge(sem, n)


def ffn_attention_program(nc, A, out, debug=None, stop=9):
    scratch_kind = "ExternalOutput" if debug else "Internal"

    def dram(name, shape, dt):
        return nc.dram_tensor(name, shape, dt, kind=scratch_kind).ap()

    xn_dram = dram("xn_dram", [T, D], F32)
    slots_y = dram("slots_y_dram", [SLOT_TILES * P, D], F32)
    shared_y = dram("shared_y_dram", [T, D], F32)
    qk_parts = dram("qk_parts_dram", [3, 2 * KD, P, T], BF16)
    v_dram = dram("v_dram", [T, D], F32)

    with ExitStack() as whole:
        def sb(ctx, name, shape, dt=F32):
            return ctx.enter_context(nc.sbuf_tensor(name, shape, dt))

        bank = [whole.enter_context(nc.psum_tensor(f"bank{i}", [P, 512], F32)) for i in range(8)]
        const = sb(whole, "const", [P, CONST_N])

        def cst(name):
            lo, hi = CONST_AT[name]
            return const[:, lo:hi]

        ident = cst("ident")
        topw = sb(whole, "topw", [P, NT, TOPK])
        slot = sb(whole, "slot", [P, NT, TOPK], U32)
        front = sb(whole, "front", [P, HEADS * SEQ])
        first_qk = Carver(front)
        q_first, k_first = (first_qk([P, HEADS, SEQ], BF16)[0:ROWS + 3] for _ in range(2))
        qk_in = [[whole.enter_context(nc.semaphore(f"qk_in{b}_{half}")) for half in range(KD)] for b in range(BATCH)]
        ones_made = whole.enter_context(nc.semaphore("ones_made"))

        with ExitStack() as ffn:
            w_gu = sb(ffn, "w_gu", [P, 2, E, KD, M])
            w_dn = sb(ffn, "w_dn", [MH, E, 2, D])
            tile_expert = sb(ffn, "tile_expert", [1, P], I32)
            slot_token = sb(ffn, "slot_token", [P, P], U32)
            place = sb(ffn, "place", [P, 2, NT, TOPK], F16)
            token16 = sb(ffn, "token16", [P, NT], F16)
            row16 = sb(ffn, "row16", [P, P], F16)
            weights_in = ffn.enter_context(nc.semaphore("weights_in"))
            dense_in = ffn.enter_context(nc.semaphore("dense_in"))
            down_in = ffn.enter_context(nc.semaphore("down_in"))
            shared_in = ffn.enter_context(nc.semaphore("shared_in"))
            h_ready = ffn.enter_context(nc.semaphore("h_ready"))
            xT_all, h_all = (w_gu[:, g, E - NT:E].rearrange("p e k m -> p e (k m)") for g in range(2))

            with ExitStack() as dense:
                ws_gu = sb(dense, "ws_gu", [P, 2, KD, MS])
                ws_dn = sb(dense, "ws_dn", [MH, 4, D])
                w_qkv = sb(dense, "w_qkv", [P, KD, 3, D])
                route_block(nc, A, whole, locals())
                dense_block(nc, locals())
            if stop > 2:
                expert_block(nc, locals())
        if stop > 3:
            attention_block(nc, A, out, locals())


def route_block(nc, A, whole, L):
    bank, cst, ident, topw, slot = L["bank"], L["cst"], L["ident"], L["topw"], L["slot"]
    w_gu, w_dn, ws_gu, ws_dn, w_qkv = L["w_gu"], L["w_dn"], L["ws_gu"], L["ws_dn"], L["w_qkv"]
    PAIRS = NT // 2
    COUNT_AFTER, OWN_AFTER = 8, 12
    with ExitStack() as ctx:
        def sb(name, shape, dt=F32):
            return ctx.enter_context(nc.sbuf_tensor(name, shape, dt))

        def sem(name):
            return ctx.enter_context(nc.semaphore(name))

        front = Carver(L["front"])
        x = front([P, NT, D])
        w_router = sb("w_router", [P, KD, E])
        bias = sb("bias", [P, E])
        stats = sb("stats", [P, NT, 6])
        mv = sb("mv", [P, NT, 2])
        var = sb("var", [P, NT])
        std = sb("std", [P, NT])
        gated = front([P, 2, MS])
        rstd = sb("rstd", [P, NT])
        xT_all, h_all = L["xT_all"], L["h_all"]
        scores = front([P, NT, E])
        sfc = front([P, NT, E])
        spare = w_gu[:, 1, 0:NT].rearrange("p e k m -> p (e k m)")
        tmpa = spare[:, 0:NT * GROUPS * GROUPS]
        tmpb = spare[:, NT * GROUPS * GROUPS:2 * NT * GROUPS * GROUPS]
        wide = w_gu[:, 0, 0:NT].rearrange("p e k m -> p (e k m)")[:, 0:TOPK * NT * E].rearrange("p (j t e) -> p j t e", j=TOPK, t=NT)
        gs = front([P, NT, GROUPS])
        keep = front([P, NT, GROUPS])
        pen = front([P, NT, GROUPS])
        top8 = front([P, NT, 8])
        top8i = front([P, NT, 8], U32)
        topf = front([P, NT, 8])
        flat = x[:].rearrange("p t n -> p (t n)")
        onehot = flat[:, 0:TOPK * NT * E // 2].bitcast(BF16).rearrange("p (j t e) -> p j t e", j=TOPK, t=NT)
        earlier = flat[:, TOPK * NT * E // 2:TOPK * NT * E // 2 + NT * E].rearrange("p (t e) -> p t e", e=E)
        chosen = front([P, NT, E], BF16)
        before16 = sb("before16", [P, P], BF16)
        ones16 = sb("ones16", [P, P], BF16)
        ntile = sb("ntile", [P, 6, E])
        slotf = front([P, NT, TOPK])
        own = sb("own", [P, 1])
        digits = front([P, 2, NT, TOPK], U32)

        x_in = [sem(f"x_in{i}") for i in range(4)]
        small_in = sem("small_in")
        g_done, u_done, silu_ready, u_copied = (sem(s) for s in ("sg_done", "su_done", "ssilu_ready", "u_copied"))
        xn_stored = sem("xn_stored")
        var_ready = sem("var_ready")
        std_ready = sem("std_ready")
        xn_ready = sem("xn_ready")
        turned = sem("turned")
        xT_ready = sem("xT_ready")
        logits_done = sem("logits_done")
        sig_done = sem("sig_done")
        step = sem("route_step")
        chosen_ready = sem("chosen_ready")
        counted = sem("counted")
        own_ready = sem("own_ready")
        own_turned = sem("own_turned")
        block = ctx.enter_context(nc.Block())

        @block.sync
        def _(sp):
            xv = A["x"].rearrange("(t p) n -> p t n", p=P)
            for i in range(4):
                sp.dma_start(x[:, 4 * i:4 * i + 4, :], xv[:, 4 * i:4 * i + 4, :]).then_inc(x_in[i], 16)
                if i == 0:
                    sp.dma_start(L["const"][:], A["const"]).then_inc(small_in, 16)
                    sp.dma_start(w_router[:], A["w_router"].rearrange("(p k) e -> p k e", k=KD)).then_inc(small_in, 16)
                    sp.dma_start(bias[:], repeat(A["bias"].rearrange("(a e) -> a e", a=1), 0, P)).then_inc(small_in, 16)
            sp.dma_start(ws_gu[:, 0], A["sh_gate"].rearrange("(p k) n -> p k n", k=KD)).then_inc(L["shared_in"], 16)
            sp.dma_start(ws_gu[:, 1], A["sh_up"].rearrange("(p k) n -> p k n", k=KD)).then_inc(L["shared_in"], 16)
            sp.dma_start(w_qkv[:, :, 0, :], A["wqT"].rearrange("(p k) n -> p k n", k=KD)).then_inc(L["dense_in"], 16)
            sp.dma_start(w_qkv[:, :, 1, :], A["wkT"].rearrange("(p k) n -> p k n", k=KD)).then_inc(L["dense_in"], 16)
            sp.dma_start(w_qkv[:, :, 2, :], A["wvT"].rearrange("(p k) n -> p k n", k=KD)).then_inc(L["dense_in"], 16)
            sp.dma_start(ws_dn[:], A["sh_down"].rearrange("(p k) n -> p k n", k=4)).then_inc(L["dense_in"], 16)
            sp.wait_ge(xn_ready, NT)
            sp.dma_start(L["xn_dram"].rearrange("(t p) n -> p t n", p=P), x[:]).then_inc(xn_stored, 16)
            sp.wait_ge(xn_stored, 16)
            for e in range(0, E, 8):
                sp.dma_start(w_dn[:, e:e + 8], A["down_w"][e:e + 8].rearrange("e (p k) n -> p e k n", k=2)).then_inc(L["down_in"], 16)
            sp.wait_ge(L["dense_in"], 64)

        @block.gpsimd
        def _(pool):
            for t in range(NT):
                pool.wait_ge(silu_ready, t + 1)
                pool.wait_ge(u_copied, t + 1)
                pool.tensor_tensor(h_all[:, t, :], h_all[:, t, :], gated[:, t % 2, :], ALU.mult).then_inc(L["h_ready"], 1)

        @block.scalar
        def _(act):
            def root(half):
                act.wait_ge(var_ready, half + 1)
                own_tiles = slice(half * NT // 2, (half + 1) * NT // 2)
                nc.scalar.activation(std[:, own_tiles], var[:, own_tiles], ACT.Sqrt).then_inc(std_ready, 1)

            root(0)
            for j in range(PAIRS):
                if j == PAIRS // 2 - 1:
                    root(1)
                act.wait_ge(turned, j + 1)
                nc.scalar.activation(xT_all[:, 2 * j:2 * j + 2, 0:D], bank[j % 2][:].rearrange("p (a b) -> p a b", a=2),
                                     ACT.Copy).then_inc(xT_ready, 1)
            act.wait_ge(logits_done, PAIRS)
            nc.scalar.activation(scores[:], bank[2][:].rearrange("p (t e) -> p t e", e=E), ACT.Sigmoid).then_inc(sig_done, 1)
            for t in range(NT):
                act.wait_ge(g_done, t + 1)
                wait(act, L["h_ready"], t - 1)
                nc.scalar.activation(gated[:, t % 2, :], bank[6][:, 0:MS], ACT.Silu).then_inc(silu_ready, 1)
                act.wait_ge(u_done, t + 1)
                nc.scalar.activation(h_all[:, t, :], bank[7][:, 0:MS], ACT.Copy).then_inc(u_copied, 1)

        @block.tensor
        def _(pe):
            pe.wait_ge(small_in, 48)

            def logits(j):
                pe.wait_ge(xT_ready, j + 1)
                for t in range(2 * j, 2 * j + 2):
                    for k in range(KD):
                        mm = pe.matmul(bank[2][:, t * E:(t + 1) * E], xT_all[:, t, k * P:(k + 1) * P],
                                       w_router[:, k, :], start=(k == 0), stop=(k == KD - 1))
                mm.then_inc(logits_done, 1)

            def shared_hidden(t):
                if t == 0:
                    pe.wait_ge(L["shared_in"], 32)
                wait(pe, silu_ready, t)
                for k in range(KD):
                    mm = pe.matmul(bank[6][:, 0:MS], xT_all[:, t, k * P:(k + 1) * P], ws_gu[:, 0, k, :], start=(k == 0), stop=(k == KD - 1))
                mm.then_inc(g_done, 1)
                wait(pe, u_copied, t)
                for k in range(KD):
                    mm = pe.matmul(bank[7][:, 0:MS], xT_all[:, t, k * P:(k + 1) * P], ws_gu[:, 1, k, :], start=(k == 0), stop=(k == KD - 1))
                mm.then_inc(u_done, 1)

            def count():
                pe.wait_ge(chosen_ready, 1)
                pe.matmul(bank[3][:], before16[:], chosen[:].rearrange("p t e -> p (t e)"), start=True, stop=True)
                for t in range(NT - 1):
                    pe.matmul(bank[3][:, (t + 1) * E:NT * E].rearrange("p (t e) -> p t e", e=E), ones16[:],
                              repeat(chosen[:, t:t + 1, :], 1, NT - 1 - t), start=False, stop=True, skip_group_check=True)
                for t in range(NT):
                    mm = pe.matmul(bank[4][:, 0:E], ones16[:], chosen[:, t, :], start=(t == 0), stop=(t == NT - 1))
                mm.then_inc(counted, 1)

            for j in range(PAIRS):
                pe.wait_ge(xn_ready, 2 * j + 2)
                if j >= 2:
                    pe.wait_ge(xT_ready, j - 1)
                for i in range(2):
                    for k in range(KD):
                        mm = pe.transpose(bank[j % 2][:, (2 * i + k) * P:(2 * i + k + 1) * P],
                                          x[:, 2 * j + i, k::KD], ident)
                mm.then_inc(turned, 1)
                if j >= 1:
                    logits(j - 1)
            logits(PAIRS - 1)
            for t in range(NT):
                shared_hidden(t)
                if t == COUNT_AFTER:
                    count()
                if t == OWN_AFTER:
                    pe.wait_ge(own_ready, 1)
                    pe.transpose(bank[5][0:1, 0:P], own[:], ident).then_inc(own_turned, 1)

        @block.vector
        def _(dve):
            n = [0]

            def link(ins):
                n[0] += 1
                ins.then_inc(step, 1)
                dve.wait_ge(step, n[0])

            for half in range(2):
                tiles = range(half * NT // 2, (half + 1) * NT // 2)
                own_tiles = slice(tiles[0], tiles[-1] + 1)
                for t in tiles:
                    if t % 4 == 0:
                        dve.wait_ge(x_in[t // 4], 16)
                    ins = dve.bn_stats(stats[:, t, :], x[:, t, :])
                link(ins)
                for t in tiles:
                    ins = dve.bn_aggr(mv[:, t, :], stats[:, t, :])
                link(ins)
                dve.tensor_scalar(var[:, own_tiles], mv[:, own_tiles, 1], EPS, None, ALU.add).then_inc(var_ready, 1)
                dve.wait_ge(std_ready, half + 1)
                link(dve.reciprocal(rstd[:, own_tiles], std[:, own_tiles]))
                for t in tiles:
                    dve.tensor_scalar(x[:, t, :], x[:, t, :], mv[:, t, 0:1], rstd[:, t:t + 1],
                                      ALU.subtract, ALU.mult).then_inc(xn_ready, 1)
            dve.wait_ge(small_in, 48)
            dve.tensor_copy(before16[:], cst("before"))
            dve.memset(ones16[:], 1.0)
            dve.tensor_copy(L["row16"][:], cst("row"))
            dve.tensor_scalar(L["token16"][:], cst("steps"), cst("tile"), None, ALU.add)

            dve.wait_ge(sig_done, 1)
            link(dve.tensor_tensor(sfc[:], scores[:], repeat(bias[:].unsqueeze(1), 1, NT), ALU.add))
            pairs = sfc[:].rearrange("p t (g a b) -> p (t g) a b", a=2, b=2)
            G = NT * GROUPS
            hi = tmpa[:, 0:2 * G].rearrange("p (g a) -> p g a", a=2)
            lo = tmpa[:, 2 * G:4 * G].rearrange("p (g a) -> p g a", a=2)
            dve.tensor_tensor(hi, pairs[:, :, :, 0], pairs[:, :, :, 1], ALU.max)
            link(dve.tensor_tensor(lo, pairs[:, :, :, 0], pairs[:, :, :, 1], ALU.min))
            m1, m2, m3 = tmpb[:, 0:G], tmpb[:, G:2 * G], tmpb[:, 2 * G:3 * G]
            dve.tensor_tensor(m1, hi[:, :, 0], hi[:, :, 1], ALU.max)
            dve.tensor_tensor(m2, hi[:, :, 0], hi[:, :, 1], ALU.min)
            link(dve.tensor_tensor(m3, lo[:, :, 0], lo[:, :, 1], ALU.max))
            link(dve.tensor_tensor(m2, m2, m3, ALU.max))
            gflat = gs[:].rearrange("p t g -> p (t g)")
            link(dve.tensor_tensor(gflat, m1, m2, ALU.add))
            def square(a):
                return a.rearrange("p (t g h) -> p t g h", g=GROUPS, h=GROUPS)
            other = repeat(gs[:].unsqueeze(2), 2, GROUPS)
            this = repeat(gs[:].unsqueeze(3), 3, GROUPS)
            dve.tensor_tensor(square(tmpa), other, this, ALU.is_gt)
            link(dve.tensor_tensor(square(tmpb), other, this, ALU.is_ge))
            lower = repeat(cst("lower").unsqueeze(1), 1, NT)
            link(dve.tensor_tensor(tmpb.rearrange("p (t a) -> p t a", t=NT), tmpb.rearrange("p (t a) -> p t a", t=NT),
                                   lower, ALU.mult))
            link(dve.tensor_tensor(tmpa, tmpa, tmpb, ALU.max))
            link(dve.tensor_reduce(gflat, tmpa.rearrange("p (g h) -> p g h", h=GROUPS), AX.X, ALU.add))
            link(dve.tensor_scalar(keep[:], gs[:], TOPG - 0.5, None, ALU.is_lt))
            dve.tensor_scalar(pen[:], keep[:], -NEG, NEG, ALU.mult, ALU.add)
            s4 = sfc[:].rearrange("p t (g a) -> p (t g) a", a=PER)
            k4 = repeat(keep[:].rearrange("p t g -> p (t g)").unsqueeze(2), 2, PER)
            p4 = repeat(pen[:].rearrange("p t g -> p (t g)").unsqueeze(2), 2, PER)
            link(dve.tensor_tensor(s4, s4, k4, ALU.mult))
            link(dve.tensor_tensor(s4, s4, p4, ALU.add))
            for t in range(NT):
                ins = dve.max(top8[:, t, :], sfc[:, t, :])
            link(ins)
            for t in range(NT):
                ins = dve.max_index(top8i[:, t, :], top8[:, t, :], sfc[:, t, :])
            link(ins)
            link(dve.tensor_copy(topf[:], top8i[:]))
            ex = repeat(cst("expert").unsqueeze(1), 1, NT)
            dve.wait_ge(xn_stored, 16)
            for j in range(TOPK):
                ins = dve.tensor_tensor(onehot[:, j], ex, repeat(topf[:, :, j:j + 1], 2, E), ALU.is_equal)
            link(ins)
            link(dve.tensor_tensor(chosen[:], onehot[:, 0], onehot[:, 1], ALU.add))
            for j in range(2, TOPK):
                ins = dve.tensor_tensor(chosen[:], chosen[:], onehot[:, j], ALU.add)
                if j < TOPK - 1:
                    link(ins)
            ins.then_inc(chosen_ready, 1)
            for j in range(TOPK):
                ins = dve.tensor_tensor(wide[:, j], onehot[:, j], scores[:], ALU.mult)
            link(ins)
            link(dve.tensor_reduce(topw[:].rearrange("p t j -> p j t"), wide, AX.X, ALU.add))
            dve.wait_ge(counted, 1)
            big = tmpa[:, 0:E * NT].rearrange("p (e s) -> p e s", s=NT)
            link(dve.tensor_tensor(big, repeat(bank[4][:, 0:E].unsqueeze(2), 2, NT),
                                   repeat(cst("steps").unsqueeze(1), 1, E), ALU.is_gt))
            link(dve.tensor_reduce(ntile[:, 0, :].unsqueeze(2), big, AX.X, ALU.add))
            at, width = 0, 1
            while width < E:
                dve.tensor_copy(ntile[:, at + 1, 0:width], ntile[:, at, 0:width])
                link(dve.tensor_tensor(ntile[:, at + 1, width:E], ntile[:, at, width:E], ntile[:, at, 0:E - width], ALU.add))
                at, width = at + 1, 2 * width
            ends = ntile[:, at, :]
            link(dve.tensor_scalar(tmpb[:, 0:E], ends, cst("tile"), None, ALU.is_le))
            link(dve.tensor_reduce(own[:], tmpb[:, 0:E], AX.X, ALU.add))
            dve.tensor_scalar(own[:], own[:], float(E - 1), None, ALU.min).then_inc(own_ready, 1)
            link(dve.tensor_tensor(ntile[:, 0, :], ends, ntile[:, 0, :], ALU.subtract))
            link(dve.tensor_scalar(ntile[:, 0, :], ntile[:, 0, :], float(P), None, ALU.mult))
            link(dve.tensor_tensor(earlier, bank[3][:].rearrange("p (t e) -> p t e", e=E), repeat(ntile[:, 0:1, :], 1, NT), ALU.add))
            for j in range(TOPK):
                ins = dve.tensor_tensor(wide[:, j], onehot[:, j], earlier, ALU.mult)
            link(ins)
            link(dve.tensor_reduce(slotf[:].rearrange("p t j -> p j t"), wide, AX.X, ALU.add))
            link(dve.tensor_copy(slot[:], slotf[:]))
            dve.tensor_scalar(digits[:, 0], slot[:], 7, None, ALU.logical_shift_right)
            link(dve.tensor_scalar(digits[:, 1], slot[:], P - 1, None, ALU.bitwise_and))
            dve.tensor_copy(L["place"][:], digits[:])
            dve.wait_ge(own_turned, 1)
            dve.tensor_copy(L["tile_expert"][:], bank[5][0:1, 0:P])


def dense_block(nc, L):
    bank, cst, ident = L["bank"], L["cst"], L["ident"]
    A, w_gu, w_dn, w_qkv, ws_dn = L["A"], L["w_gu"], L["w_dn"], L["w_qkv"], L["ws_dn"]
    place, token16, row16 = L["place"], L["token16"], L["row16"]
    psList, psQK, psV, _, _, psR, psH, psY = bank
    with ExitStack() as ctx:
        def sb(name, shape, dt=F32):
            return ctx.enter_context(nc.sbuf_tensor(name, shape, dt))

        def sem(name):
            return ctx.enter_context(nc.semaphore(name))

        front = Carver(L["front"])
        xT = front([P, 2, D])
        h = front([P, 2, MS])
        xres = front([P, 2, D])
        rot = front([P, 2, 2 * D])
        swapped = front([P, 2 * D])
        rest = front([P, 2 * D])
        parts = front([P, 2, 3, 2 * KD, 2, P], BF16)
        free = L["ws_gu"][:].rearrange("p g k m -> p (g k m)")
        vout = free[:, 0:2 * D].rearrange("p (b n) -> p b n", b=2)
        at_place = free[:, 2 * D:2 * D + TOPK * P].bitcast(F16).rearrange("p (b j a) -> p b j a", b=2, j=TOPK)
        hT = front([MH, 4, P])
        yout = sb("yout", [P, 2, D])
        in_tile = front([P, 2, TOPK, P], F16)

        tile_of, tile_of_ready = sb("tile_of", [P, 2, TOPK]), sem("tile_of_ready")
        waited, waited_sp = sem("waited"), sem("waited_sp")
        copied, xres_in = sem("copied"), [sem(f"xres_in{b}") for b in range(2)]
        tile_ready, place_cmp, place_ready, listed = sem("tile_ready"), sem("place_cmp"), sem("place_ready"), sem("listed")
        qk_done, rope_read, rot_ready = sem("qk_done"), sem("rope_read"), sem("rot_ready")
        rotT_done, part1, rest_ready, part2, part3 = (sem(s) for s in ("rotT_done", "part1", "rest_ready", "part2", "part3"))
        v_done, v_copied = sem("v_done"), sem("v_copied")
        hT_done, hT_ready, y_done, y_ready, y_summed = (sem(s) for s in ("hT_done", "hT_ready", "y_done", "y_ready", "y_summed"))
        parts_stored = [sem(f"parts_stored{i}") for i in range(2)]
        v_stored = [sem(f"v_stored{i}") for i in range(2)]
        y_stored = [sem(f"y_stored{i}") for i in range(2)]
        block = ctx.enter_context(nc.Block())

        def tiles(eng, body):
            for c in range(TPB):
                body(c, c, 0)
            with eng.Fori(1, NT // TPB) as g:
                for c in range(TPB):
                    body(TPB * g + c, c, g)

        @block.sync
        def _(sp):
            def load_x(t, b):
                wait(sp, y_summed, t - 1)
                sp.sem_inc(waited_sp, 1)
                sp.dma_start(xres[:, b, :], A["x"][bass.ts(t, P), :]).then_inc(xres_in[b], 16)

            def load_experts(t):
                sp.wait_ge(copied, t + 1)
                sp.sem_inc(waited_sp, 1)
                e = bass.ts(t, 2)
                for g, name in enumerate(("gate_w", "up_w")):
                    sp.dma_start(w_gu[:, g, e], A[name][e].rearrange("e (p k) m -> p e k m", k=KD)).then_inc(L["weights_in"], 16)

            def store(t, c, g):
                b, pair = c % 2, c // 2
                sp.wait_ge(v_copied, t + 1)
                sp.dma_start(L["v_dram"][bass.ts(t, P), :], vout[:, b, :]).then_inc(v_stored[b], 16)
                sp.wait_ge(y_summed, t + 1)
                sp.dma_start(L["shared_y"][bass.ts(t, P), :], yout[:, b, :]).then_inc(y_stored[b], 16)
                if b == 1:
                    sp.wait_ge(part3, t + 1)
                    sp.dma_start(L["qk_parts"][:, :, :, bass.ts(2 * g + pair, 2 * P)].rearrange("a c p t -> p (a c) t"),
                                 parts[:, pair].rearrange("p a c b t -> p (a c) (b t)")).then_inc(parts_stored[pair], 16)

            def body(t, c, g):
                load_x(t, c % 2)
                load_experts(t)
                if not (isinstance(t, int) and t == 0):
                    store(t - 1, (c - 1) % TPB, g if c else g - 1)

            tiles(sp, body)
            store(NT - 1, TPB - 1, NT // TPB - 1)
            sp.wait_ge(L["weights_in"], 16 * 2 * NT)
            sp.wait_ge(L["down_in"], 16 * 4)
            for b in range(2):
                sp.wait_ge(v_stored[b], 16 * (NT // 2))
                sp.wait_ge(y_stored[b], 16 * (NT // 2))
                sp.wait_ge(parts_stored[b], 16 * (NT // TPB))

        @block.gpsimd
        def _(pool):
            def add_x(t, c, g):
                b, pair = c % 2, c // 2
                pool.wait_ge(y_ready, t + 1)
                pool.sem_inc(waited, 1)
                pool.wait_ge(xres_in[b], 16 * (2 * g + pair) + 16)
                pool.sem_inc(waited, 1)
                pool.tensor_tensor(yout[:, b, :], yout[:, b, :], xres[:, b, :], ALU.add).then_inc(y_summed, 1)

            def body(t, c, g):
                b = c % 2
                if not (isinstance(t, int) and t == 0):
                    add_x(t - 1, (c - 1) % TPB, g if c else g - 1)
                wait(pool, listed, t - 1)
                pool.sem_inc(waited, 1)
                pool.tensor_copy(tile_of[:, b, :], place[:, 0, bass.ds(t, 1), :].rearrange("p t j -> p (t j)")).then_inc(tile_of_ready, 1)
                pool.wait_ge(tile_of_ready, t + 1)
                pool.sem_inc(waited, 1)
                for j in range(TOPK):
                    ins = pool.tensor_scalar(in_tile[:, b, j, :], row16[:], tile_of[:, b, j:j + 1], None, ALU.is_equal)
                ins.then_inc(tile_ready, 1)

            tiles(pool, body)
            add_x(NT - 1, TPB - 1, NT // TPB - 1)

        @block.tensor
        def _(pe):
            def list_tokens(t, b):
                pe.wait_ge(tile_ready, t + 1)
                pe.wait_ge(place_ready, t + 1)
                for j in range(TOPK):
                    mm = pe.matmul(psList[:, 0:P], at_place[:, b, j, :], in_tile[:, b, j, :],
                                   start=(isinstance(t, int) and t == 0 and j == 0), stop=True, skip_group_check=True)
                mm.then_inc(listed, 1)

            def body(t, c, g):
                b = c % 2
                if isinstance(t, int) and t == 0:
                    pe.wait_ge(L["dense_in"], 64)
                pe.wait_ge(copied, t + 1)
                wait(pe, rope_read, t)
                for k in range(KD):
                    mm = pe.matmul(psQK[:], xT[:, b, k * P:(k + 1) * P], w_qkv[:, k, 0:2, :].rearrange("p a n -> p (a n)"),
                                   start=(k == 0), stop=(k == KD - 1))
                mm.then_inc(qk_done, 1)
                wait(pe, hT_ready, t)
                for q in range(4):
                    mm = pe.transpose(psH[0:MH, q * P:(q + 1) * P], h[:, b, q::4], ident)
                mm.then_inc(hT_done, 1)
                wait(pe, v_copied, t)
                for k in range(KD):
                    mm = pe.matmul(psV[:, 0:D], xT[:, b, k * P:(k + 1) * P], w_qkv[:, k, 2, :], start=(k == 0), stop=(k == KD - 1))
                mm.then_inc(v_done, 1)
                pe.wait_ge(hT_ready, t + 1)
                wait(pe, y_ready, t)
                for q in range(4):
                    mm = pe.matmul(psY[:, 0:D], hT[:, q, :], ws_dn[:, q, :], start=(q == 0), stop=(q == 3))
                mm.then_inc(y_done, 1)
                if not (isinstance(t, int) and t == 0):
                    list_tokens(t - 1, 1 - b)
                pe.wait_ge(rot_ready, t + 1)
                wait(pe, rest_ready, t)
                for q in range(2 * KD):
                    mm = pe.transpose(psR[:, q * P:(q + 1) * P], rot[:, b, q * P:(q + 1) * P], ident)
                mm.then_inc(rotT_done, 1)

            tiles(pe, body)
            list_tokens(NT - 1, 1)

        @block.scalar
        def _(act):
            def fetch(t, b):
                wait(act, v_done, t - 1)
                nc.scalar.activation(xT[:, b, :], L["xT_all"][:, bass.ds(t, 1), 0:D].rearrange("p t n -> p (t n)"), ACT.Copy)
                nc.scalar.activation(h[:, b, :], L["h_all"][:, bass.ds(t, 1), :].rearrange("p t n -> p (t n)"), ACT.Copy).then_inc(copied, 1)

            def second(t, c):
                b, pair = c % 2, c // 2
                act.wait_ge(rest_ready, t + 1)
                nc.scalar.activation(parts[:, pair, 1, :, b, :], rest[:].rearrange("p (c t) -> p c t", c=2 * KD), ACT.Copy).then_inc(part2, 1)

            def body(t, c, g, last=False):
                b, pair = c % 2, c // 2
                act.wait_ge(hT_done, t + 1)
                wait(act, y_done, t)
                nc.scalar.activation(hT[:].rearrange("p q t -> p (q t)"), psH[0:MH, :], ACT.Copy).then_inc(hT_ready, 1)
                if not (isinstance(t, int) and t == 0):
                    second(t - 1, (c - 1) % TPB)
                act.wait_ge(v_done, t + 1)
                wait(act, v_stored[b], 16 * (2 * g + pair))
                nc.scalar.activation(vout[:, b, :], psV[:, 0:D], ACT.Copy).then_inc(v_copied, 1)
                if not last:
                    fetch(t + 1, 1 - b)
                act.wait_ge(y_done, t + 1)
                wait(act, y_stored[b], 16 * (2 * g + pair))
                nc.scalar.activation(yout[:, b, :], psY[:, 0:D], ACT.Copy).then_inc(y_ready, 1)
                act.wait_ge(rotT_done, t + 1)
                if b == 0:
                    wait(act, parts_stored[pair], 16 * g)
                nc.scalar.activation(parts[:, pair, 0, :, b, :], psR[:].rearrange("p (c t) -> p c t", c=2 * KD), ACT.Copy).then_inc(part1, 1)

            fetch(0, 0)
            for c in range(TPB):
                body(c, c, 0)
            with act.Fori(1, NT // TPB - 1) as g:
                for c in range(TPB):
                    body(TPB * g + c, c, g)
            for c in range(TPB):
                body(NT - TPB + c, c, NT // TPB - 1, last=(c == TPB - 1))
            second(NT - 1, TPB - 1)

        @block.vector
        def _(dve):
            def rope(t, b, c):
                dve.wait_ge(qk_done, t + 1)
                wait(dve, rotT_done, t - 1)
                heads = psQK[:].rearrange("p (h d) -> p h d", d=HD)
                pairs = psQK[:].rearrange("p (h i a) -> p h i a", i=HD // 2, a=2)
                tp = swapped[:].rearrange("p (h i a) -> p h i a", i=HD // 2, a=2)
                cos = repeat(cst("cos")[:, c * HD:(c + 1) * HD].unsqueeze(1), 1, 2 * HEADS)
                nsin = repeat(cst("nsin")[:, c * HD // 2:(c + 1) * HD // 2].unsqueeze(1), 1, 2 * HEADS)
                sin = repeat(cst("sin")[:, c * HD // 2:(c + 1) * HD // 2].unsqueeze(1), 1, 2 * HEADS)
                dve.tensor_tensor(rot[:, b, :].rearrange("p (h d) -> p h d", d=HD), heads, cos, ALU.mult)
                dve.tensor_tensor(tp[:, :, :, 0], pairs[:, :, :, 1], nsin, ALU.mult)
                dve.tensor_tensor(tp[:, :, :, 1], pairs[:, :, :, 0], sin, ALU.mult).then_inc(rope_read, 1)
                dve.wait_ge(rope_read, t + 1)
                dve.tensor_tensor(rot[:, b, :], rot[:, b, :], swapped[:], ALU.add).then_inc(rot_ready, 1)

            def places(t, b):
                wait(dve, listed, t - 1)
                dve.tensor_tensor(at_place[:, b], repeat(row16[:].unsqueeze(1), 1, TOPK),
                                  repeat(place[:, 1, bass.ds(t, 1), :].rearrange("p t j -> p (t j)").unsqueeze(2), 2, P),
                                  ALU.is_equal).then_inc(place_cmp, 1)
                dve.wait_ge(place_cmp, t + 1)
                flat = at_place[:, b].rearrange("p j a -> p (j a)")
                dve.tensor_tensor(flat, flat, repeat(token16[:, bass.ds(t, 1)], 1, TOPK * P), ALU.mult).then_inc(place_ready, 1)

            def third(t, c):
                b, pair = c % 2, c // 2
                dve.wait_ge(part2, t + 1)
                dve.tensor_tensor(parts[:, pair, 2, :, b, :], rest[:].rearrange("p (c t) -> p c t", c=2 * KD),
                                  parts[:, pair, 1, :, b, :], ALU.subtract).then_inc(part3, 1)

            def body(t, c, g):
                b, pair = c % 2, c // 2
                rope(t, b, c)
                if not (isinstance(t, int) and t == 0):
                    third(t - 1, (c - 1) % TPB)
                places(t, b)
                dve.wait_ge(part1, t + 1)
                dve.tensor_tensor(rest[:].rearrange("p (c t) -> p c t", c=2 * KD), psR[:].rearrange("p (c t) -> p c t", c=2 * KD),
                                  parts[:, pair, 0, :, b, :], ALU.subtract).then_inc(rest_ready, 1)

            tiles(dve, body)
            third(NT - 1, TPB - 1)
            dve.wait_ge(listed, NT)
            dve.tensor_copy(L["slot_token"][:], psList[:, 0:P])


def expert_block(nc, L):
    ident, w_gu, w_dn, tile_expert, slot_token = L["ident"], L["w_gu"], L["w_dn"], L["tile_expert"], L["slot_token"]
    bank = L["bank"]
    psX, psGU, psH, psY = bank[0:2], bank[2:4], bank[4:6], bank[6:8]
    N = SLOT_TILES
    UNROLL = 4
    FIRST = 7
    assert (N - FIRST) % UNROLL == 0 and FIRST % 2 == 1
    with ExitStack() as ctx:
        def sb(name, shape, dt=F32):
            return ctx.enter_context(nc.sbuf_tensor(name, shape, dt))

        def sem(name):
            return ctx.enter_context(nc.semaphore(name))

        xg = sb("xg", [P, 2, D])
        xT = sb("exT", [P, 2, KD, P])
        silu = sb("esilu", [P, 2, M])
        h = sb("eh", [P, 2, M])
        hT = sb("ehT", [MH, 2, 2, P])
        y = sb("ey", [P, 2, D])
        token = sb("token", [P, 2], U32)
        token_ready, waited = sem("token_ready"), sem("ewaited")
        x_in = [sem(f"ex_in{i}") for i in range(2)]
        y_stored = [sem(f"ey_stored{i}") for i in range(2)]
        xt_done, xT_ready, gu_done, silu_ready, h_ready, ht_done, hT_ready, y_done, y_copied = (
            sem(f"e_{s}") for s in ("xt_done", "xT_ready", "gu_done", "silu_ready", "h_ready", "ht_done", "hT_ready",
                                    "y_done", "y_copied"))
        block = ctx.enter_context(nc.Block())

        def steps(eng, step):
            for s in range(FIRST):
                step(s, s % 2, s // 2, s)
            with eng.Fori(0, (N - FIRST) // UNROLL) as i:
                for c in range(FIRST, FIRST + UNROLL):
                    step(UNROLL * i + c, c % 2, UNROLL // 2 * i + c // 2, c)
            for s in range(N, N + 3):
                step(s, s % 2, s // 2, s)

        def inside(j):
            return not isinstance(j, int) or 0 <= j < N

        @block.sync
        def _(sp):
            def store(j, b):
                sp.wait_ge(y_copied, j + 1)
                sp.dma_start(L["slots_y"][bass.ts(j, P), :], y[:, b, :]).then_inc(y_stored[b], 16)

            store(0, 0)
            loads = [(half, pair) for half in range(KD) for pair in operand_loads(L["qk_parts"], L["q_first"], L["k_first"], 0, half)]
            for j, (half, (dst, src)) in enumerate(loads):
                sp.dma_start(dst, src).then_inc(L["qk_in"][0][half], 16)
                store(j + 1, (j + 1) % 2)
            with sp.Fori(len(loads) // 2, N // 2) as i:
                store(2 * i + 1, 1)
                store(2 * i + 2, 0)
            sp.wait_ge(y_stored[0], 16 * ((N + 1) // 2))
            sp.wait_ge(y_stored[1], 16 * (N // 2))

        @block.gpsimd
        def _(pool):
            def load(j, b, use):
                wait(pool, x_in[b], 16 * use)
                pool.sem_inc(waited, 1)
                pool.tensor_copy(token[:, b:b + 1], slot_token[:, bass.ds(j, 1)]).then_inc(token_ready, 1)
                pool.wait_ge(token_ready, j + 1)
                pool.sem_inc(waited, 1)
                wait(pool, xt_done, j - 1)
                pool.sem_inc(waited, 1)
                pool.indirect_dma_start(out=xg[:, b, :], out_offset=None, in_=L["xn_dram"],
                                        in_offset=bass.IndirectOffsetOnAxis(ap=token[:, b:b + 1], axis=0)).then_inc(x_in[b], 16)

            for j in range(3):
                load(j, j % 2, j // 2)
            with pool.Fori(1, N // 2) as i:
                load(2 * i + 1, 1, i)
                load(2 * i + 2, 0, i + 1)

        @block.tensor
        def _(pe):
            def turn_x(j, b, use):
                pe.wait_ge(x_in[b], 16 * use + 16)
                wait(pe, xT_ready, j - 1)
                for k in range(KD):
                    mm = pe.transpose(psX[b][:, k * P:(k + 1) * P], xg[:, b, k::KD], ident)
                mm.then_inc(xt_done, 1)

            def gate_up(j, b, e):
                pe.wait_ge(xT_ready, j + 1)
                wait(pe, h_ready, j - 1)
                for k in range(KD):
                    mm = pe.matmul(psGU[b][:, 0:2 * M].rearrange("p (g m) -> p g m", g=2), xT[:, b, k, :],
                                   w_gu[:, :, bass.ds(e, 1), k, :].rearrange("p g e m -> p g (e m)"),
                                   start=(k == 0), stop=(k == KD - 1))
                mm.then_inc(gu_done, 1)

            def turn_h(j, b):
                pe.wait_ge(h_ready, j + 1)
                wait(pe, hT_ready, j - 1)
                for k in range(2):
                    mm = pe.transpose(psH[b][0:MH, k * P:(k + 1) * P], h[:, b, k::2], ident)
                mm.then_inc(ht_done, 1)

            def down(j, b, e):
                pe.wait_ge(hT_ready, j + 1)
                wait(pe, y_copied, j - 1)
                for k in range(2):
                    mm = pe.matmul(psY[b][:, 0:D], hT[:, b, k, :], w_dn[:, bass.ds(e, 1), k, :].rearrange("p e n -> p (e n)"),
                                   start=(k == 0), stop=(k == 1))
                mm.then_inc(y_done, 1)

            number = [pe.alloc_register(f"expert{k}") for k in range(UNROLL)]

            def expert(c):
                return pe.snap(number[c % UNROLL], min_val=0, max_val=E - 1)

            def step(s, b, use, c):
                if inside(s - 3):
                    turn_h(s - 3, 1 - b)
                if inside(s):
                    turn_x(s, b, use)
                if inside(s - 1):
                    gate_up(s - 1, 1 - b, expert(c - 1))
                if inside(s):
                    pe.reg_load(number[c % UNROLL], tile_expert[0:1, bass.ds(s, 1)])
                if inside(s - 3):
                    down(s - 3, 1 - b, expert(c - 3))

            steps(pe, step)

        @block.scalar
        def _(act):
            nc.scalar.activation(L["k_first"][ROWS:ROWS + 3].rearrange("p h t -> p (h t)"),
                                 repeat(ident[ROWS:ROWS + 3, 0:1], 1, HEADS * SEQ), ACT.Copy, scale=0.0, bias=1.0).then_inc(L["ones_made"], 1)

            def copy_hT(j, b):
                act.wait_ge(ht_done, j + 1)
                wait(act, y_done, j - 1)
                nc.scalar.activation(hT[:, b].rearrange("p k t -> p (k t)"), psH[b][0:MH, 0:2 * P], ACT.Copy).then_inc(hT_ready, 1)

            def gate(j, b):
                act.wait_ge(gu_done, j + 1)
                wait(act, h_ready, j - 1)
                nc.scalar.activation(silu[:, b, :], psGU[b][:, 0:M], ACT.Silu).then_inc(silu_ready, 1)

            def step(s, b, use, c):
                if inside(s - 3):
                    copy_hT(s - 3, 1 - b)
                if inside(s - 1):
                    gate(s - 1, 1 - b)

            steps(act, step)

        @block.vector
        def _(dve):
            def copy_xT(j, b):
                dve.wait_ge(xt_done, j + 1)
                wait(dve, gu_done, j - 1)
                dve.tensor_copy(xT[:, b].rearrange("p k t -> p (k t)"), psX[b][:, 0:D]).then_inc(xT_ready, 1)

            def gated(j, b):
                dve.wait_ge(silu_ready, j + 1)
                wait(dve, ht_done, j - 1)
                dve.tensor_tensor(h[:, b, :], psGU[b][:, M:2 * M], silu[:, b, :], ALU.mult).then_inc(h_ready, 1)

            def copy_y(j, b, use):
                dve.wait_ge(y_done, j + 1)
                wait(dve, y_stored[b], 16 * use)
                dve.tensor_copy(y[:, b, :], psY[b][:, 0:D]).then_inc(y_copied, 1)

            def step(s, b, use, c):
                if inside(s):
                    copy_xT(s, b)
                if inside(s - 1):
                    gated(s - 1, 1 - b)
                if inside(s - 3):
                    copy_y(s - 3, 1 - b, use - 1 if b == 1 else use - 2)

            steps(dve, step)


def attention_block(nc, A, out, L):
    bank, cst, ident, slot, topw = L["bank"], L["cst"], L["ident"], L["slot"], L["topw"]
    G = 4
    NG = BATCH * HEADS // G
    GPB = HEADS // G
    LEAD = 2
    WIDE = [SEQ - P * j for j in range(TPB)]
    AT = [0, SEQ, 2 * SEQ, 2 * SEQ - WIDE[3]]
    PT_N = sum(WIDE)
    BUFS = 2
    qk_in, ones_made = L["qk_in"], L["ones_made"]
    SCALE = 1.0 / np.sqrt(HD)
    bST, bS, bO, bT, bW = bank[0:2], bank[2:5], bank[5], bank[6], bank[7]
    MUNITS = [(3, [h]) for h in range(G)] + [(2, [h]) for h in range(G)] + [(1, [0, 1]), (1, [2, 3]), (0, [0, 1, 2, 3])]
    NM = len(MUNITS)
    SUNITS = []
    for h in (0, 2):
        SUNITS += [[(h, 0, 0)], [(h, 1, 0), (h, 3, WIDE[1])], [(h, 2, 0), (h + 1, 2, WIDE[2])],
                   [(h + 1, 0, 0)], [(h + 1, 1, 0), (h + 1, 3, WIDE[1])]]
    NS = len(SUNITS)
    max_dram = nc.dram_tensor("max_dram", [NG, 3, G, SEQ], BF16, kind="Internal").ap()

    with ExitStack() as ctx:
        def sb(name, shape, dt=F32):
            return ctx.enter_context(nc.sbuf_tensor(name, shape, dt))

        def sem(name):
            return ctx.enter_context(nc.semaphore(name))

        qs = [L["q_first"], sb("q_second", [ROWS + 3, HEADS, SEQ], BF16)]
        ks = [L["k_first"], sb("k_second", [ROWS + 3, HEADS, SEQ], BF16)]
        vraw = sb("vraw", [P, BATCH, TPB, D])
        vpad = sb("vpad", [P, 2, TPB, G, 32])
        pt = sb("pt", [P, 2, G, PT_N])
        oT = sb("oT", [P, 2, SEQ])
        attn = sb("attn", [P, TPB, D])
        aT = sb("aT", [P, TPB, KD, P])
        recip = sb("recip", [P, TPB, G])
        mx = sb("mx", [P, 2, G, TPB])
        negm = sb("negm", [G * TPB, 3, P], BF16)
        mrest = sb("mrest", [G * TPB, P])
        w_o = sb("w_o", [P, KD, D])
        ident16 = sb("ident16", [P, P], BF16)
        future16 = sb("future16", [P, P], BF16)
        futureT16 = sb("futureT16", [P, P], BF16)
        gath = sb("gath", [P, 2, TOPK, D])
        base = sb("base", [P, 2, D])
        acc = sb("acc", [P, 2 * TPB, D])
        idx = sb("cidx", [P, 2, TOPK], U32)

        v_in = [sem(f"v_in{b}") for b in range(BATCH)]
        wo_in, ones_in, masks_ready = sem("wo_in"), sem("ones_in"), sem("masks_ready")
        vpad_zero, vpad_ready = sem("vpad_zero"), sem("vpad_ready")
        s_done, s_read = sem("s_done"), sem("s_read")
        m_turned, m_part1, m_rest, m_part2, m_part3, m_out = (sem(f"m_{s}") for s in ("turned", "part1", "rest", "part2", "part3", "out"))
        m_in = [sem(f"m_in{i}") for i in range(2)]
        st_done, exp_done = sem("st_done"), sem("exp_done")
        pv_done, oT_ready, o_turned, recip_ready, attn_ready = (sem(s) for s in ("pv_done", "oT_ready", "o_turned", "recip_ready", "attn_ready"))
        a_turned, aT_ready, wo_done, added = (sem(s) for s in ("a_turned", "aT_ready", "wo_done", "added"))
        base_in = [sem(f"base_in{b}") for b in range(2)]
        gathered = [sem(f"gathered{b}") for b in range(2)]
        cidx_ready, cwaited = sem("cidx_ready"), sem("cwaited")
        combine, combined, stored = sem("combine"), sem("combined"), sem("stored")
        block = ctx.enter_context(nc.Block())

        def exp_bank(g, n):
            m = n - NS * (NG - LEAD)
            if m < 0:
                return bST[n % 2], n - 1
            return (bST + bS)[m % 5], n - 1 if m < 2 else n - 4 if m >= 5 else 0

        @block.sync
        def _(sp):
            def load_qk(b, half):
                if b >= BUFS:
                    sp.wait_ge(st_done, NS * (GPB * (b - BUFS) + GPB // 2 * (half + 1)))
                for dst, src in operand_loads(L["qk_parts"], qs[b % BUFS], ks[b % BUFS], b, half):
                    sp.dma_start(dst, src).then_inc(qk_in[b][half], 16)

            def load_base(t):
                wait(sp, combined, t - 1)
                sp.dma_start(base[:, t % 2, :], L["shared_y"][t * P:(t + 1) * P, :]).then_inc(base_in[t % 2], 16)

            def max_rows(g):
                sp.wait_ge(m_part3, g + 1)
                sp.dma_start(max_dram[g].rearrange("a h (c t) -> (h c) a t", t=P), negm[:]).then_inc(m_out, 16)
                sp.wait_ge(m_out, 16 * (g + 1))
                h0 = G * (g % GPB)
                sp.dma_start(qs[(g // GPB) % BUFS][ROWS:ROWS + 3, h0:h0 + G], max_dram[g]).then_inc(m_in[g % 2], 16)

            def load_v(b):
                sp.dma_start(vraw[:, b], L["v_dram"][SEQ * b:SEQ * (b + 1), :].rearrange("(j p) n -> p j n", p=P)).then_inc(v_in[b], 16)

            load_base(0)
            load_base(1)
            load_v(0)
            sp.wait_ge(ones_made, 1)
            sp.dma_start(ks[1][ROWS:ROWS + 3], ks[0][ROWS:ROWS + 3]).then_inc(ones_in, 16)
            for g in range(LEAD):
                max_rows(g)
                load_qk(1, g)
            sp.dma_start(w_o[:], A["woT"].rearrange("(p k) n -> p k n", k=KD)).then_inc(wo_in, 16)
            for k in range(2, NT):
                load_base(k)
                if k % GPB == 2 and k // GPB + 1 < BATCH:
                    load_v(k // GPB + 1)
                if k - 2 + LEAD < NG:
                    max_rows(k - 2 + LEAD)
                if k % GPB == 3 and (k + 5) // GPB < BATCH:
                    load_qk((k + 5) // GPB, 0)
                if k % GPB == 1 and k > GPB and (k + 3) // GPB < BATCH:
                    load_qk((k + 3) // GPB, 1)
            sp.wait_ge(stored, 16 * BATCH)

        @block.gpsimd
        def _(pool):
            pool.memset(vpad[:], 0.0).then_inc(vpad_zero, 1)
            pool.wait_ge(vpad_zero, 1)
            pool.memset(vpad[:, :, :, :, HD:HD + 1], 1.0).then_inc(vpad_zero, 1)
            pool.wait_ge(vpad_zero, 2)

            def group(s, r, first=False):
                t, b = GPB * s + r, r % 2
                wait(pool, combined, t - 1)
                pool.sem_inc(cwaited, 1)
                pool.tensor_copy(idx[:, b, :], slot[:, bass.ds(t, 1), :].rearrange("p a j -> p (a j)")).then_inc(cidx_ready, 1)
                pool.wait_ge(cidx_ready, t + 1)
                pool.sem_inc(cwaited, 1)
                for j in range(TOPK):
                    pool.indirect_dma_start(out=gath[:, b, j, :], out_offset=None, in_=L["slots_y"],
                                            in_offset=bass.IndirectOffsetOnAxis(ap=idx[:, b, j:j + 1], axis=0)).then_inc(gathered[b], 16)
                if r == 0:
                    pool.wait_ge(v_in[s], 16)
                wait(pool, pv_done, t - 1)
                pool.sem_inc(cwaited, 1)
                pool.tensor_copy(vpad[:, b, :, :, 0:HD],
                                 vraw[:, s, :, G * HD * r:G * HD * (r + 1)].rearrange("p j (h d) -> p j h d", d=HD)).then_inc(vpad_ready, 1)

            for s in range(BATCH):
                for r in range(GPB):
                    group(s, r)

        @block.tensor
        def _(pe):
            pe.wait_ge(masks_ready, 3)

            def max_unit(g, u):
                b, n = g // GPB, NM * g + u
                c, heads = MUNITS[u]
                if u == 0 and g % 2 == 0:
                    pe.wait_ge(qk_in[b][g % GPB // 2], 16 * 2 * len(QPART))
                wait(pe, s_read, n - 2)
                bk, w = bS[n % 3], P * (c + 1)
                for i, h in enumerate(heads):
                    hh = G * (g % GPB) + h
                    pe.matmul(bk[:, i * w:(i + 1) * w], qs[b % BUFS][0:ROWS, hh, c * P:(c + 1) * P],
                              ks[b % BUFS][0:ROWS, hh, 0:w], start=True, stop=True)
                    mm = pe.matmul(bk[:, i * w + c * P:(i + 1) * w], ident16[:], future16[:], start=False, stop=True,
                                   skip_group_check=True)
                mm.then_inc(s_done, 1)

            def exp_unit(g, u):
                b, n = g // GPB, NS * g + u
                if u == 0:
                    pe.wait_ge(m_in[g % 2], 16 * (g // 2 + 1))
                    if g == 0:
                        pe.wait_ge(ones_made, 1)
                    if g == GPB:
                        pe.wait_ge(ones_in, 16)
                bk, used = exp_bank(g, n)
                wait(pe, exp_done, used)
                if g == NG - LEAD and 2 <= u < 5:
                    pe.wait_ge(s_read, NM * NG)
                for h, j, col in SUNITS[u]:
                    hh = G * (g % GPB) + h
                    pe.matmul(bk[:, col:col + WIDE[j]], ks[b % BUFS][:, hh, j * P:(j + 1) * P],
                              qs[b % BUFS][:, hh, j * P:SEQ], start=True, stop=True)
                    mm = pe.matmul(bk[:, col:col + P], ident16[:], futureT16[:], start=False, stop=True, skip_group_check=True)
                mm.then_inc(st_done, 1)

            def pv(g, j):
                if j == 0:
                    pe.wait_ge(exp_done, NS * (g + 1))
                    pe.wait_ge(vpad_ready, g + 1)
                    wait(pe, oT_ready, g)
                for h in range(G):
                    mm = pe.matmul(bO[32 * h:32 * h + 32, j * P:SEQ], vpad[:, g % 2, j, h, :],
                                   pt[:, g % 2, h, AT[j]:AT[j] + WIDE[j]], start=(j == 0), stop=True,
                                   skip_group_check=True)
                if j == TPB - 1:
                    mm.then_inc(pv_done, 1)

            def turn_o(g):
                pe.wait_ge(oT_ready, g + 1)
                wait(pe, attn_ready, g)
                for c in range(TPB):
                    mm = pe.transpose(bT[:, c * P:(c + 1) * P], oT[:, g % 2, c * P:(c + 1) * P], ident)
                mm.then_inc(o_turned, 1)

            def turn_max(g, halves):
                pe.wait_ge(s_read, NM * (g + 1))
                wait(pe, added, halves)
                wait(pe, m_rest, g)
                pe.transpose(bW[0:G * TPB, 0:P], mx[:, g % 2].rearrange("p h c -> p (h c)"), ident).then_inc(m_turned, 1)

            def turn_attn(b, half, maxima):
                pe.wait_ge(attn_ready, GPB * (b + 1))
                pe.wait_ge(m_rest, maxima)
                wait(pe, added, 2 * b)
                if half:
                    pe.wait_ge(aT_ready, 2 * b + 1)
                for c in range(2):
                    for k in range(KD):
                        mm = pe.transpose(bW[:, (2 * c + k) * P:(2 * c + k + 1) * P], attn[:, 2 * half + c, k::KD], ident)
                mm.then_inc(a_turned, 1)

            def project(b, c):
                pe.wait_ge(aT_ready, 2 * b + 2)
                if b == 0 and c == 0:
                    pe.wait_ge(wo_in, 16)
                if c == 2:
                    pe.wait_ge(added, 2 * b + 1)
                for k in range(KD):
                    mm = pe.matmul(bW[:, (c % 2) * D:(c % 2 + 1) * D], aT[:, c, k, :], w_o[:, k, :],
                                   start=(k == 0), stop=(k == KD - 1))
                if c % 2 == 1:
                    mm.then_inc(wo_done, 1)

            for g in range(LEAD):
                for u in range(NM):
                    max_unit(g, u)
                if g < LEAD - 1:
                    turn_max(g, 0)
            for g in range(NG + 3):
                b, r = g // GPB, g % GPB
                for u in range(NM):
                    if g + LEAD < NG:
                        max_unit(g + LEAD, u)
                    if g < NG and u < NS:
                        exp_unit(g, u)
                    attn_step = b >= 1 and r == 1
                    if u < 2 and r == 2 and b >= 1:
                        project(b - 1, 2 + u)
                    if u == 3 and g - 1 + LEAD < NG:
                        turn_max(g - 1 + LEAD, 2 * b if r >= 2 else 2 * (b - 1))
                    if 4 <= u < 4 + TPB and 1 <= g <= NG:
                        pv(g - 1, u - 4)
                    if attn_step and u in (5, 7):
                        turn_attn(b - 1, (u - 5) // 2, min(g + LEAD, NG))
                    if u == 10 and 1 <= g <= NG:
                        turn_o(g - 1)
                    if attn_step and u >= 9:
                        project(b - 1, u - 9)

        @block.scalar
        def _(act):
            nc.scalar.activation(ident16[:], ident, ACT.Copy).then_inc(masks_ready, 1)
            nc.scalar.activation(future16[:], cst("future"), ACT.Copy).then_inc(masks_ready, 1)
            nc.scalar.activation(futureT16[:], cst("futureT"), ACT.Copy).then_inc(masks_ready, 1)

            def exp_unit(g, u):
                n = NS * g + u
                act.wait_ge(st_done, n + 1)
                if u == 0:
                    wait(act, pv_done, g - 1)
                bk, _ = exp_bank(g, n)
                pieces = SUNITS[u]
                if len(pieces) == 1 or pieces[0][0] == pieces[1][0]:
                    h, j, _ = pieces[0]
                    nc.scalar.activation(pt[:, g % 2, h, AT[j]:AT[j] + SEQ], bk[:], ACT.Exp, scale=float(SCALE)).then_inc(exp_done, 1)
                else:
                    h, j, _ = pieces[0]
                    nc.scalar.activation(pt[:, g % 2, h:h + 2, AT[j]:AT[j] + WIDE[j]], bk[:].rearrange("p (h q) -> p h q", h=2),
                                         ACT.Exp, scale=float(SCALE)).then_inc(exp_done, 1)

            def copy_o(g):
                act.wait_ge(pv_done, g + 1)
                wait(act, o_turned, g - 1)
                nc.scalar.activation(oT[:, g % 2, :], bO[:], ACT.Copy).then_inc(oT_ready, 1)

            def part1(g):
                act.wait_ge(m_turned, g + 1)
                wait(act, m_out, 16 * g)
                nc.scalar.activation(negm[:, 0, :], bW[0:G * TPB, 0:P], ACT.Copy, scale=-1.0).then_inc(m_part1, 1)

            def copy_attn(b, half):
                act.wait_ge(a_turned, 2 * b + half + 1)
                wait(act, wo_done, 2 * b)
                nc.scalar.activation(aT[:, 2 * half:2 * half + 2].rearrange("p c k t -> p (c k t)"), bW[:], ACT.Copy).then_inc(aT_ready, 1)

            for g in range(LEAD - 1):
                part1(g)
            for g in range(NG + 3):
                b, r = g // GPB, g % GPB
                for u in range(NS):
                    if g < NG:
                        exp_unit(g, u)
                    if u == 3 and g - 1 + LEAD < NG:
                        part1(g - 1 + LEAD)
                    if u in (6, 8) and r == 1 and b >= 1:
                        copy_attn(b - 1, (u - 6) // 2)
                    if u == 8 and 1 <= g <= NG:
                        copy_o(g - 1)
                if r == 2 and b >= 1:
                    act.wait_ge(added, 2 * b)
                    act.dma_start(out[SEQ * (b - 1):SEQ * b, :].rearrange("(c p) n -> p c n", p=P),
                                  acc[:, TPB * ((b - 1) % 2):TPB * ((b - 1) % 2 + 1), :]).then_inc(stored, 16)

        @block.vector
        def _(dve):
            n_combine = [0]

            def max_unit(g, u):
                b, n = g // GPB, NM * g + u
                c, heads = MUNITS[u]
                w, h0 = P * (c + 1), heads[0]
                dve.wait_ge(s_done, n + 1)
                if u == 0:
                    wait(dve, m_turned, g - 1)
                dve.tensor_reduce(mx[:, g % 2, h0:h0 + len(heads), c], bS[n % 3][:, 0:w * len(heads)].rearrange("p (h k) -> p h k", k=w),
                                  AX.X, ALU.max).then_inc(s_read, 1)

            def split_max(g):
                dve.wait_ge(m_part1, g + 1)
                dve.scalar_tensor_tensor(out=mrest[:], in0=bW[0:G * TPB, 0:P], scalar=-1.0, in1=negm[:, 0, :],
                                         op0=ALU.mult, op1=ALU.subtract).then_inc(m_rest, 1)
                dve.wait_ge(m_rest, g + 1)
                dve.tensor_copy(negm[:, 1, :], mrest[:]).then_inc(m_part2, 1)
                dve.wait_ge(m_part2, g + 1)
                dve.tensor_tensor(negm[:, 2, :], mrest[:], negm[:, 1, :], ALU.subtract).then_inc(m_part3, 1)

            def add_experts(t, j):
                a = acc[:, t % (2 * TPB), :]
                if j == 0:
                    dve.wait_ge(base_in[t % 2], 16 * (t // 2 + 1))
                    dve.wait_ge(gathered[t % 2], 16 * TOPK * (t // 2 + 1))
                    if t % TPB == 0 and t >= 2 * TPB:
                        dve.wait_ge(stored, 16 * (t // TPB - 1))
                else:
                    dve.wait_ge(combine, n_combine[0])
                ins = dve.scalar_tensor_tensor(out=a, in0=gath[:, t % 2, j, :], scalar=topw[:, t, j:j + 1],
                                               in1=base[:, t % 2, :] if j == 0 else a, op0=ALU.mult, op1=ALU.add)
                if j == TOPK - 1:
                    ins.then_inc(combined, 1)
                else:
                    n_combine[0] += 1
                    ins.then_inc(combine, 1)

            def normalise(g):
                dve.wait_ge(o_turned, g + 1)
                if g % GPB == 0:
                    wait(dve, a_turned, 2 * (g // GPB))
                o = bT[:].rearrange("p (c h x) -> p c h x", c=TPB, h=G)
                dve.reciprocal(recip[:], o[:, :, :, HD]).then_inc(recip_ready, 1)
                dve.wait_ge(recip_ready, g + 1)
                dst = attn[:, :, G * HD * (g % GPB):G * HD * (g % GPB + 1)].rearrange("p c (h d) -> p c h d", h=G)
                dve.tensor_tensor(dst, o[:, :, :, 0:HD], repeat(recip[:].unsqueeze(3), 3, HD), ALU.mult).then_inc(attn_ready, 1)

            def add_attention(b, half):
                dve.wait_ge(wo_done, 2 * b + half + 1)
                dve.wait_ge(combined, TPB * (b + 1))
                a = acc[:, TPB * (b % 2) + 2 * half:TPB * (b % 2) + 2 * half + 2, :].rearrange("p c n -> p (c n)")
                dve.tensor_tensor(a, bW[:], a, ALU.add).then_inc(added, 1)

            for g in range(LEAD):
                for u in range(NM):
                    max_unit(g, u)
                if g < LEAD - 1:
                    split_max(g)
            for g in range(NG + 3):
                b, r = g // GPB, g % GPB
                for u in range(NM):
                    if g + LEAD < NG:
                        max_unit(g + LEAD, u)
                    if g < NT and 1 <= u <= TOPK:
                        add_experts(g, u - 1)
                    if u == 2 and r == 2 and b >= 1:
                        add_attention(b - 1, 1)
                    if u == 4 and g - 1 + LEAD < NG:
                        split_max(g - 1 + LEAD)
                    if u == 0 and 2 <= g <= NG + 1:
                        normalise(g - 2)
                    if u == 10 and r == 1 and b >= 1:
                        add_attention(b - 1, 0)


INPUTS = {"x": "L0_attn_x", "wqT": "L0_attn_Wq", "wkT": "L0_attn_Wk", "wvT": "L0_attn_Wv", "woT": "L0_attn_Wo",
          "w_router": "L0_ffn_w_router", "bias": "L0_ffn_corr_bias", "gate_w": "L0_ffn_gate_w", "up_w": "L0_ffn_up_w",
          "down_w": "L0_ffn_down_w", "sh_gate": "L0_ffn_sh_gate_w", "sh_up": "L0_ffn_sh_up_w", "sh_down": "L0_ffn_sh_down_w"}


def host_arrays(inputs):
    arrays = {}
    for short, name in INPUTS.items():
        a = np.asarray(inputs[name])
        if short == "x":
            a = a.reshape(T, D)
        arrays[short] = np.ascontiguousarray(a.T if short.endswith("T") else a)
    arrays["const"] = constants()
    return arrays


def kernel(**inputs):
    from concourse import bacc
    from concourse.bass_utils import run_bass_kernel_spmd

    nc = bacc.Bacc("TRN2", target_bir_lowering=False, num_devices=1)
    arrays = host_arrays(inputs)
    A = {n: nc.dram_tensor(f"in_{n}_dram", a.shape, mybir.dt.from_np(a.dtype), kind="ExternalInput").ap()
         for n, a in arrays.items()}
    out = nc.dram_tensor("out_dram", [T, D], F32, kind="ExternalOutput").ap()
    ffn_attention_program(nc, A, out)
    r = run_bass_kernel_spmd(nc, [{f"in_{n}_dram": a for n, a in arrays.items()}], core_ids=[0])
    return r.results[0]["out_dram"].reshape(BATCH, SEQ, D)
```

```python
from contextlib import ExitStack

import numpy as np

import concourse.bass as bass
from concourse import mybir

ALU = mybir.AluOpType
ACT = mybir.ActivationFunctionType
AX = mybir.AxisListType
F32 = mybir.dt.float32
F16 = mybir.dt.float16
BF16 = mybir.dt.bfloat16
I32 = mybir.dt.int32
U32 = mybir.dt.uint32

P = 128
BATCH, SEQ, D = 4, 512, 256
T = BATCH * SEQ
NT = T // P
TPB = SEQ // P
KD = D // P
HEADS, HD = 16, 16
E, M, TOPK = 32, 176, 6
GROUPS, TOPG = 8, 4
PER = E // GROUPS
MS = 2 * M
SHARED = [(m, min(P, MS - m)) for m in range(0, MS, P)]
HC = len(SHARED)
MH = M // 2
SLOT_TILES = (T * TOPK + E * (P - 1)) // P
QPART, KPART = (0, 0, 1, 0, 1, 2), (0, 1, 0, 2, 1, 0)
ROWS = len(QPART) * HD
HT_AT = 14
assert (E - HT_AT) * KD * M >= NT * HC * P and all((2 * t + 2 - HT_AT) * KD * M <= (t + 1) * HC * P for t in range(NT - 1))
G = 4
GPB = HEADS // G
NG = BATCH * GPB
assert NG == NT
EPS = 1e-5
NEG = -3.0e38

CONST_COLS = [("ident", P), ("before", P), ("row", P), ("expert", E), ("tile", 1), ("steps", NT),
              ("lower", GROUPS * GROUPS), ("cos", TPB * HD), ("nsin", TPB * HD // 2), ("sin", TPB * HD // 2),
              ("future", P), ("futureT", P)]
CONST_AT = {}
_at = 0
for _name, _n in CONST_COLS:
    CONST_AT[_name] = (_at, _at + _n)
    _at += _n
CONST_N = _at


def constants():
    c = np.zeros((P, CONST_N), np.float32)

    def put(name, a):
        lo, hi = CONST_AT[name]
        c[:, lo:hi] = np.asarray(a, np.float32).reshape(P, hi - lo)

    r = np.arange(P)
    put("ident", np.eye(P))
    put("before", r[:, None] < r[None, :])
    put("row", np.broadcast_to(r, (P, P)))
    put("expert", np.broadcast_to(np.arange(E), (P, E)))
    put("tile", r)
    put("steps", np.broadcast_to(np.arange(NT) * P, (P, NT)))
    g = np.arange(GROUPS)
    put("lower", np.broadcast_to((g[None, :] < g[:, None]).reshape(1, -1), (P, GROUPS * GROUPS)))
    inv = (1.0 / np.float32(10000.0) ** (np.arange(0, HD, 2, dtype=np.float32) / np.float32(HD))).astype(np.float32)
    pos = (np.arange(TPB)[None, :] * P + r[:, None]).astype(np.float32)
    ang = (pos[:, :, None] * inv).astype(np.float32)
    put("cos", np.repeat(np.cos(ang), 2, axis=-1))
    put("nsin", -np.sin(ang))
    put("sin", np.sin(ang))
    put("futureT", np.where(r[:, None] > r[None, :], -1.0e30, 0.0))
    put("future", np.where(r[None, :] > r[:, None], -1.0e30, 0.0))
    return c


def repeat(ap, axis, n):
    shape = list(ap.shape)
    assert shape[axis] == 1
    shape[axis] = n
    return ap.broadcast_to(shape)


def constant(shared, name):
    lo, hi = CONST_AT[name]
    return shared.const[:, lo:hi]


class Shared:
    pass


class Carver:

    def __init__(self, tensor):
        self.tensor, self.at = tensor, 0

    def __call__(self, shape, dt=F32):
        n = int(np.prod(shape[1:]))
        words = n if dt in (F32, U32) else n // 2
        piece = self.tensor[0:shape[0], self.at:self.at + words]
        self.at += words
        assert self.at <= self.tensor.shape[1]
        if dt != F32:
            piece = piece.bitcast(dt)
        if len(shape) == 2:
            return piece
        names = [f"d{i}" for i in range(len(shape) - 1)]
        return piece.rearrange(f"p ({' '.join(names)}) -> p {' '.join(names)}", **dict(zip(names, shape[1:])))


def operand_loads(qk_parts, q, k, b, half):
    for i, (qpart, kpart) in enumerate(zip(QPART, KPART)):
        rows = slice(HD * i, HD * (i + 1))
        for dst, part, chunk in ((q, qpart, half), (k, kpart, KD + half)):
            yield (dst[rows, HEADS // KD * half:HEADS // KD * (half + 1)],
                   qk_parts[part, chunk, :, SEQ * b:SEQ * (b + 1)].rearrange("(h d) t -> d h t", d=HD))


def is_first(t):
    return isinstance(t, int) and t == 0


def wait(eng, sem, n):
    if isinstance(n, int) and n <= 0:
        return
    eng.wait_ge(sem, n)


def ffn_attention_program(nc, A, out):
    def dram(name, shape, dt=F32):
        return nc.dram_tensor(name, shape, dt, kind="Internal").ap()

    shared = Shared()
    shared.A, shared.out = A, out
    shared.xn_dram = dram("xn_dram", [T, D])
    shared.slots_y = dram("slots_y_dram", [SLOT_TILES * P, D])
    shared.shared_y = dram("shared_y_dram", [T, D])
    shared.qk_parts = dram("qk_parts_dram", [3, 2 * KD, P, T], BF16)
    shared.v_dram = dram("v_dram", [T, D])
    shared.max_dram = dram("max_dram", [NG, 3, G, SEQ], BF16)

    def sb(ctx, name, shape, dt=F32):
        return ctx.enter_context(nc.sbuf_tensor(name, shape, dt))

    def sem(ctx, name):
        return ctx.enter_context(nc.semaphore(name))

    with ExitStack() as whole:
        shared.bank = [whole.enter_context(nc.psum_tensor(f"bank{i}", [P, 512], F32)) for i in range(8)]
        shared.const = sb(whole, "const", [P, CONST_N])
        shared.ident = constant(shared, "ident")
        shared.topw = sb(whole, "topw", [P, NT, TOPK])
        shared.slot = sb(whole, "slot", [P, NT, TOPK], U32)
        shared.front = sb(whole, "front", [P, HEADS * SEQ])
        first_qk = Carver(shared.front)
        shared.q_first = first_qk([P, HEADS, SEQ], BF16)[0:ROWS + 3]
        shared.k_first = first_qk([P, HEADS, SEQ], BF16)[0:ROWS + 3]
        shared.qk_in = [[sem(whole, f"qk_in{b}_{half}") for half in range(KD)] for b in range(BATCH)]
        shared.ones_made = sem(whole, "ones_made")

        with ExitStack() as ffn:
            shared.w_gu = sb(ffn, "w_gu", [P, 2, E, KD, M])
            shared.w_dn = sb(ffn, "w_dn", [MH, E, 2, D])
            shared.tile_expert = sb(ffn, "tile_expert", [1, P], I32)
            shared.slot_token = sb(ffn, "slot_token", [P, P], U32)
            shared.place = sb(ffn, "place", [P, 2, NT, TOPK], F16)
            shared.token = sb(ffn, "token_number", [P, NT])
            shared.row16 = sb(ffn, "row16", [P, P], F16)
            shared.xT_all = shared.w_gu[:, 0, E - NT:E].rearrange("p e k m -> p e (k m)")
            shared.hT_all = shared.w_gu[:, 1, HT_AT:E].rearrange("p e k m -> p (e k m)")[:, 0:NT * HC * P].rearrange(
                "p (t c n) -> p t c n", t=NT, c=HC)
            shared.dense_in, shared.shared_in = sem(ffn, "dense_in"), sem(ffn, "shared_in")
            shared.weights_in, shared.down_in = sem(ffn, "weights_in"), sem(ffn, "down_in")
            with ExitStack() as dense:
                shared.ws_gu = sb(dense, "ws_gu", [P, 2, KD, MS])
                shared.ws_dn = sb(dense, "ws_dn", [P, HC, D])
                shared.w_qkv = sb(dense, "w_qkv", [P, KD, 3, D])
                route_block(nc, shared)
                dense_block(nc, shared)
            expert_block(nc, shared)
        attention_block(nc, shared)


def route_block(nc, shared):
    A, bank, ident, topw, slot = shared.A, shared.bank, shared.ident, shared.topw, shared.slot
    w_gu, w_dn, ws_gu, ws_dn, w_qkv = shared.w_gu, shared.w_dn, shared.ws_gu, shared.ws_dn, shared.w_qkv
    PAIRS = NT // 2
    LOADS = 4
    UNITS = [(g, c, rows) for g in range(NT // TPB) for c, (_, rows) in enumerate(SHARED)]
    COUNT_AFTER, OWN_AFTER = 6, 9
    with ExitStack() as ctx:
        def sb(name, shape, dt=F32):
            return ctx.enter_context(nc.sbuf_tensor(name, shape, dt))

        def sem(name):
            return ctx.enter_context(nc.semaphore(name))

        front = Carver(shared.front)
        x = front([P, NT, D])
        w_router = sb("w_router", [P, KD, E])
        bias = sb("bias", [P, E])
        stats = sb("stats", [P, NT, 6])
        mv = sb("mv", [P, NT, 2])
        var = sb("var", [P, NT])
        std = sb("std", [P, NT])
        gated = front([P, 2, TPB * P])
        rstd = sb("rstd", [P, NT])
        xT_all, hT_all = shared.xT_all, shared.hT_all
        scores = front([P, NT, E])
        sfc = front([P, NT, E])
        spare = w_gu[:, 1, 0:NT].rearrange("p e k m -> p (e k m)")
        tmpa = spare[:, 0:NT * GROUPS * GROUPS]
        tmpb = spare[:, NT * GROUPS * GROUPS:2 * NT * GROUPS * GROUPS]
        wide = w_gu[:, 0, 0:NT].rearrange("p e k m -> p (e k m)")[:, 0:TOPK * NT * E].rearrange("p (j t e) -> p j t e", j=TOPK, t=NT)
        gs = front([P, NT, GROUPS])
        keep = front([P, NT, GROUPS])
        pen = front([P, NT, GROUPS])
        top8 = front([P, NT, 8])
        top8i = front([P, NT, 8], U32)
        topf = front([P, NT, 8])
        flat = x[:].rearrange("p t n -> p (t n)")
        onehot = flat[:, 0:TOPK * NT * E // 2].bitcast(BF16).rearrange("p (j t e) -> p j t e", j=TOPK, t=NT)
        earlier = flat[:, TOPK * NT * E // 2:TOPK * NT * E // 2 + NT * E].rearrange("p (t e) -> p t e", e=E)
        chosen = front([P, NT, E], BF16)
        before16 = sb("before16", [P, P], BF16)
        ones16 = sb("ones16", [P, P], BF16)
        ntile = sb("ntile", [P, 6, E])
        slotf = front([P, NT, TOPK])
        own = sb("own", [P, 1])
        digits = front([P, 2, NT, TOPK], U32)

        x_in = [sem(f"x_in{i}") for i in range(LOADS)]
        small_in = sem("small_in")
        g_done, u_done, silu_ready, u_copied = (sem(s) for s in ("g_done", "u_done", "silu_ready", "u_copied"))
        rest_zero, h_ready, xn_stored = sem("rest_zero"), sem("h_ready"), sem("xn_stored")
        var_ready = sem("var_ready")
        std_ready = sem("std_ready")
        xn_ready = sem("xn_ready")
        turned = sem("turned")
        xT_ready = sem("xT_ready")
        logits_done = sem("logits_done")
        sig_done = sem("sig_done")
        step = sem("route_step")
        chosen_ready = sem("chosen_ready")
        counted = sem("counted")
        own_ready = sem("own_ready")
        own_turned = sem("own_turned")
        block = ctx.enter_context(nc.Block())

        @block.sync
        def _(sp):
            xv = A["x"].rearrange("(t p) n -> p t n", p=P)
            for i in range(LOADS):
                own_tiles = slice(i * NT // LOADS, (i + 1) * NT // LOADS)
                sp.dma_start(x[:, own_tiles, :], xv[:, own_tiles, :]).then_inc(x_in[i], 16)
                if i == 0:
                    sp.dma_start(shared.const[:], A["const"]).then_inc(small_in, 16)
                    sp.dma_start(w_router[:], A["w_router"].rearrange("(p k) e -> p k e", k=KD)).then_inc(small_in, 16)
                    sp.dma_start(bias[:], repeat(A["bias"].rearrange("(a e) -> a e", a=1), 0, P)).then_inc(small_in, 16)
            sp.dma_start(ws_gu[:, 0], A["sh_gate"].rearrange("(p k) n -> p k n", k=KD)).then_inc(shared.shared_in, 16)
            sp.dma_start(ws_gu[:, 1], A["sh_up"].rearrange("(p k) n -> p k n", k=KD)).then_inc(shared.shared_in, 16)
            sp.dma_start(w_qkv[:, :, 0, :], A["wqT"].rearrange("(p k) n -> p k n", k=KD)).then_inc(shared.dense_in, 16)
            sp.dma_start(w_qkv[:, :, 1, :], A["wkT"].rearrange("(p k) n -> p k n", k=KD)).then_inc(shared.dense_in, 16)
            sp.dma_start(w_qkv[:, :, 2, :], A["wvT"].rearrange("(p k) n -> p k n", k=KD)).then_inc(shared.dense_in, 16)
            for c, (m, rows) in enumerate(SHARED):
                sp.dma_start(ws_dn[0:rows, c, :], A["sh_down"][m:m + rows, :]).then_inc(shared.dense_in, 16)
            sp.wait_ge(xn_ready, NT)
            sp.dma_start(shared.xn_dram.rearrange("(t p) n -> p t n", p=P), x[:]).then_inc(xn_stored, 16)
            sp.wait_ge(xn_stored, 16)
            for e in range(0, E, 8):
                sp.dma_start(w_dn[:, e:e + 8], A["down_w"][e:e + 8].rearrange("e (p k) n -> p e k n", k=2)).then_inc(shared.down_in, 16)
            sp.wait_ge(shared.dense_in, 16 * (3 + HC))

        @block.gpsimd
        def _(pool):
            pool.memset(hT_all[SHARED[-1][1]:P, :, HC - 1, :], 0.0).then_inc(rest_zero, 1)
            pool.wait_ge(rest_zero, 1)
            for u, (g, c, rows) in enumerate(UNITS):
                pool.wait_ge(silu_ready, u + 1)
                pool.wait_ge(u_copied, u + 1)
                h = hT_all[0:rows, TPB * g:TPB * (g + 1), c, :]
                pool.tensor_tensor(h, h, gated[0:rows, u % 2, :].rearrange("p (t n) -> p t n", n=P), ALU.mult).then_inc(h_ready, 1)

        @block.scalar
        def _(act):
            def root(q):
                act.wait_ge(var_ready, q + 1)
                own_tiles = slice(q * NT // LOADS, (q + 1) * NT // LOADS)
                nc.scalar.activation(std[:, own_tiles], var[:, own_tiles], ACT.Sqrt).then_inc(std_ready, 1)

            root(0)
            for j in range(PAIRS):
                if j % (PAIRS // LOADS) == 1 and j // (PAIRS // LOADS) + 1 < LOADS:
                    root(j // (PAIRS // LOADS) + 1)
                act.wait_ge(turned, j + 1)
                nc.scalar.activation(xT_all[:, 2 * j:2 * j + 2, 0:D], bank[j % 2][:].rearrange("p (a b) -> p a b", a=2),
                                     ACT.Copy).then_inc(xT_ready, 1)
            act.wait_ge(logits_done, PAIRS)
            nc.scalar.activation(scores[:], bank[2][:].rearrange("p (t e) -> p t e", e=E), ACT.Sigmoid).then_inc(sig_done, 1)
            for u, (g, c, rows) in enumerate(UNITS):
                act.wait_ge(g_done, u + 1)
                wait(act, h_ready, u - 1)
                nc.scalar.activation(gated[0:rows, u % 2, :], bank[6][0:rows, :], ACT.Silu).then_inc(silu_ready, 1)
                act.wait_ge(u_done, u + 1)
                nc.scalar.activation(hT_all[0:rows, TPB * g:TPB * (g + 1), c, :], bank[7][0:rows, :].rearrange("p (t n) -> p t n", n=P),
                                     ACT.Copy).then_inc(u_copied, 1)

        @block.tensor
        def _(pe):
            pe.wait_ge(small_in, 48)

            def logits(j):
                pe.wait_ge(xT_ready, j + 1)
                for t in range(2 * j, 2 * j + 2):
                    for k in range(KD):
                        mm = pe.matmul(bank[2][:, t * E:(t + 1) * E], xT_all[:, t, k * P:(k + 1) * P],
                                       w_router[:, k, :], start=(k == 0), stop=(k == KD - 1))
                mm.then_inc(logits_done, 1)

            def shared_hidden(u):
                g, c, rows = UNITS[u]
                if u == 0:
                    pe.wait_ge(shared.shared_in, 32)
                for i, (ps, used, done) in enumerate(((bank[6], silu_ready, g_done), (bank[7], u_copied, u_done))):
                    wait(pe, used, u)
                    for k in range(KD):
                        mm = pe.matmul(ps[0:rows, :].rearrange("p (t n) -> p t n", n=P), ws_gu[:, i, k, P * c:P * c + rows],
                                       xT_all[:, TPB * g:TPB * (g + 1), k * P:(k + 1) * P], start=(k == 0), stop=(k == KD - 1))
                    mm.then_inc(done, 1)

            def count():
                pe.wait_ge(chosen_ready, 1)
                pe.matmul(bank[3][:], before16[:], chosen[:].rearrange("p t e -> p (t e)"), start=True, stop=True)
                for t in range(NT - 1):
                    pe.matmul(bank[3][:, (t + 1) * E:NT * E].rearrange("p (t e) -> p t e", e=E), ones16[:],
                              repeat(chosen[:, t:t + 1, :], 1, NT - 1 - t), start=False, stop=True, skip_group_check=True)
                for t in range(NT):
                    mm = pe.matmul(bank[4][:, 0:E], ones16[:], chosen[:, t, :], start=(t == 0), stop=(t == NT - 1))
                mm.then_inc(counted, 1)

            for j in range(PAIRS):
                pe.wait_ge(xn_ready, 2 * j + 2)
                if j >= 2:
                    pe.wait_ge(xT_ready, j - 1)
                for i in range(2):
                    for k in range(KD):
                        mm = pe.transpose(bank[j % 2][:, (2 * i + k) * P:(2 * i + k + 1) * P],
                                          x[:, 2 * j + i, k::KD], ident)
                mm.then_inc(turned, 1)
                if j >= 1:
                    logits(j - 1)
            logits(PAIRS - 1)
            for u in range(len(UNITS)):
                shared_hidden(u)
                if u == COUNT_AFTER:
                    count()
                if u == OWN_AFTER:
                    pe.wait_ge(own_ready, 1)
                    pe.transpose(bank[5][0:1, 0:P], own[:], ident).then_inc(own_turned, 1)

        @block.vector
        def _(dve):
            n = [0]

            def link(ins):
                n[0] += 1
                ins.then_inc(step, 1)
                dve.wait_ge(step, n[0])

            for q in range(LOADS):
                tiles = range(q * NT // LOADS, (q + 1) * NT // LOADS)
                own_tiles = slice(tiles[0], tiles[-1] + 1)
                dve.wait_ge(x_in[q], 16)
                for t in tiles:
                    ins = dve.bn_stats(stats[:, t, :], x[:, t, :])
                link(ins)
                for t in tiles:
                    ins = dve.bn_aggr(mv[:, t, :], stats[:, t, :])
                link(ins)
                dve.tensor_scalar(var[:, own_tiles], mv[:, own_tiles, 1], EPS, None, ALU.add).then_inc(var_ready, 1)
                dve.wait_ge(std_ready, q + 1)
                link(dve.reciprocal(rstd[:, own_tiles], std[:, own_tiles]))
                for t in tiles:
                    dve.tensor_scalar(x[:, t, :], x[:, t, :], mv[:, t, 0:1], rstd[:, t:t + 1],
                                      ALU.subtract, ALU.mult).then_inc(xn_ready, 1)
            dve.wait_ge(small_in, 48)
            dve.tensor_copy(before16[:], constant(shared, "before"))
            dve.memset(ones16[:], 1.0)
            dve.tensor_copy(shared.row16[:], constant(shared, "row"))
            dve.tensor_scalar(shared.token[:], constant(shared, "steps"), constant(shared, "tile"), None, ALU.add)

            dve.wait_ge(sig_done, 1)
            link(dve.tensor_tensor(sfc[:], scores[:], repeat(bias[:].unsqueeze(1), 1, NT), ALU.add))
            pairs = sfc[:].rearrange("p t (g a b) -> p (t g) a b", a=2, b=2)
            G = NT * GROUPS
            hi = tmpa[:, 0:2 * G].rearrange("p (g a) -> p g a", a=2)
            lo = tmpa[:, 2 * G:4 * G].rearrange("p (g a) -> p g a", a=2)
            dve.tensor_tensor(hi, pairs[:, :, :, 0], pairs[:, :, :, 1], ALU.max)
            link(dve.tensor_tensor(lo, pairs[:, :, :, 0], pairs[:, :, :, 1], ALU.min))
            m1, m2, m3 = tmpb[:, 0:G], tmpb[:, G:2 * G], tmpb[:, 2 * G:3 * G]
            dve.tensor_tensor(m1, hi[:, :, 0], hi[:, :, 1], ALU.max)
            dve.tensor_tensor(m2, hi[:, :, 0], hi[:, :, 1], ALU.min)
            link(dve.tensor_tensor(m3, lo[:, :, 0], lo[:, :, 1], ALU.max))
            link(dve.tensor_tensor(m2, m2, m3, ALU.max))
            gflat = gs[:].rearrange("p t g -> p (t g)")
            link(dve.tensor_tensor(gflat, m1, m2, ALU.add))
            def square(a):
                return a.rearrange("p (t g h) -> p t g h", g=GROUPS, h=GROUPS)
            other = repeat(gs[:].unsqueeze(2), 2, GROUPS)
            this = repeat(gs[:].unsqueeze(3), 3, GROUPS)
            dve.tensor_tensor(square(tmpa), other, this, ALU.is_gt)
            link(dve.tensor_tensor(square(tmpb), other, this, ALU.is_ge))
            lower = repeat(constant(shared, "lower").unsqueeze(1), 1, NT)
            link(dve.tensor_tensor(tmpb.rearrange("p (t a) -> p t a", t=NT), tmpb.rearrange("p (t a) -> p t a", t=NT),
                                   lower, ALU.mult))
            link(dve.tensor_tensor(tmpa, tmpa, tmpb, ALU.max))
            link(dve.tensor_reduce(gflat, tmpa.rearrange("p (g h) -> p g h", h=GROUPS), AX.X, ALU.add))
            link(dve.tensor_scalar(keep[:], gs[:], TOPG - 0.5, None, ALU.is_lt))
            dve.tensor_scalar(pen[:], keep[:], -NEG, NEG, ALU.mult, ALU.add)
            s4 = sfc[:].rearrange("p t (g a) -> p (t g) a", a=PER)
            k4 = repeat(keep[:].rearrange("p t g -> p (t g)").unsqueeze(2), 2, PER)
            p4 = repeat(pen[:].rearrange("p t g -> p (t g)").unsqueeze(2), 2, PER)
            link(dve.tensor_tensor(s4, s4, k4, ALU.mult))
            link(dve.tensor_tensor(s4, s4, p4, ALU.add))
            for t in range(NT):
                ins = dve.max(top8[:, t, :], sfc[:, t, :])
            link(ins)
            for t in range(NT):
                ins = dve.max_index(top8i[:, t, :], top8[:, t, :], sfc[:, t, :])
            link(ins)
            link(dve.tensor_copy(topf[:], top8i[:]))
            ex = repeat(constant(shared, "expert").unsqueeze(1), 1, NT)
            dve.wait_ge(xn_stored, 16)
            for j in range(TOPK):
                ins = dve.tensor_tensor(onehot[:, j], ex, repeat(topf[:, :, j:j + 1], 2, E), ALU.is_equal)
            link(ins)
            link(dve.tensor_tensor(chosen[:], onehot[:, 0], onehot[:, 1], ALU.add))
            for j in range(2, TOPK):
                ins = dve.tensor_tensor(chosen[:], chosen[:], onehot[:, j], ALU.add)
                if j < TOPK - 1:
                    link(ins)
            ins.then_inc(chosen_ready, 1)
            for j in range(TOPK):
                ins = dve.tensor_tensor(wide[:, j], onehot[:, j], scores[:], ALU.mult)
            link(ins)
            link(dve.tensor_reduce(topw[:].rearrange("p t j -> p j t"), wide, AX.X, ALU.add))
            dve.wait_ge(counted, 1)
            big = tmpa[:, 0:E * NT].rearrange("p (e s) -> p e s", s=NT)
            link(dve.tensor_tensor(big, repeat(bank[4][:, 0:E].unsqueeze(2), 2, NT),
                                   repeat(constant(shared, "steps").unsqueeze(1), 1, E), ALU.is_gt))
            link(dve.tensor_reduce(ntile[:, 0, :].unsqueeze(2), big, AX.X, ALU.add))
            at, width = 0, 1
            while width < E:
                dve.tensor_copy(ntile[:, at + 1, 0:width], ntile[:, at, 0:width])
                link(dve.tensor_tensor(ntile[:, at + 1, width:E], ntile[:, at, width:E], ntile[:, at, 0:E - width], ALU.add))
                at, width = at + 1, 2 * width
            ends = ntile[:, at, :]
            link(dve.tensor_scalar(tmpb[:, 0:E], ends, constant(shared, "tile"), None, ALU.is_le))
            link(dve.tensor_reduce(own[:], tmpb[:, 0:E], AX.X, ALU.add))
            dve.tensor_scalar(own[:], own[:], float(E - 1), None, ALU.min).then_inc(own_ready, 1)
            link(dve.tensor_tensor(ntile[:, 0, :], ends, ntile[:, 0, :], ALU.subtract))
            link(dve.tensor_scalar(ntile[:, 0, :], ntile[:, 0, :], float(P), None, ALU.mult))
            link(dve.tensor_tensor(earlier, bank[3][:].rearrange("p (t e) -> p t e", e=E), repeat(ntile[:, 0:1, :], 1, NT), ALU.add))
            for j in range(TOPK):
                ins = dve.tensor_tensor(wide[:, j], onehot[:, j], earlier, ALU.mult)
            link(ins)
            link(dve.tensor_reduce(slotf[:].rearrange("p t j -> p j t"), wide, AX.X, ALU.add))
            link(dve.tensor_copy(slot[:], slotf[:]))
            dve.tensor_scalar(digits[:, 0], slot[:], 7, None, ALU.logical_shift_right)
            link(dve.tensor_scalar(digits[:, 1], slot[:], P - 1, None, ALU.bitwise_and))
            dve.tensor_copy(shared.place[:], digits[:])
            dve.wait_ge(own_turned, 1)
            dve.tensor_copy(shared.tile_expert[:], bank[5][0:1, 0:P])


def dense_block(nc, shared):
    bank, ident = shared.bank, shared.ident
    A, w_gu, w_dn, w_qkv, ws_dn = shared.A, shared.w_gu, shared.w_dn, shared.w_qkv, shared.ws_dn
    place, token, row16 = shared.place, shared.token, shared.row16
    psList, psQK, psV, psR, psY = bank[0:5]
    with ExitStack() as ctx:
        def sb(name, shape, dt=F32):
            return ctx.enter_context(nc.sbuf_tensor(name, shape, dt))

        def sem(name):
            return ctx.enter_context(nc.semaphore(name))

        front = Carver(shared.front)
        xT = front([P, 2, D])
        hT = front([P, 2, HC, P])
        xres = front([P, 2, D])
        rot = front([P, 2, 2 * D])
        swapped = front([P, 2 * D])
        rest = front([P, 2 * D])
        parts = front([P, 2, 3, 2 * KD, 2, P], BF16)
        free = shared.ws_gu[:].rearrange("p g k m -> p (g k m)")
        vout = free[:, 0:2 * D].rearrange("p (b n) -> p b n", b=2)
        at_place = free[:, 2 * D:2 * D + TOPK * P].bitcast(F16).rearrange("p (b j a) -> p b j a", b=2, j=TOPK)
        yout = sb("yout", [P, 2, D])
        in_tile = front([P, 2, TOPK, P], F16)

        tile_of, tile_of_ready = sb("tile_of", [P, 2, TOPK]), sem("tile_of_ready")
        number = sb("number", [P, 2])
        waited, waited_sp = sem("waited"), sem("waited_sp")
        copied, xres_in = sem("copied"), [sem(f"xres_in{b}") for b in range(2)]
        tile_ready, place_found, number_ready, place_ready, listed = (
            sem(s) for s in ("tile_ready", "place_found", "number_ready", "place_ready", "listed"))
        qk_done, rope_read, rot_ready = sem("qk_done"), sem("rope_read"), sem("rot_ready")
        rotT_done, part1, rest_ready, part2, part3 = (sem(s) for s in ("rotT_done", "part1", "rest_ready", "part2", "part3"))
        v_done, v_copied = sem("v_done"), sem("v_copied")
        y_done, y_ready, y_summed = (sem(s) for s in ("y_done", "y_ready", "y_summed"))
        parts_stored = [sem(f"parts_stored{i}") for i in range(2)]
        v_stored = [sem(f"v_stored{i}") for i in range(2)]
        y_stored = [sem(f"y_stored{i}") for i in range(2)]
        block = ctx.enter_context(nc.Block())

        def tiles(eng, body):
            for c in range(TPB):
                body(c, c, 0)
            with eng.Fori(1, NT // TPB) as g:
                for c in range(TPB):
                    body(TPB * g + c, c, g)

        @block.sync
        def _(sp):
            def load_x(t, b):
                wait(sp, y_summed, t - 1)
                sp.sem_inc(waited_sp, 1)
                sp.dma_start(xres[:, b, :], A["x"][bass.ts(t, P), :]).then_inc(xres_in[b], 16)

            def load_experts(t):
                sp.wait_ge(copied, t + 1)
                sp.sem_inc(waited_sp, 1)
                e = bass.ts(t, 2)
                for g, name in enumerate(("gate_w", "up_w")):
                    sp.dma_start(w_gu[:, g, e], A[name][e].rearrange("e (p k) m -> p e k m", k=KD)).then_inc(shared.weights_in, 16)

            def store(t, c, g):
                b, pair = c % 2, c // 2
                sp.wait_ge(v_copied, t + 1)
                sp.dma_start(shared.v_dram[bass.ts(t, P), :], vout[:, b, :]).then_inc(v_stored[b], 16)
                sp.wait_ge(y_summed, t + 1)
                sp.dma_start(shared.shared_y[bass.ts(t, P), :], yout[:, b, :]).then_inc(y_stored[b], 16)
                if b == 1:
                    for a, ready in enumerate((part1, part2, part3)):
                        sp.wait_ge(ready, t + 1)
                        sp.dma_start(shared.qk_parts[a, :, :, bass.ts(2 * g + pair, 2 * P)].rearrange("c p t -> p c t"),
                                     parts[:, pair, a].rearrange("p c b t -> p c (b t)")).then_inc(parts_stored[pair], 16)

            def body(t, c, g):
                load_x(t, c % 2)
                load_experts(t)
                if not is_first(t):
                    store(t - 1, (c - 1) % TPB, g if c else g - 1)

            tiles(sp, body)
            store(NT - 1, TPB - 1, NT // TPB - 1)
            sp.wait_ge(shared.weights_in, 16 * 2 * NT)
            sp.wait_ge(shared.down_in, 16 * 4)
            for b in range(2):
                sp.wait_ge(v_stored[b], 16 * (NT // 2))
                sp.wait_ge(y_stored[b], 16 * (NT // 2))
                sp.wait_ge(parts_stored[b], 48 * (NT // TPB))

        @block.gpsimd
        def _(pool):
            def add_x(t, c, g):
                b, pair = c % 2, c // 2
                pool.wait_ge(y_ready, t + 1)
                pool.sem_inc(waited, 1)
                pool.wait_ge(xres_in[b], 16 * (2 * g + pair) + 16)
                pool.sem_inc(waited, 1)
                pool.tensor_tensor(yout[:, b, :], yout[:, b, :], xres[:, b, :], ALU.add).then_inc(y_summed, 1)

            def body(t, c, g):
                b = c % 2
                if not is_first(t):
                    add_x(t - 1, (c - 1) % TPB, g if c else g - 1)
                wait(pool, listed, t - 1)
                pool.sem_inc(waited, 1)
                pool.tensor_copy(number[:, b:b + 1], token[:, bass.ds(t, 1)]).then_inc(number_ready, 1)
                pool.tensor_copy(tile_of[:, b, :], place[:, 0, bass.ds(t, 1), :].rearrange("p t j -> p (t j)")).then_inc(tile_of_ready, 1)
                pool.wait_ge(tile_of_ready, t + 1)
                pool.sem_inc(waited, 1)
                for j in range(TOPK):
                    ins = pool.tensor_scalar(in_tile[:, b, j, :], row16[:], tile_of[:, b, j:j + 1], None, ALU.is_equal)
                ins.then_inc(tile_ready, 1)

            tiles(pool, body)
            add_x(NT - 1, TPB - 1, NT // TPB - 1)

        @block.tensor
        def _(pe):
            def list_tokens(t, b):
                pe.wait_ge(tile_ready, t + 1)
                pe.wait_ge(place_ready, t + 1)
                for j in range(TOPK):
                    mm = pe.matmul(psList[:, 0:P], at_place[:, b, j, :], in_tile[:, b, j, :],
                                   start=(is_first(t) and j == 0), stop=True, skip_group_check=True)
                mm.then_inc(listed, 1)

            def body(t, c, g):
                b = c % 2
                if is_first(t):
                    pe.wait_ge(shared.dense_in, 16 * (3 + HC))
                pe.wait_ge(copied, t + 1)
                wait(pe, rope_read, t)
                for k in range(KD):
                    mm = pe.matmul(psQK[:], xT[:, b, k * P:(k + 1) * P], w_qkv[:, k, 0:2, :].rearrange("p a n -> p (a n)"),
                                   start=(k == 0), stop=(k == KD - 1))
                mm.then_inc(qk_done, 1)
                wait(pe, v_copied, t)
                for k in range(KD):
                    mm = pe.matmul(psV[:, 0:D], xT[:, b, k * P:(k + 1) * P], w_qkv[:, k, 2, :], start=(k == 0), stop=(k == KD - 1))
                mm.then_inc(v_done, 1)
                wait(pe, y_ready, t)
                for q, (_, rows) in enumerate(SHARED):
                    mm = pe.matmul(psY[:, 0:D], hT[0:rows, b, q, :], ws_dn[0:rows, q, :], start=(q == 0), stop=(q == HC - 1))
                mm.then_inc(y_done, 1)
                if not is_first(t):
                    list_tokens(t - 1, 1 - b)
                pe.wait_ge(rot_ready, t + 1)
                wait(pe, rest_ready, t)
                for q in range(2 * KD):
                    mm = pe.transpose(psR[:, q * P:(q + 1) * P], rot[:, b, q * P:(q + 1) * P], ident)
                mm.then_inc(rotT_done, 1)

            tiles(pe, body)
            list_tokens(NT - 1, 1)

        @block.scalar
        def _(act):
            def fetch(t, b):
                wait(act, v_done, t - 1)
                wait(act, y_done, t - 1)
                nc.scalar.activation(xT[:, b, :], shared.xT_all[:, bass.ds(t, 1), 0:D].rearrange("p t n -> p (t n)"), ACT.Copy)
                nc.scalar.activation(hT[:, b], shared.hT_all[:, bass.ds(t, 1)].rearrange("p t c n -> p (t c) n"), ACT.Copy).then_inc(copied, 1)

            def numbers(t, b):
                act.wait_ge(place_found, t + 1)
                act.wait_ge(number_ready, t + 1)
                flat = at_place[:, b].rearrange("p j a -> p (j a)")
                nc.scalar.activation(flat, flat, ACT.Copy, scale=number[:, b:b + 1]).then_inc(place_ready, 1)

            def second(t, c):
                b, pair = c % 2, c // 2
                act.wait_ge(rest_ready, t + 1)
                nc.scalar.activation(parts[:, pair, 1, :, b, :], rest[:].rearrange("p (c t) -> p c t", c=2 * KD), ACT.Copy).then_inc(part2, 1)

            def body(t, c, g, last=False):
                b, pair = c % 2, c // 2
                if not is_first(t):
                    second(t - 1, (c - 1) % TPB)
                    numbers(t - 1, 1 - b)
                act.wait_ge(v_done, t + 1)
                wait(act, v_stored[b], 16 * (2 * g + pair))
                nc.scalar.activation(vout[:, b, :], psV[:, 0:D], ACT.Copy).then_inc(v_copied, 1)
                if not last:
                    fetch(t + 1, 1 - b)
                act.wait_ge(y_done, t + 1)
                wait(act, y_stored[b], 16 * (2 * g + pair))
                nc.scalar.activation(yout[:, b, :], psY[:, 0:D], ACT.Copy).then_inc(y_ready, 1)
                act.wait_ge(rotT_done, t + 1)
                if b == 0:
                    wait(act, parts_stored[pair], 48 * g)
                nc.scalar.activation(parts[:, pair, 0, :, b, :], psR[:].rearrange("p (c t) -> p c t", c=2 * KD), ACT.Copy).then_inc(part1, 1)

            fetch(0, 0)
            for c in range(TPB):
                body(c, c, 0)
            with act.Fori(1, NT // TPB - 1) as g:
                for c in range(TPB):
                    body(TPB * g + c, c, g)
            for c in range(TPB):
                body(NT - TPB + c, c, NT // TPB - 1, last=(c == TPB - 1))
            numbers(NT - 1, 1)
            second(NT - 1, TPB - 1)

        @block.vector
        def _(dve):
            def rope(t, b, c):
                dve.wait_ge(qk_done, t + 1)
                wait(dve, rotT_done, t - 1)
                heads = psQK[:].rearrange("p (h d) -> p h d", d=HD)
                pairs = psQK[:].rearrange("p (h i a) -> p h i a", i=HD // 2, a=2)
                tp = swapped[:].rearrange("p (h i a) -> p h i a", i=HD // 2, a=2)
                cos = repeat(constant(shared, "cos")[:, c * HD:(c + 1) * HD].unsqueeze(1), 1, 2 * HEADS)
                nsin = repeat(constant(shared, "nsin")[:, c * HD // 2:(c + 1) * HD // 2].unsqueeze(1), 1, 2 * HEADS)
                sin = repeat(constant(shared, "sin")[:, c * HD // 2:(c + 1) * HD // 2].unsqueeze(1), 1, 2 * HEADS)
                dve.tensor_tensor(rot[:, b, :].rearrange("p (h d) -> p h d", d=HD), heads, cos, ALU.mult)
                dve.tensor_tensor(tp[:, :, :, 0], pairs[:, :, :, 1], nsin, ALU.mult)
                dve.tensor_tensor(tp[:, :, :, 1], pairs[:, :, :, 0], sin, ALU.mult).then_inc(rope_read, 1)
                dve.wait_ge(rope_read, t + 1)
                dve.tensor_tensor(rot[:, b, :], rot[:, b, :], swapped[:], ALU.add).then_inc(rot_ready, 1)

            def places(t, b):
                wait(dve, listed, t - 1)
                dve.tensor_tensor(at_place[:, b], repeat(row16[:].unsqueeze(1), 1, TOPK),
                                  repeat(place[:, 1, bass.ds(t, 1), :].rearrange("p t j -> p (t j)").unsqueeze(2), 2, P),
                                  ALU.is_equal).then_inc(place_found, 1)

            def third(t, c):
                b, pair = c % 2, c // 2
                dve.wait_ge(part2, t + 1)
                dve.tensor_tensor(parts[:, pair, 2, :, b, :], rest[:].rearrange("p (c t) -> p c t", c=2 * KD),
                                  parts[:, pair, 1, :, b, :], ALU.subtract).then_inc(part3, 1)

            def body(t, c, g):
                b, pair = c % 2, c // 2
                rope(t, b, c)
                if not is_first(t):
                    third(t - 1, (c - 1) % TPB)
                places(t, b)
                wait(dve, part3, t)
                dve.wait_ge(part1, t + 1)
                dve.tensor_tensor(rest[:].rearrange("p (c t) -> p c t", c=2 * KD), psR[:].rearrange("p (c t) -> p c t", c=2 * KD),
                                  parts[:, pair, 0, :, b, :], ALU.subtract).then_inc(rest_ready, 1)

            tiles(dve, body)
            third(NT - 1, TPB - 1)
            dve.wait_ge(listed, NT)
            dve.tensor_copy(shared.slot_token[:], psList[:, 0:P])


def expert_block(nc, shared):
    ident, w_gu, w_dn, tile_expert, slot_token = shared.ident, shared.w_gu, shared.w_dn, shared.tile_expert, shared.slot_token
    bank = shared.bank
    psX, psGU, psH, psY = bank[0:2], bank[2:4], bank[4:6], bank[6:8]
    N = SLOT_TILES
    UNROLL = 4
    FIRST = 7
    assert (N - FIRST) % UNROLL == 0 and FIRST % 2 == 1
    with ExitStack() as ctx:
        def sb(name, shape, dt=F32):
            return ctx.enter_context(nc.sbuf_tensor(name, shape, dt))

        def sem(name):
            return ctx.enter_context(nc.semaphore(name))

        xg = sb("xg", [P, 2, D])
        xT = sb("exT", [P, 2, KD, P])
        silu = sb("esilu", [P, 2, M])
        h = sb("eh", [P, 2, M])
        hT = sb("ehT", [MH, 2, 2, P])
        y = sb("ey", [P, 2, D])
        token = sb("token", [P, 2], U32)
        token_ready, waited = sem("token_ready"), sem("ewaited")
        x_in = [sem(f"ex_in{i}") for i in range(2)]
        y_stored = [sem(f"ey_stored{i}") for i in range(2)]
        xt_done, xT_ready, gu_done, silu_ready, h_ready, ht_done, hT_ready, y_done, y_copied = (
            sem(f"e_{s}") for s in ("xt_done", "xT_ready", "gu_done", "silu_ready", "h_ready", "ht_done", "hT_ready",
                                    "y_done", "y_copied"))
        block = ctx.enter_context(nc.Block())

        def steps(eng, step):
            for s in range(FIRST):
                step(s, s % 2, s // 2, s)
            with eng.Fori(0, (N - FIRST) // UNROLL) as i:
                for c in range(FIRST, FIRST + UNROLL):
                    step(UNROLL * i + c, c % 2, UNROLL // 2 * i + c // 2, c)
            for s in range(N, N + 3):
                step(s, s % 2, s // 2, s)

        def inside(j):
            return not isinstance(j, int) or 0 <= j < N

        @block.sync
        def _(sp):
            def store(j, b):
                sp.wait_ge(y_copied, j + 1)
                sp.dma_start(shared.slots_y[bass.ts(j, P), :], y[:, b, :]).then_inc(y_stored[b], 16)

            store(0, 0)
            loads = [(half, pair) for half in range(KD) for pair in operand_loads(shared.qk_parts, shared.q_first, shared.k_first, 0, half)]
            for j, (half, (dst, src)) in enumerate(loads):
                sp.dma_start(dst, src).then_inc(shared.qk_in[0][half], 16)
                store(j + 1, (j + 1) % 2)
            with sp.Fori(len(loads) // 2, N // 2) as i:
                store(2 * i + 1, 1)
                store(2 * i + 2, 0)
            sp.wait_ge(y_stored[0], 16 * ((N + 1) // 2))
            sp.wait_ge(y_stored[1], 16 * (N // 2))

        @block.gpsimd
        def _(pool):
            def load(j, b, use):
                wait(pool, x_in[b], 16 * use)
                pool.sem_inc(waited, 1)
                pool.tensor_copy(token[:, b:b + 1], slot_token[:, bass.ds(j, 1)]).then_inc(token_ready, 1)
                pool.wait_ge(token_ready, j + 1)
                pool.sem_inc(waited, 1)
                wait(pool, xt_done, j - 1)
                pool.sem_inc(waited, 1)
                pool.indirect_dma_start(out=xg[:, b, :], out_offset=None, in_=shared.xn_dram,
                                        in_offset=bass.IndirectOffsetOnAxis(ap=token[:, b:b + 1], axis=0)).then_inc(x_in[b], 16)

            for j in range(3):
                load(j, j % 2, j // 2)
            with pool.Fori(1, N // 2) as i:
                load(2 * i + 1, 1, i)
                load(2 * i + 2, 0, i + 1)

        @block.tensor
        def _(pe):
            def turn_x(j, b, use):
                pe.wait_ge(x_in[b], 16 * use + 16)
                wait(pe, xT_ready, j - 1)
                for k in range(KD):
                    mm = pe.transpose(psX[b][:, k * P:(k + 1) * P], xg[:, b, k::KD], ident)
                mm.then_inc(xt_done, 1)

            def gate_up(j, b, e):
                pe.wait_ge(xT_ready, j + 1)
                wait(pe, h_ready, j - 1)
                for k in range(KD):
                    mm = pe.matmul(psGU[b][:, 0:2 * M].rearrange("p (g m) -> p g m", g=2), xT[:, b, k, :],
                                   w_gu[:, :, bass.ds(e, 1), k, :].rearrange("p g e m -> p g (e m)"),
                                   start=(k == 0), stop=(k == KD - 1))
                mm.then_inc(gu_done, 1)

            def turn_h(j, b):
                pe.wait_ge(h_ready, j + 1)
                wait(pe, hT_ready, j - 1)
                for k in range(2):
                    mm = pe.transpose(psH[b][0:MH, k * P:(k + 1) * P], h[:, b, k::2], ident)
                mm.then_inc(ht_done, 1)

            def down(j, b, e):
                pe.wait_ge(hT_ready, j + 1)
                wait(pe, y_copied, j - 1)
                for k in range(2):
                    mm = pe.matmul(psY[b][:, 0:D], hT[:, b, k, :], w_dn[:, bass.ds(e, 1), k, :].rearrange("p e n -> p (e n)"),
                                   start=(k == 0), stop=(k == 1))
                mm.then_inc(y_done, 1)

            number = [pe.alloc_register(f"expert{k}") for k in range(UNROLL)]

            def expert(c):
                return pe.snap(number[c % UNROLL], min_val=0, max_val=E - 1)

            def step(s, b, use, c):
                if inside(s - 3):
                    turn_h(s - 3, 1 - b)
                if inside(s):
                    turn_x(s, b, use)
                if inside(s - 1):
                    gate_up(s - 1, 1 - b, expert(c - 1))
                if inside(s):
                    pe.reg_load(number[c % UNROLL], tile_expert[0:1, bass.ds(s, 1)])
                if inside(s - 3):
                    down(s - 3, 1 - b, expert(c - 3))

            steps(pe, step)

        @block.scalar
        def _(act):
            nc.scalar.activation(shared.k_first[ROWS:ROWS + 3].rearrange("p h t -> p (h t)"),
                                 repeat(ident[ROWS:ROWS + 3, 0:1], 1, HEADS * SEQ), ACT.Copy, scale=0.0, bias=1.0).then_inc(shared.ones_made, 1)

            def copy_hT(j, b):
                act.wait_ge(ht_done, j + 1)
                wait(act, y_done, j - 1)
                nc.scalar.activation(hT[:, b].rearrange("p k t -> p (k t)"), psH[b][0:MH, 0:2 * P], ACT.Copy).then_inc(hT_ready, 1)

            def gate(j, b):
                act.wait_ge(gu_done, j + 1)
                wait(act, h_ready, j - 1)
                nc.scalar.activation(silu[:, b, :], psGU[b][:, 0:M], ACT.Silu).then_inc(silu_ready, 1)

            def step(s, b, use, c):
                if inside(s - 3):
                    copy_hT(s - 3, 1 - b)
                if inside(s - 1):
                    gate(s - 1, 1 - b)

            steps(act, step)

        @block.vector
        def _(dve):
            def copy_xT(j, b):
                dve.wait_ge(xt_done, j + 1)
                wait(dve, gu_done, j - 1)
                dve.tensor_copy(xT[:, b].rearrange("p k t -> p (k t)"), psX[b][:, 0:D]).then_inc(xT_ready, 1)

            def gated(j, b):
                dve.wait_ge(silu_ready, j + 1)
                wait(dve, ht_done, j - 1)
                dve.tensor_tensor(h[:, b, :], psGU[b][:, M:2 * M], silu[:, b, :], ALU.mult).then_inc(h_ready, 1)

            def copy_y(j, b, use):
                dve.wait_ge(y_done, j + 1)
                wait(dve, y_stored[b], 16 * use)
                dve.tensor_copy(y[:, b, :], psY[b][:, 0:D]).then_inc(y_copied, 1)

            def step(s, b, use, c):
                if inside(s):
                    copy_xT(s, b)
                if inside(s - 1):
                    gated(s - 1, 1 - b)
                if inside(s - 3):
                    copy_y(s - 3, 1 - b, use - 1 if b == 1 else use - 2)

            steps(dve, step)


def attention_block(nc, shared):
    bank, ident, slot, topw = shared.bank, shared.ident, shared.slot, shared.topw
    LEAD = 2
    WIDE = [SEQ - P * j for j in range(TPB)]
    AT = [0, SEQ, 2 * SEQ, 2 * SEQ - WIDE[3]]
    PT_N = sum(WIDE)
    BUFS = 2
    qk_in, ones_made = shared.qk_in, shared.ones_made
    SCALE = 1.0 / np.sqrt(HD)
    bST, bS, bO, bT, bW = bank[0:2], bank[2:5], bank[5], bank[6], bank[7]
    MUNITS = [(3, [h]) for h in range(G)] + [(2, [h]) for h in range(G)] + [(1, [0, 1]), (1, [2, 3]), (0, [0, 1, 2, 3])]
    NM = len(MUNITS)
    SUNITS = []
    for h in (0, 2):
        SUNITS += [[(h, 0, 0)], [(h, 1, 0), (h, 3, WIDE[1])], [(h, 2, 0), (h + 1, 2, WIDE[2])],
                   [(h + 1, 0, 0)], [(h + 1, 1, 0), (h + 1, 3, WIDE[1])]]
    NS = len(SUNITS)
    A, out, max_dram = shared.A, shared.out, shared.max_dram

    with ExitStack() as ctx:
        def sb(name, shape, dt=F32):
            return ctx.enter_context(nc.sbuf_tensor(name, shape, dt))

        def sem(name):
            return ctx.enter_context(nc.semaphore(name))

        qs = [shared.q_first, sb("q_second", [ROWS + 3, HEADS, SEQ], BF16)]
        ks = [shared.k_first, sb("k_second", [ROWS + 3, HEADS, SEQ], BF16)]
        vraw = sb("vraw", [P, BATCH, TPB, D])
        vpad = sb("vpad", [P, 2, TPB, G, 32])
        pt = sb("pt", [P, 2, G, PT_N])
        oT = sb("oT", [P, 2, SEQ])
        attn = sb("attn", [P, TPB, D])
        aT = sb("aT", [P, TPB, KD, P])
        recip = sb("recip", [P, TPB, G])
        mx = sb("mx", [P, 2, G, TPB])
        negm = sb("negm", [G * TPB, 3, P], BF16)
        mrest = sb("mrest", [G * TPB, P])
        w_o = sb("w_o", [P, KD, D])
        ident16 = sb("ident16", [P, P], BF16)
        future16 = sb("future16", [P, P], BF16)
        futureT16 = sb("futureT16", [P, P], BF16)
        gath = sb("gath", [P, 2, TOPK, D])
        base = sb("base", [P, 2, D])
        acc = sb("acc", [P, 2 * TPB, D])
        idx = sb("cidx", [P, 2, TOPK], U32)

        v_in = [sem(f"v_in{b}") for b in range(BATCH)]
        wo_in, ones_in, masks_ready = sem("wo_in"), sem("ones_in"), sem("masks_ready")
        vpad_zero, vpad_ready = sem("vpad_zero"), sem("vpad_ready")
        s_done, s_read = sem("s_done"), sem("s_read")
        m_turned, m_part1, m_rest, m_part2, m_part3, m_out = (sem(f"m_{s}") for s in ("turned", "part1", "rest", "part2", "part3", "out"))
        m_in = [sem(f"m_in{i}") for i in range(2)]
        st_done, exp_done = sem("st_done"), sem("exp_done")
        pv_done, oT_ready, o_turned, recip_ready, attn_ready = (sem(s) for s in ("pv_done", "oT_ready", "o_turned", "recip_ready", "attn_ready"))
        a_turned, aT_ready, wo_done, added = (sem(s) for s in ("a_turned", "aT_ready", "wo_done", "added"))
        base_in = [sem(f"base_in{b}") for b in range(2)]
        gathered = [sem(f"gathered{b}") for b in range(2)]
        cidx_ready, cwaited = sem("cidx_ready"), sem("cwaited")
        combine, combined, stored = sem("combine"), sem("combined"), sem("stored")
        block = ctx.enter_context(nc.Block())

        def exp_bank(g, n):
            m = n - NS * (NG - LEAD)
            if m < 0:
                return bST[n % 2], n - 1
            return (bST + bS)[m % 5], n - 1 if m < 2 else n - 4 if m >= 5 else 0

        @block.sync
        def _(sp):
            def load_qk(b, half):
                if b >= BUFS:
                    sp.wait_ge(st_done, NS * (GPB * (b - BUFS) + GPB // 2 * (half + 1)))
                for dst, src in operand_loads(shared.qk_parts, qs[b % BUFS], ks[b % BUFS], b, half):
                    sp.dma_start(dst, src).then_inc(qk_in[b][half], 16)

            def load_base(t):
                wait(sp, combined, t - 1)
                sp.dma_start(base[:, t % 2, :], shared.shared_y[t * P:(t + 1) * P, :]).then_inc(base_in[t % 2], 16)

            def max_rows(g):
                sp.wait_ge(m_part3, g + 1)
                sp.dma_start(max_dram[g].rearrange("a h (c t) -> (h c) a t", t=P), negm[:]).then_inc(m_out, 16)
                sp.wait_ge(m_out, 16 * (g + 1))
                h0 = G * (g % GPB)
                sp.dma_start(qs[(g // GPB) % BUFS][ROWS:ROWS + 3, h0:h0 + G], max_dram[g]).then_inc(m_in[g % 2], 16)

            def load_v(b):
                sp.dma_start(vraw[:, b], shared.v_dram[SEQ * b:SEQ * (b + 1), :].rearrange("(j p) n -> p j n", p=P)).then_inc(v_in[b], 16)

            load_base(0)
            load_base(1)
            load_v(0)
            sp.wait_ge(ones_made, 1)
            sp.dma_start(ks[1][ROWS:ROWS + 3], ks[0][ROWS:ROWS + 3]).then_inc(ones_in, 16)
            for g in range(LEAD):
                max_rows(g)
                load_qk(1, g)
            sp.dma_start(w_o[:], A["woT"].rearrange("(p k) n -> p k n", k=KD)).then_inc(wo_in, 16)
            for k in range(2, NT):
                load_base(k)
                if k % GPB == 2 and k // GPB + 1 < BATCH:
                    load_v(k // GPB + 1)
                if k - 2 + LEAD < NG:
                    max_rows(k - 2 + LEAD)
                if k % GPB == 3 and (k + 5) // GPB < BATCH:
                    load_qk((k + 5) // GPB, 0)
                if k % GPB == 1 and k > GPB and (k + 3) // GPB < BATCH:
                    load_qk((k + 3) // GPB, 1)
            sp.wait_ge(stored, 32 * BATCH)

        @block.gpsimd
        def _(pool):
            pool.memset(vpad[:], 0.0).then_inc(vpad_zero, 1)
            pool.wait_ge(vpad_zero, 1)
            pool.memset(vpad[:, :, :, :, HD:HD + 1], 1.0).then_inc(vpad_zero, 1)
            pool.wait_ge(vpad_zero, 2)

            def group(s, r):
                t, b = GPB * s + r, r % 2
                wait(pool, combined, t - 1)
                pool.sem_inc(cwaited, 1)
                pool.tensor_copy(idx[:, b, :], slot[:, bass.ds(t, 1), :].rearrange("p a j -> p (a j)")).then_inc(cidx_ready, 1)
                pool.wait_ge(cidx_ready, t + 1)
                pool.sem_inc(cwaited, 1)
                for j in range(TOPK):
                    pool.indirect_dma_start(out=gath[:, b, j, :], out_offset=None, in_=shared.slots_y,
                                            in_offset=bass.IndirectOffsetOnAxis(ap=idx[:, b, j:j + 1], axis=0)).then_inc(gathered[b], 16)
                if r == 0:
                    pool.wait_ge(v_in[s], 16)
                wait(pool, pv_done, t - 1)
                pool.sem_inc(cwaited, 1)
                pool.tensor_copy(vpad[:, b, :, :, 0:HD],
                                 vraw[:, s, :, G * HD * r:G * HD * (r + 1)].rearrange("p j (h d) -> p j h d", d=HD)).then_inc(vpad_ready, 1)

            for s in range(BATCH):
                for r in range(GPB):
                    group(s, r)

        @block.tensor
        def _(pe):
            pe.wait_ge(masks_ready, 3)

            def max_unit(g, u):
                b, n = g // GPB, NM * g + u
                c, heads = MUNITS[u]
                if u == 0 and g % 2 == 0:
                    pe.wait_ge(qk_in[b][g % GPB // 2], 16 * 2 * len(QPART))
                wait(pe, s_read, n - 2)
                bk, w = bS[n % 3], P * (c + 1)
                for i, h in enumerate(heads):
                    hh = G * (g % GPB) + h
                    pe.matmul(bk[:, i * w:(i + 1) * w], qs[b % BUFS][0:ROWS, hh, c * P:(c + 1) * P],
                              ks[b % BUFS][0:ROWS, hh, 0:w], start=True, stop=True)
                    mm = pe.matmul(bk[:, i * w + c * P:(i + 1) * w], ident16[:], future16[:], start=False, stop=True,
                                   skip_group_check=True)
                mm.then_inc(s_done, 1)

            def exp_unit(g, u):
                b, n = g // GPB, NS * g + u
                if u == 0:
                    pe.wait_ge(m_in[g % 2], 16 * (g // 2 + 1))
                    if g == 0:
                        pe.wait_ge(ones_made, 1)
                    if g == GPB:
                        pe.wait_ge(ones_in, 16)
                bk, used = exp_bank(g, n)
                wait(pe, exp_done, used)
                if g == NG - LEAD and 2 <= u < 5:
                    pe.wait_ge(s_read, NM * NG)
                for h, j, col in SUNITS[u]:
                    hh = G * (g % GPB) + h
                    pe.matmul(bk[:, col:col + WIDE[j]], ks[b % BUFS][:, hh, j * P:(j + 1) * P],
                              qs[b % BUFS][:, hh, j * P:SEQ], start=True, stop=True)
                    mm = pe.matmul(bk[:, col:col + P], ident16[:], futureT16[:], start=False, stop=True, skip_group_check=True)
                mm.then_inc(st_done, 1)

            def pv(g, j):
                if j == 0:
                    pe.wait_ge(exp_done, NS * (g + 1))
                    pe.wait_ge(vpad_ready, g + 1)
                    wait(pe, oT_ready, g)
                for h in range(G):
                    mm = pe.matmul(bO[32 * h:32 * h + 32, j * P:SEQ], vpad[:, g % 2, j, h, :],
                                   pt[:, g % 2, h, AT[j]:AT[j] + WIDE[j]], start=(j == 0), stop=True,
                                   skip_group_check=True)
                if j == TPB - 1:
                    mm.then_inc(pv_done, 1)

            def turn_o(g):
                pe.wait_ge(oT_ready, g + 1)
                wait(pe, attn_ready, g)
                for c in range(TPB):
                    mm = pe.transpose(bT[:, c * P:(c + 1) * P], oT[:, g % 2, c * P:(c + 1) * P], ident)
                mm.then_inc(o_turned, 1)

            def turn_max(g, halves):
                pe.wait_ge(s_read, NM * (g + 1))
                wait(pe, added, halves)
                wait(pe, m_rest, g)
                pe.transpose(bW[0:G * TPB, 0:P], mx[:, g % 2].rearrange("p h c -> p (h c)"), ident).then_inc(m_turned, 1)

            def turn_attn(b, half, maxima):
                pe.wait_ge(attn_ready, GPB * (b + 1))
                pe.wait_ge(m_rest, maxima)
                wait(pe, added, 2 * b)
                if half:
                    pe.wait_ge(aT_ready, 2 * b + 1)
                for c in range(2):
                    for k in range(KD):
                        mm = pe.transpose(bW[:, (2 * c + k) * P:(2 * c + k + 1) * P], attn[:, 2 * half + c, k::KD], ident)
                mm.then_inc(a_turned, 1)

            def project(b, c):
                pe.wait_ge(aT_ready, 2 * b + 2)
                if b == 0 and c == 0:
                    pe.wait_ge(wo_in, 16)
                if c == 2:
                    pe.wait_ge(added, 2 * b + 1)
                for k in range(KD):
                    mm = pe.matmul(bW[:, (c % 2) * D:(c % 2 + 1) * D], aT[:, c, k, :], w_o[:, k, :],
                                   start=(k == 0), stop=(k == KD - 1))
                if c % 2 == 1:
                    mm.then_inc(wo_done, 1)

            for g in range(LEAD):
                for u in range(NM):
                    max_unit(g, u)
                if g < LEAD - 1:
                    turn_max(g, 0)
            for g in range(NG + 3):
                b, r = g // GPB, g % GPB
                for u in range(NM):
                    if g + LEAD < NG:
                        max_unit(g + LEAD, u)
                    if g < NG and u < NS:
                        exp_unit(g, u)
                    attn_step = b >= 1 and r == 1
                    if u < 2 and r == 2 and b >= 1:
                        project(b - 1, 2 + u)
                    if u == 3 and g - 1 + LEAD < NG:
                        turn_max(g - 1 + LEAD, 2 * b if r >= 2 else 2 * (b - 1))
                    if 4 <= u < 4 + TPB and 1 <= g <= NG:
                        pv(g - 1, u - 4)
                    if attn_step and u in (5, 7):
                        turn_attn(b - 1, (u - 5) // 2, min(g + LEAD, NG))
                    if u == 10 and 1 <= g <= NG:
                        turn_o(g - 1)
                    if attn_step and u >= 9:
                        project(b - 1, u - 9)

        @block.scalar
        def _(act):
            nc.scalar.activation(ident16[:], ident, ACT.Copy).then_inc(masks_ready, 1)
            nc.scalar.activation(future16[:], constant(shared, "future"), ACT.Copy).then_inc(masks_ready, 1)
            nc.scalar.activation(futureT16[:], constant(shared, "futureT"), ACT.Copy).then_inc(masks_ready, 1)

            def exp_unit(g, u):
                n = NS * g + u
                act.wait_ge(st_done, n + 1)
                if u == 0:
                    wait(act, pv_done, g - 1)
                bk, _ = exp_bank(g, n)
                pieces = SUNITS[u]
                if len(pieces) == 1 or pieces[0][0] == pieces[1][0]:
                    h, j, _ = pieces[0]
                    nc.scalar.activation(pt[:, g % 2, h, AT[j]:AT[j] + SEQ], bk[:], ACT.Exp, scale=float(SCALE)).then_inc(exp_done, 1)
                else:
                    h, j, _ = pieces[0]
                    nc.scalar.activation(pt[:, g % 2, h:h + 2, AT[j]:AT[j] + WIDE[j]], bk[:].rearrange("p (h q) -> p h q", h=2),
                                         ACT.Exp, scale=float(SCALE)).then_inc(exp_done, 1)

            def copy_o(g):
                act.wait_ge(pv_done, g + 1)
                wait(act, o_turned, g - 1)
                nc.scalar.activation(oT[:, g % 2, :], bO[:], ACT.Copy).then_inc(oT_ready, 1)

            def part1(g):
                act.wait_ge(m_turned, g + 1)
                wait(act, m_out, 16 * g)
                nc.scalar.activation(negm[:, 0, :], bW[0:G * TPB, 0:P], ACT.Copy, scale=-1.0).then_inc(m_part1, 1)

            def copy_attn(b, half):
                act.wait_ge(a_turned, 2 * b + half + 1)
                wait(act, wo_done, 2 * b)
                nc.scalar.activation(aT[:, 2 * half:2 * half + 2].rearrange("p c k t -> p (c k t)"), bW[:], ACT.Copy).then_inc(aT_ready, 1)

            for g in range(LEAD - 1):
                part1(g)
            for g in range(NG + 3):
                b, r = g // GPB, g % GPB
                for u in range(NS):
                    if g < NG:
                        exp_unit(g, u)
                    if u == 3 and g - 1 + LEAD < NG:
                        part1(g - 1 + LEAD)
                    if u in (6, 8) and r == 1 and b >= 1:
                        copy_attn(b - 1, (u - 6) // 2)
                    if u == 8 and 1 <= g <= NG:
                        copy_o(g - 1)
                if r in (1, 2) and b >= 1:
                    n = 2 * (b - 1) + r - 1
                    act.wait_ge(added, n + 1)
                    first = 2 * P * n
                    act.dma_start(out[first:first + 2 * P, :].rearrange("(c p) n -> p c n", p=P),
                                  acc[:, 2 * (n % TPB):2 * (n % TPB) + 2, :]).then_inc(stored, 16)

        @block.vector
        def _(dve):
            n_combine = [0]

            def max_unit(g, u):
                b, n = g // GPB, NM * g + u
                c, heads = MUNITS[u]
                w, h0 = P * (c + 1), heads[0]
                dve.wait_ge(s_done, n + 1)
                if u == 0:
                    wait(dve, m_turned, g - 1)
                dve.tensor_reduce(mx[:, g % 2, h0:h0 + len(heads), c], bS[n % 3][:, 0:w * len(heads)].rearrange("p (h k) -> p h k", k=w),
                                  AX.X, ALU.max).then_inc(s_read, 1)

            def split_max(g):
                dve.wait_ge(m_part1, g + 1)
                dve.scalar_tensor_tensor(out=mrest[:], in0=bW[0:G * TPB, 0:P], scalar=-1.0, in1=negm[:, 0, :],
                                         op0=ALU.mult, op1=ALU.subtract).then_inc(m_rest, 1)
                dve.wait_ge(m_rest, g + 1)
                dve.tensor_copy(negm[:, 1, :], mrest[:]).then_inc(m_part2, 1)
                dve.wait_ge(m_part2, g + 1)
                dve.tensor_tensor(negm[:, 2, :], mrest[:], negm[:, 1, :], ALU.subtract).then_inc(m_part3, 1)

            def add_experts(t, j):
                a = acc[:, t % (2 * TPB), :]
                if j == 0:
                    dve.wait_ge(base_in[t % 2], 16 * (t // 2 + 1))
                    dve.wait_ge(gathered[t % 2], 16 * TOPK * (t // 2 + 1))
                    if t % TPB == 0 and t >= 2 * TPB:
                        dve.wait_ge(stored, 32 * (t // TPB - 1))
                else:
                    dve.wait_ge(combine, n_combine[0])
                ins = dve.scalar_tensor_tensor(out=a, in0=gath[:, t % 2, j, :], scalar=topw[:, t, j:j + 1],
                                               in1=base[:, t % 2, :] if j == 0 else a, op0=ALU.mult, op1=ALU.add)
                if j == TOPK - 1:
                    ins.then_inc(combined, 1)
                else:
                    n_combine[0] += 1
                    ins.then_inc(combine, 1)

            def normalise(g):
                dve.wait_ge(o_turned, g + 1)
                if g % GPB == 0:
                    wait(dve, a_turned, 2 * (g // GPB))
                o = bT[:].rearrange("p (c h x) -> p c h x", c=TPB, h=G)
                dve.reciprocal(recip[:], o[:, :, :, HD]).then_inc(recip_ready, 1)
                dve.wait_ge(recip_ready, g + 1)
                dst = attn[:, :, G * HD * (g % GPB):G * HD * (g % GPB + 1)].rearrange("p c (h d) -> p c h d", h=G)
                dve.tensor_tensor(dst, o[:, :, :, 0:HD], repeat(recip[:].unsqueeze(3), 3, HD), ALU.mult).then_inc(attn_ready, 1)

            def add_attention(b, half):
                dve.wait_ge(wo_done, 2 * b + half + 1)
                dve.wait_ge(combined, TPB * (b + 1))
                a = acc[:, TPB * (b % 2) + 2 * half:TPB * (b % 2) + 2 * half + 2, :].rearrange("p c n -> p (c n)")
                dve.tensor_tensor(a, bW[:], a, ALU.add).then_inc(added, 1)

            for g in range(LEAD):
                for u in range(NM):
                    max_unit(g, u)
                if g < LEAD - 1:
                    split_max(g)
            for g in range(NG + 3):
                b, r = g // GPB, g % GPB
                for u in range(NM):
                    if g + LEAD < NG:
                        max_unit(g + LEAD, u)
                    if g < NT and 1 <= u <= TOPK:
                        add_experts(g, u - 1)
                    if u == 2 and r == 2 and b >= 1:
                        add_attention(b - 1, 1)
                    if u == 4 and g - 1 + LEAD < NG:
                        split_max(g - 1 + LEAD)
                    if u == 0 and 2 <= g <= NG + 1:
                        normalise(g - 2)
                    if u == 10 and r == 1 and b >= 1:
                        add_attention(b - 1, 0)


INPUTS = {"x": "L0_attn_x", "wqT": "L0_attn_Wq", "wkT": "L0_attn_Wk", "wvT": "L0_attn_Wv", "woT": "L0_attn_Wo",
          "w_router": "L0_ffn_w_router", "bias": "L0_ffn_corr_bias", "gate_w": "L0_ffn_gate_w", "up_w": "L0_ffn_up_w",
          "down_w": "L0_ffn_down_w", "sh_gate": "L0_ffn_sh_gate_w", "sh_up": "L0_ffn_sh_up_w", "sh_down": "L0_ffn_sh_down_w"}


def host_arrays(inputs):
    arrays = {}
    for short, name in INPUTS.items():
        a = np.asarray(inputs[name])
        if short == "x":
            a = a.reshape(T, D)
        arrays[short] = np.ascontiguousarray(a.T if short.endswith("T") else a)
    arrays["const"] = constants()
    return arrays


def kernel(**inputs):
    from concourse import bacc
    from concourse.bass_utils import run_bass_kernel_spmd

    nc = bacc.Bacc("TRN2", target_bir_lowering=False, num_devices=1)
    arrays = host_arrays(inputs)
    A = {n: nc.dram_tensor(f"in_{n}_dram", a.shape, mybir.dt.from_np(a.dtype), kind="ExternalInput").ap()
         for n, a in arrays.items()}
    out = nc.dram_tensor("out_dram", [T, D], F32, kind="ExternalOutput").ap()
    ffn_attention_program(nc, A, out)
    r = run_bass_kernel_spmd(nc, [{f"in_{n}_dram": a for n, a in arrays.items()}], core_ids=[0])
    return r.results[0]["out_dram"].reshape(BATCH, SEQ, D)
```
